# Optimizing a Trainium2 kernel written in Bass

```python
import numpy as np
import jax
import jax.numpy as jnp

def _softmax(x, axis=-1):
    return jax.nn.softmax(x, axis=axis)

def _gelu(x):
    return jax.nn.gelu(x, approximate=True)

def _silu(x):
    return jax.nn.silu(x)

def _sigmoid(x):
    return jax.nn.sigmoid(x)

def _layernorm(x, axis=-1, eps=1e-05):
    m = jnp.mean(x, axis=axis, keepdims=True)
    v = jnp.var(x, axis=axis, keepdims=True)
    return (x - m) / jnp.sqrt(v + eps)

def _scatter_add(tgt, idx, src, axis=0):
    return tgt.at[idx].add(src)

def _segment_sum(src, seg, n):
    return jax.ops.segment_sum(src, seg, n)
kernel_name = 'mk_xattn_ffn_d2_seqx_r4_27e445'

def setup_inputs(seed: int=0):
    np.random.seed(seed)
    _w = jnp.asarray

    def _rec_inputs():
        import jax
        import jax.numpy as jnp
        _rk = jax.random.key(seed)
        x = -0.0003929 + 0.9999 * jax.random.normal(jax.random.fold_in(_rk, 1), (4, 512, 256), jnp.float32)
        _lenS = 512 - jax.random.randint(jax.random.fold_in(_rk, 7), (4,), 0, max(1, 512 // 4) + 1, jnp.int32)
        _lenS2 = 1601 - jax.random.randint(jax.random.fold_in(_rk, 8), (4,), 0, max(1, 1601 // 4) + 1, jnp.int32)
        _ctx_1024P = jax.random.normal(jax.random.fold_in(_rk, 11), (4, 16, 256), jnp.float32)
        _ctx_1024c = jax.random.dirichlet(jax.random.fold_in(_rk, 511), 0.3 * jnp.ones((16,), jnp.float32), (4, 1601))
        _ctx_1024t = jnp.einsum('bsk,bkd->bsd', _ctx_1024c, _ctx_1024P)
        _ctx_1024t = _ctx_1024t * jax.lax.rsqrt(jnp.mean(jnp.square(_ctx_1024t)) + 1e-12) * 0.953939
        ctx_1024 = 2.81802e-05 + 1.00001 * (_ctx_1024t + 0.3 * jax.random.normal(jax.random.fold_in(_rk, 611), (4, 1601, 256), jnp.float32))
        _validS = jnp.arange(512)[None, :] < _lenS[:, None]
        _validS2 = jnp.arange(1601)[None, :] < _lenS2[:, None]
        _causal = jnp.tril(jnp.ones((512, 512), dtype=bool))
        mask_Bx1xSxS2_ik1 = jnp.where(jnp.broadcast_to(_validS2[:, None, None, :], (4, 1, 512, 1601)), 1, 0).astype(jnp.int32)
        return (x, ctx_1024, mask_Bx1xSxS2_ik1)
    x, ctx_1024, mask_Bx1xSxS2_ik1 = _rec_inputs()

    def _L0_xattn_setup():
        import jax, jax.numpy as jnp
        import numpy as np
        D_MODEL = 256
        key = jax.random.key(seed)
        ks = jax.random.split(key, 8)
        B, S, D = (8, 512, D_MODEL)
        scale = 1.0 / np.sqrt(D)
        return {'x1': jax.random.normal(ks[0], (B, S, D), dtype=jnp.float32), 'x2': jax.random.normal(ks[1], (B, S, D), dtype=jnp.float32), 'Wq': jax.random.normal(ks[2], (D, D), dtype=jnp.float32) * scale, 'bq': jnp.zeros((D,), dtype=jnp.float32), 'Wk': jax.random.normal(ks[3], (D, D), dtype=jnp.float32) * scale, 'bk': jnp.zeros((D,), dtype=jnp.float32), 'Wv': jax.random.normal(ks[4], (D, D), dtype=jnp.float32) * scale, 'bv': jnp.zeros((D,), dtype=jnp.float32)}
    _L0_xattn_all = _L0_xattn_setup()
    _L0_xattn_in = {k: v for k, v in _L0_xattn_all.items() if k in ('Wq', 'bq', 'Wk', 'bk', 'Wv', 'bv')}
    del _L0_xattn_all

    def _L0_ffn_setup():
        import jax, jax.numpy as jnp
        import numpy as np
        B, N, DIM = (2, 512, 256)
        HEADS, DIM_HEAD, EXPERTS = (8, 64, 8)
        SCALE = DIM_HEAD ** (-0.5)
        key = jax.random.key(seed)
        ks = jax.random.split(key, 6)
        dim_inner = HEADS * DIM_HEAD
        return {'x': jax.random.normal(ks[0], (B, N, DIM), jnp.float32), 'w_q': jax.random.normal(ks[1], (DIM, dim_inner), jnp.float32) * 0.02, 'w_k': jax.random.normal(ks[2], (DIM, dim_inner), jnp.float32) * 0.02, 'w_gate': jax.random.normal(ks[3], (DIM, HEADS * EXPERTS), jnp.float32) * 0.02, 'value_experts': jax.random.normal(ks[4], (EXPERTS, HEADS, DIM, DIM_HEAD), jnp.float32) * 0.02, 'output_experts': jax.random.normal(ks[5], (EXPERTS, HEADS, DIM_HEAD, DIM), jnp.float32) * 0.02}
    _L0_ffn_all = _L0_ffn_setup()
    _L0_ffn_in = {k: v for k, v in _L0_ffn_all.items() if k in ('w_q', 'w_k', 'w_gate', 'value_experts', 'output_experts')}
    del _L0_ffn_all

    def _L1_xattn_setup():
        import jax, jax.numpy as jnp
        import numpy as np
        EMBED = 256
        HEADS = 16
        HEAD_DIM = EMBED // HEADS
        B, S = (4, 512)
        key = jax.random.key(seed)
        ks = jax.random.split(key, 13)
        std = 1.0 / np.sqrt(EMBED)
        inp = {'q': jax.random.normal(ks[0], (B, S, EMBED), jnp.float32), 'k': jax.random.normal(ks[1], (B, S, EMBED), jnp.float32), 'v': jax.random.normal(ks[2], (B, S, EMBED), jnp.float32), 'mask': jax.random.randint(ks[3], (B, 1, S, S), 0, 2, jnp.int32), 'wq_w': jax.random.normal(ks[4], (EMBED, EMBED), jnp.float32) * std, 'wq_b': jax.random.normal(ks[5], (EMBED,), jnp.float32) * std, 'wk_w': jax.random.normal(ks[6], (EMBED, EMBED), jnp.float32) * std, 'wk_b': jax.random.normal(ks[7], (EMBED,), jnp.float32) * std, 'wv_w': jax.random.normal(ks[8], (EMBED, EMBED), jnp.float32) * std, 'wv_b': jax.random.normal(ks[9], (EMBED,), jnp.float32) * std, 'fo_w': jax.random.normal(ks[10], (EMBED, EMBED), jnp.float32) * std, 'fo_b': jax.random.normal(ks[11], (EMBED,), jnp.float32) * std}
        return inp
    _L1_xattn_all = _L1_xattn_setup()
    _L1_xattn_in = {k: v for k, v in _L1_xattn_all.items() if k in ('wq_w', 'wq_b', 'wk_w', 'wk_b', 'wv_w', 'wv_b', 'fo_w', 'fo_b')}
    del _L1_xattn_all

    def _L1_ffn_setup():
        import jax, jax.numpy as jnp
        import numpy as np
        TOP_K = 8
        NUM_EXPERTS = 32
        CAPACITY = 256
        key = jax.random.key(seed)
        k1, k2, k3, k4 = jax.random.split(key, 4)
        B, S, H, E, F = (2, 256, 256, NUM_EXPERTS, 192)
        return {'hidden_states': jax.random.normal(k1, (B, S, H), dtype=jnp.float32), 'gate_weight': jax.random.normal(k2, (E, H), dtype=jnp.float32) * 0.02, 'gate_up_proj': jax.random.normal(k3, (E, 2 * F, H), dtype=jnp.float32) * 0.02, 'down_proj': jax.random.normal(k4, (E, H, F), dtype=jnp.float32) * 0.02}
    _L1_ffn_all = _L1_ffn_setup()
    _L1_ffn_in = {k: v for k, v in _L1_ffn_all.items() if k in ('gate_weight', 'gate_up_proj', 'down_proj')}
    del _L1_ffn_all
    return {'x': x, 'ctx_1024': ctx_1024, 'mask_Bx1xSxS2_ik1': mask_Bx1xSxS2_ik1, 'L0_xattn_Wq': _L0_xattn_in['Wq'], 'L0_xattn_bq': _L0_xattn_in['bq'], 'L0_xattn_Wk': _L0_xattn_in['Wk'], 'L0_xattn_bk': _L0_xattn_in['bk'], 'L0_xattn_Wv': _L0_xattn_in['Wv'], 'L0_xattn_bv': _L0_xattn_in['bv'], 'L0_ffn_w_q': _L0_ffn_in['w_q'], 'L0_ffn_w_k': _L0_ffn_in['w_k'], 'L0_ffn_w_gate': _L0_ffn_in['w_gate'], 'L0_ffn_value_experts': _L0_ffn_in['value_experts'], 'L0_ffn_output_experts': _L0_ffn_in['output_experts'], 'L1_xattn_wq_w': _L1_xattn_in['wq_w'], 'L1_xattn_wq_b': _L1_xattn_in['wq_b'], 'L1_xattn_wk_w': _L1_xattn_in['wk_w'], 'L1_xattn_wk_b': _L1_xattn_in['wk_b'], 'L1_xattn_wv_w': _L1_xattn_in['wv_w'], 'L1_xattn_wv_b': _L1_xattn_in['wv_b'], 'L1_xattn_fo_w': _L1_xattn_in['fo_w'], 'L1_xattn_fo_b': _L1_xattn_in['fo_b'], 'L1_ffn_gate_weight': _L1_ffn_in['gate_weight'], 'L1_ffn_gate_up_proj': _L1_ffn_in['gate_up_proj'], 'L1_ffn_down_proj': _L1_ffn_in['down_proj']}

def reference(x, ctx_1024, mask_Bx1xSxS2_ik1, L0_xattn_Wq, L0_xattn_bq, L0_xattn_Wk, L0_xattn_bk, L0_xattn_Wv, L0_xattn_bv, L0_ffn_w_q, L0_ffn_w_k, L0_ffn_w_gate, L0_ffn_value_experts, L0_ffn_output_experts, L1_xattn_wq_w, L1_xattn_wq_b, L1_xattn_wk_w, L1_xattn_wk_b, L1_xattn_wv_w, L1_xattn_wv_b, L1_xattn_fo_w, L1_xattn_fo_b, L1_ffn_gate_weight, L1_ffn_gate_up_proj, L1_ffn_down_proj):
    import jax
    import jax.numpy as jnp

    def _L0_xattn_ref(x1, x2, Wq, bq, Wk, bk, Wv, bv):
        import jax, jax.numpy as jnp
        import numpy as np
        D_MODEL = 256
        q1 = jnp.einsum('bsd,de->bse', x1, Wq) + bq
        k2 = jnp.einsum('bsd,de->bse', x2, Wk) + bk
        v2 = jnp.einsum('bsd,de->bse', x2, Wv) + bv
        scale = 1.0 / np.sqrt(q1.shape[-1]).astype(np.float32)
        scores = jnp.einsum('bqd,bkd->bqk', q1, k2) * scale
        probs = jax.nn.softmax(scores, axis=-1)
        return jnp.einsum('bqk,bkd->bqd', probs, v2)

    def _L0_ffn_ref(x, w_q, w_k, w_gate, value_experts, output_experts):
        import jax, jax.numpy as jnp
        import numpy as np
        B, N, DIM = (2, 512, 256)
        HEADS, DIM_HEAD, EXPERTS = (8, 64, 8)
        SCALE = DIM_HEAD ** (-0.5)
        b, n, _ = x.shape
        q = (x @ w_q).reshape(b, n, HEADS, DIM_HEAD).transpose(0, 2, 1, 3)
        k = (x @ w_k).reshape(b, n, HEADS, DIM_HEAD).transpose(0, 2, 1, 3)
        gates = jax.nn.sigmoid((x @ w_gate).reshape(b, n, HEADS, EXPERTS).transpose(0, 2, 1, 3))
        sel = jnp.argmax(gates, axis=-1)
        gm = jax.nn.one_hot(sel, EXPERTS, dtype=x.dtype) * gates
        values = jnp.einsum('bhne,ehdk,bnd->bhnk', gm, value_experts, x)
        sim = jnp.einsum('bhid,bhjd->bhij', q * SCALE, k)
        causal_mask = jnp.triu(jnp.ones((n, n), dtype=bool), 1)
        sim = jnp.where(causal_mask, jnp.finfo(sim.dtype).min, sim)
        attn = jax.nn.softmax(sim, axis=-1)
        out = jnp.einsum('bhij,bhjk->bhik', attn, values)
        out = jnp.einsum('bhne,ehkd,bhnk->bhnd', gm, output_experts, out)
        return out.sum(axis=1)

    def _L1_xattn_ref(q, k, v, mask, wq_w, wq_b, wk_w, wk_b, wv_w, wv_b, fo_w, fo_b):
        import jax, jax.numpy as jnp
        import numpy as np
        EMBED = 256
        HEADS = 16
        HEAD_DIM = EMBED // HEADS
        B, S = (4, 512)
        N = q.shape[0]
        qp = (q @ wq_w.T + wq_b).reshape(N, -1, HEADS, HEAD_DIM)
        kp = (k @ wk_w.T + wk_b).reshape(N, -1, HEADS, HEAD_DIM)
        vp = (v @ wv_w.T + wv_b).reshape(N, -1, HEADS, HEAD_DIM)
        energy = jnp.einsum('nqhd,nkhd->nhqk', qp, kp)
        energy = jnp.where(mask == 0, jnp.float32(-1e+20), energy)
        attention = jax.nn.softmax(energy / np.float32(np.sqrt(EMBED)), axis=3)
        out = jnp.einsum('nhql,nlhd->nqhd', attention, vp).reshape(N, -1, EMBED)
        return out @ fo_w.T + fo_b

    def _L1_ffn_ref(hidden_states, gate_weight, gate_up_proj, down_proj):
        import jax, jax.numpy as jnp
        import numpy as np
        TOP_K = 8
        NUM_EXPERTS = 32
        CAPACITY = 256
        B, S, H = hidden_states.shape
        E = gate_weight.shape[0]
        N = B * S
        x = hidden_states.reshape(N, H)
        logits = x @ gate_weight.T
        probs = jax.nn.softmax(logits.astype(jnp.float32), axis=-1)
        topw, topi = jax.lax.top_k(probs, TOP_K)
        topw = topw / topw.sum(-1, keepdims=True)
        topw = topw.astype(x.dtype)
        flat_e = topi.reshape(-1)
        flat_w = topw.reshape(-1)
        flat_x = jnp.repeat(x, TOP_K, axis=0)
        oh = jax.nn.one_hot(flat_e, E, dtype=jnp.int32)
        pos = (jnp.cumsum(oh, axis=0) * oh).sum(-1) - 1
        buf = jnp.zeros((E, CAPACITY, H), x.dtype).at[flat_e, pos].set(flat_x, mode='drop')
        gu = jnp.einsum('ech,efh->ecf', buf, gate_up_proj)
        gate, up = jnp.split(gu, 2, axis=-1)
        h = jax.nn.silu(gate) * up
        eo = jnp.einsum('ecf,ehf->ech', h, down_proj)
        tok_out = eo.at[flat_e, pos].get(mode='fill', fill_value=0)
        out = (tok_out * flat_w[:, None]).reshape(N, TOP_K, H).sum(1)
        return out.reshape(B, S, H)
    x = x + _L0_xattn_ref(_layernorm(x, axis=-1), ctx_1024, L0_xattn_Wq, L0_xattn_bq, L0_xattn_Wk, L0_xattn_bk, L0_xattn_Wv, L0_xattn_bv)
    x = x + _L0_ffn_ref(_layernorm(x, axis=-1), L0_ffn_w_q, L0_ffn_w_k, L0_ffn_w_gate, L0_ffn_value_experts, L0_ffn_output_experts)
    x = x + _L1_xattn_ref(_layernorm(x, axis=-1), ctx_1024, ctx_1024, mask_Bx1xSxS2_ik1, L1_xattn_wq_w, L1_xattn_wq_b, L1_xattn_wk_w, L1_xattn_wk_b, L1_xattn_wv_w, L1_xattn_wv_b, L1_xattn_fo_w, L1_xattn_fo_b)
    x = x + _L1_ffn_ref(_layernorm(x, axis=-1), L1_ffn_gate_weight, L1_ffn_gate_up_proj, L1_ffn_down_proj)
    return x

_drawn_inputs = setup_inputs


def setup_inputs(seed=0):
    import zlib

    import numpy as np

    out = dict(_drawn_inputs(seed))
    spreads = {'L0_xattn_bq': (0.0, 0.507), 'L0_xattn_bk': (0.0, 0.8), 'L0_xattn_bv': (0.0, 0.1)}
    factors = {'L0_ffn_w_q': 8.0,
     'L0_ffn_w_k': 8.0,
     'L0_ffn_w_gate': 5.69,
     'L0_ffn_value_experts': 5.394,
     'L0_ffn_output_experts': 5.367,
     'L1_xattn_wq_b': 8.0,
     'L1_xattn_wk_b': 8.0,
     'L1_ffn_gate_weight': 8.0,
     'L1_ffn_gate_up_proj': 8.0,
     'L1_ffn_down_proj': 8.0}
    for name, (base, spread) in spreads.items():
        noise = np.random.default_rng([zlib.crc32(name.encode()), seed]).standard_normal(out[name].shape)
        drawn = base * np.exp(spread * noise) if base else spread * noise
        out[name] = jnp.asarray(drawn.astype(out[name].dtype))
    for name, factor in factors.items():
        out[name] = (out[name] * factor).astype(out[name].dtype)
    return out
```

```python
from contextlib import ExitStack, contextmanager

import numpy as np

import concourse.bass as bass
from concourse import mybir

ALU = mybir.AluOpType
ACT = mybir.ActivationFunctionType
AX_X = mybir.AxisListType.X
F32 = mybir.dt.float32
BF16 = mybir.dt.bfloat16
I32 = mybir.dt.int32

P = 128
NB, S, D = 4, 512, 256
SK = 1601
NT = S // P
NC = D // P
NKT = -(-SK // P)
KW = [min(P, SK - P * i) for i in range(NKT)]
BANK = 512
NKC = -(-SK // BANK)
KC = [min(BANK, SK - BANK * i) for i in range(NKC)]
EPS = 1e-5
SCALE_A = float(D) ** -0.5

HB, DB, EB = 8, 64, 8
SCALE_B = float(DB) ** -0.5
NJ = EB // 2

HC, DC = 16, 16
SCALE_C = float(D) ** -0.5
NG, GH = 4, 4
NS = 3
VW = 32
TERMS = [(0, 0), (0, 1), (0, 2), (1, 0), (1, 1), (2, 0)]
KROWS = len(TERMS) * DC
MASKED = -1e20

ED, KD = 32, 8
CAP, FD = 256, 192
NSLOT = ED * CAP
ZFILL = 8
TWO_ONES = float(np.array(0x3F803F80, np.uint32).view(np.float32))


class Build:

    def __init__(self, nc, ctx):
        self.nc, self.ctx = nc, ctx
        self.sems = []

    def sb(self, ctx, name, shape, dt=F32):
        return ctx.enter_context(self.nc.sbuf_tensor(name, shape, dt))

    def sem(self, name):
        s = self.ctx.enter_context(self.nc.semaphore(name))
        self.sems.append(s)
        return s


    @contextmanager
    def semaphores(self):
        self.sems = []
        with ExitStack() as self.ctx:
            yield
            numbers = sorted(s.num for s in self.sems)
            self.nc.sync.sem_clear(range(numbers[0], numbers[-1] + 1))
            self.nc.all_engine_barrier()


class NormSems:

    def __init__(self, k, layer):
        self.stats = k.sem(f"{layer}_stats")
        self.aggr = k.sem(f"{layer}_aggr")
        self.std = k.sem(f"{layer}_std")
        self.rstd = k.sem(f"{layer}_rstd")
        self.normed = k.sem(f"{layer}_normed")
        self.turned = k.sem(f"{layer}_turned")
        self.xT_a = k.sem(f"{layer}_xT_a")
        self.xT_v = k.sem(f"{layer}_xT_v")


def norm_vector(v, k, n, x, xn):
    for t in range(NT):
        v.bn_stats(k.stats[:, t, :], x[:, t, :]).then_inc(n.stats, 1)
    for t in range(NT):
        v.wait_ge(n.stats, t + 1)
        v.bn_aggr(k.mv[:, t, :], k.stats[:, t, :]).then_inc(n.aggr, 1)
    v.wait_ge(n.std, 1)
    v.reciprocal(k.rstd[:, :], k.std[:, :]).then_inc(n.rstd, 1)
    v.wait_ge(n.rstd, 1)
    for t in range(NT):
        v.tensor_scalar(xn[:, t, :], x[:, t, :], k.mv[:, t, 0:1], k.rstd[:, t:t + 1],
                        ALU.subtract, ALU.mult).then_inc(n.normed, 1)


def norm_scalar(act, k, n):
    act.wait_ge(n.aggr, NT)
    k.nc.scalar.activation(k.std[:, :], k.mv[:, :, 1], ACT.Sqrt, bias=k.eps[:, 0:1]).then_inc(n.std, 1)


def norm_tensor(pe, k, n, xn):
    for t in range(NT):
        pe.wait_ge(n.normed, t + 1)
        for c in range(NC):
            mm = pe.transpose(k.ps[:, c, t * P:(t + 1) * P], xn[:, t, c * P:(c + 1) * P], k.ident[:, :])
    mm.then_inc(n.turned, 1)


def turned_scalar(act, k, n, xT):
    act.wait_ge(n.turned, 1)
    k.nc.scalar.copy(xT[:, 0, :], k.ps[:, 0, :]).then_inc(n.xT_a, 1)


def turned_vector(v, k, n, xT):
    v.wait_ge(n.turned, 1)
    v.tensor_copy(xT[:, 1, :], k.ps[:, 1, :]).then_inc(n.xT_v, 1)


def turned_wait(eng, n):
    eng.wait_ge(n.xT_a, 1)
    eng.wait_ge(n.xT_v, 1)


def setup(k, A):
    nc = k.nc
    ones_done, sel_done, loaded, eps_done = (k.sem(x) for x in ("set_zero", "set_sel", "set_weights", "set_eps"))
    zeros_done = k.sem("set_zeros")
    with ExitStack() as own:
        zeros = k.sb(own, "zeros", [P, NSLOT * D // P // ZFILL])
        block = own.enter_context(nc.Block())

        @block.gpsimd
        def _(g):
            g.memset(k.ident[:, :], 0.0).then_inc(ones_done, 1)
            g.memset(k.identb[:, :], 0.0).then_inc(ones_done, 1)
            g.memset(k.causal[:, :], 0.0).then_inc(ones_done, 1)
            g.memset(k.sel[:, :, :], 0.0).then_inc(ones_done, 1)
            g.memset(k.onesb[:, :], 1.0).then_inc(ones_done, 1)
            g.memset(k.before[:, :], 0.0).then_inc(ones_done, 1)
            g.wait_ge(ones_done, 6)
            g.affine_select(out=k.before[:, :], in_=k.before[:, :], compare_op=ALU.is_ge, fill=1.0, base=0,
                            pattern=[[-1, P]], channel_multiplier=1).then_inc(sel_done, 1)
            for m in (k.ident, k.identb):
                g.affine_select(out=m[:, :], in_=m[:, :], compare_op=ALU.not_equal, fill=1.0, base=0,
                                pattern=[[-1, P]], channel_multiplier=1).then_inc(sel_done, 1)
            g.affine_select(out=k.causal[:, :], in_=k.causal[:, :], compare_op=ALU.is_ge, fill=MASKED, base=0,
                            pattern=[[-1, P]], channel_multiplier=1).then_inc(sel_done, 1)
            for part in range(3):
                g.wait_ge(sel_done, 4 + part)
                v = k.sel[:, :, :].rearrange("p j (a i) -> p j a i", a=2)
                g.affine_select(out=v, in_=v, compare_op=ALU.not_equal, fill=1.0, base=-EB * part,
                                pattern=[[-2, NJ], [-1, 2], [0, DB]], channel_multiplier=1).then_inc(sel_done, 1)

        @block.vector
        def _(v):
            v.memset(k.eps[:, :], EPS).then_inc(eps_done, 1)
            for e in range(EB):
                v.memset(k.desc[:, e:e + 1], float(EB - e)).then_inc(eps_done, 1)
            v.memset(k.gp[:, :, :], 0.0).then_inc(eps_done, 1)
            for i in range(KD):
                v.memset(k.number[:, i:i + 1], float(i + 1)).then_inc(eps_done, 1)
            for e in range(ED):
                v.memset(k.base[:, e:e + 1], float(CAP * e - NSLOT)).then_inc(eps_done, 1)
            v.memset(k.carry[:, :], 0.0).then_inc(eps_done, 1)
            v.memset(zeros[:, :], 0.0).then_inc(zeros_done, 1)

        @block.sync
        def _(sp):
            sp.wait_ge(zeros_done, 1)
            for i in range(ZFILL):
                sp.dma_start(k.table_in.rearrange("(i p r) d -> i p (r d)", i=ZFILL, p=P)[i], zeros[:, :]).then_inc(k.zeroed, 16)
            sp.wait_ge(k.zeroed, 16 * ZFILL)
            n = 0
            for dst, src in k.weights(A):
                sp.dma_start(dst, src).then_inc(loaded, 16)
                n += 1
            sp.wait_ge(loaded, 16 * n)


def attention_a(k, A, b):
    k.ld_vx, k.ld_ox = k.sem("ld_vx"), k.sem("ld_ox")
    nc, ps = k.nc, k.ps
    n = NormSems(k, "na")
    (ld_x, ld_ctxT, ld_ctx, q_mm, q_ev, qk_mm, qk_ev, kb_mm, kb_ev, s_mm, top, top2, bias, exped, turned,
     pt_v, pt_a, pv_mm, o_ev, f_mm, f_ev, rsum, xb_done) = (
        k.sem("a_" + x) for x in (
            "ld_x", "ld_ctxT", "ld_ctx", "q_mm", "q_ev", "qk_mm", "qk_ev", "kb_mm", "kb_ev", "s_mm", "top", "top2",
            "bias", "exp", "turned", "pt_v", "pt_a", "pv_mm", "o_ev", "f_mm", "f_ev", "rsum", "xb"))
    with ExitStack() as own:
        ctxN = k.sb(own, "ctxN", [P, NKT, D])
        qT = k.sb(own, "a_qT", [P, NC, S])
        qk = k.sb(own, "a_qk", [P, NC, S])
        kb = k.sb(own, "a_kb", [P, NT])
        mx = k.sb(own, "a_mx", [P, 3, NT])
        rs = k.sb(own, "a_rs", [P, 2, NT])
        prob = k.sb(own, "a_prob", [P, 2, SK])
        pT = k.sb(own, "a_pT", [P, NKT, P])
        oT = k.sb(own, "a_oT", [P, NC, P])
        xb = k.sb(own, "a_xb", [P, NT, D])
        ctxT = k.sb(own, "a_ctxT", [P, NC, SK])
        block = own.enter_context(nc.Block())

        @block.sync
        def _(sp):
            sp.dma_start(k.x[:, :, :], A["x"][bass.ds(b, 1)].rearrange("a (t p) d -> p (a t) d", p=P)).then_inc(ld_x, 16)
            sp.dma_start(ctxT[:, :, :], A["ctxT"][bass.ds(b, 1)].rearrange("a (c p) s -> p (a c) s", p=P)).then_inc(ld_ctxT, 16)
            sp.dma_start(ctxN[:, 0:NKT - 1, :], A["ctx"][bass.ds(b, 1), 0:P * (NKT - 1)].rearrange(
                "a (t p) d -> p (a t) d", p=P)).then_inc(ld_ctx, 16)
            sp.dma_start(ctxN[0:KW[-1], NKT - 1, :], A["ctx"][bass.ds(b, 1), P * (NKT - 1):SK].rearrange(
                "a p d -> p (a d)")).then_inc(ld_ctx, 16)
            for c in range(NC):
                sp.dma_start(k.vxB[:, c], A["B_vx"][c * P:(c + 1) * P].rearrange("p h n -> p h n")).then_inc(k.ld_vx, 16)
            for a in range(2):
                for h in range(0, HB, 4):
                    sp.dma_start(k.oxB[a * DB:(a + 1) * DB, h:h + 4], A["B_ox"][h:h + 4, :, a].rearrange(
                        "h j p n -> p h j n")).then_inc(k.ld_ox, 16)

        @block.gpsimd
        def _(g):
            g.wait_ge(ld_x, 16)
            g.tensor_tensor(xb[:, :, :], k.x[:, :, :], k.bvA[:, :].unsqueeze(1).to_broadcast([P, NT, D]),
                            ALU.add).then_inc(xb_done, 1)

        @block.tensor
        def _(pe):
            norm_tensor(pe, k, n, k.xn)
            turned_wait(pe, n)
            for m in range(NC):
                for c in range(NC):
                    mm = pe.matmul(ps[:, 2 + m, :], k.wqA[:, c, m * P:(m + 1) * P], k.xT[:, c, :],
                                   start=c == 0, stop=c == NC - 1)
                mm.then_inc(q_mm, 1)
            pe.wait_ge(q_ev, NC)
            for m in range(NC):
                for c in range(NC):
                    mm = pe.matmul(ps[:, 4 + m, :], k.wkTA[:, c, m * P:(m + 1) * P], qT[:, c, :],
                                   start=c == 0, stop=c == NC - 1)
                mm.then_inc(qk_mm, 1)
            for t in range(NT):
                for c in range(NC):
                    mm = pe.matmul(ps[:, 6, t:t + 1], qT[:, c, t * P:(t + 1) * P], k.bkA[:, c:c + 1],
                                   start=c == 0, stop=c == NC - 1)
            mm.then_inc(kb_mm, 1)

            def scores(t):
                if t == 0:
                    pe.wait_ge(qk_ev, NC)
                    pe.wait_ge(ld_ctxT, 16)
                else:
                    pe.wait_ge(exped, t)
                for i in range(NKC):
                    for c in range(NC):
                        mm = pe.matmul(ps[:, i, 0:KC[i]], qk[:, c, t * P:(t + 1) * P],
                                       ctxT[:, c, i * BANK:i * BANK + KC[i]], start=c == 0, stop=c == NC - 1)
                mm.then_inc(s_mm, 1)

            def turn(t):
                pe.wait_ge(exped, t + 1)
                for g in range(NKC):
                    if (t, g) == (0, 0):
                        pe.wait_ge(qk_ev, NC)
                    if g % 2 == 0 and 2 * t + g // 2 > 0:
                        pe.wait_ge(pt_v, 2 * t + g // 2)
                    if g % 2 == 1 and 2 * t + g // 2 > 0:
                        pe.wait_ge(pt_a, 2 * t + g // 2)
                    for i in range(4 * g, min(4 * g + 4, NKT)):
                        mm = pe.transpose(ps[0:KW[i], 4 + g % 2, (i - 4 * g) * P:(i - 4 * g + 1) * P],
                                          prob[:, t % 2, i * P:i * P + KW[i]], k.ident[:, :])
                    mm.then_inc(turned, 1)

            def context(t):
                pe.wait_ge(pt_v, 2 * t + 2)
                pe.wait_ge(pt_a, 2 * t + 2)
                if t == 0:
                    pe.wait_ge(ld_ctx, 32)
                    pe.wait_ge(kb_ev, 1)
                else:
                    pe.wait_ge(o_ev, t)
                for m in range(NC):
                    for i in range(NKT):
                        mm = pe.matmul(ps[:, 6, m * P:(m + 1) * P], ctxN[0:KW[i], i, m * P:(m + 1) * P],
                                       pT[0:KW[i], i, :], start=i == 0, stop=i == NKT - 1)
                mm.then_inc(pv_mm, 1)

            def project(t):
                pe.wait_ge(o_ev, t + 1)
                if t >= 1:
                    pe.wait_ge(f_ev, t)
                for c in range(NC):
                    mm = pe.matmul(ps[:, 7, 0:D], oT[:, c, :], k.wvA[:, c, :], start=c == 0, stop=c == NC - 1)
                mm.then_inc(f_mm, 1)

            for i in range(NT + 2):
                if i < NT:
                    scores(i)
                if i >= 2:
                    project(i - 2)
                if 1 <= i <= NT:
                    turn(i - 1)
                    context(i - 1)

        @block.scalar
        def _(act):
            norm_scalar(act, k, n)
            turned_scalar(act, k, n, k.xT)
            for m in range(NC):
                act.wait_ge(q_mm, m + 1)
                nc.scalar.activation(qT[:, m, :], ps[:, 2 + m, :], ACT.Identity,
                                     bias=k.bqA[:, m:m + 1]).then_inc(q_ev, 1)
            for i in range(NT + 1):
                if i < NT:
                    act.wait_ge(bias, i + 1)
                    if i >= 2:
                        act.wait_ge(turned, NKC * (i - 1))
                    nc.scalar.activation(prob[:, i % 2, :], ps[:, 0:4, :].rearrange("p a n -> p (a n)")[:, 0:SK],
                                         ACT.Exp, bias=mx[:, 2, i:i + 1], scale=SCALE_A,
                                         accum_out=rs[:, 0, i:i + 1]).then_inc(exped, 1)
                if i >= 1:
                    t = i - 1
                    for g in (1, 3):
                        act.wait_ge(turned, NKC * t + g + 1)
                        w = min(4, NKT - 4 * g)
                        rows = P if w == 4 else KW[-1]
                        nc.scalar.copy(pT[0:rows, 4 * g:4 * g + w, :],
                                       ps[0:rows, 4 + g % 2, 0:w * P].rearrange("p (a n) -> p a n", n=P)).then_inc(pt_a, 1)
                    act.wait_ge(pv_mm, t + 1)
                    nc.scalar.copy(oT[:, :, :].rearrange("p c n -> p (c n)"), ps[:, 6, 0:D]).then_inc(o_ev, 1)

        @block.vector
        def _(v):
            v.wait_ge(ld_x, 16)
            norm_vector(v, k, n, k.x, k.xn)
            turned_vector(v, k, n, k.xT)
            for m in range(NC):
                v.wait_ge(qk_mm, m + 1)
                v.tensor_copy(qk[:, m, :], ps[:, 4 + m, :]).then_inc(qk_ev, 1)
            v.wait_ge(kb_mm, 1)
            v.tensor_copy(kb[:, :], ps[:, 6, 0:NT]).then_inc(kb_ev, 1)
            v.wait_ge(kb_ev, 1)

            def finish(t):
                v.wait_ge(exped, t + 1)
                v.reciprocal(rs[:, 1, t:t + 1], rs[:, 0, t:t + 1]).then_inc(rsum, 1)
                v.wait_ge(rsum, t + 1)
                v.wait_ge(f_mm, t + 1)
                v.wait_ge(xb_done, 1)
                v.scalar_tensor_tensor(out=k.x[:, t, :], in0=ps[:, 7, 0:D], scalar=rs[:, 1, t:t + 1],
                                       in1=xb[:, t, :], op0=ALU.mult, op1=ALU.add).then_inc(f_ev, 1)

            for i in range(NT + 2):
                if i < NT:
                    v.wait_ge(s_mm, i + 1)
                    v.tensor_reduce(mx[:, 0, i:i + 1], ps[:, 0:4, :].rearrange("p a n -> p (a n)")[:, 0:SK],
                                    AX_X, ALU.max).then_inc(top, 1)
                    v.wait_ge(top, i + 1)
                    v.tensor_tensor(mx[:, 1, i:i + 1], mx[:, 0, i:i + 1], kb[:, i:i + 1], ALU.add).then_inc(top2, 1)
                    v.wait_ge(top2, i + 1)
                    v.tensor_scalar(mx[:, 2, i:i + 1], mx[:, 1, i:i + 1], kb[:, i:i + 1], -SCALE_A, ALU.subtract,
                                    ALU.mult).then_inc(bias, 1)
                if i >= 2:
                    finish(i - 2)
                if 1 <= i <= NT:
                    t = i - 1
                    for g in (0, 2):
                        v.wait_ge(turned, NKC * t + g + 1)
                        v.tensor_copy(pT[:, 4 * g:4 * g + 4, :],
                                      ps[:, 4 + g % 2, :].rearrange("p (a n) -> p a n", n=P)).then_inc(pt_v, 1)


def attention_b(k, A, b):
    nc, ps = k.nc, k.ps
    n = NormSems(k, "nb")
    (qk_mm, q_ev, k_ev, g_mm, g_exp, g_one, g_sig, g_top, g_eq, g_key, g_first, g_pick, g_gm, val_mm, val_mul,
     val_sum, val_two, s_mm, top, exped, rinv, gp_done, turned, g_turned, ev_a, ev_v, pv_mm, o_ev, sel_mm, out_mm, x_done, zero_q, split) = (
        k.sem("b_" + x) for x in (
            "qk_mm", "q_ev", "k_ev", "g_mm", "g_exp", "g_one", "g_sig", "g_top", "g_eq", "g_key", "g_first",
            "g_pick", "g_gm", "val_mm", "val_mul", "val_sum", "val_two", "s_mm", "top", "exp", "rinv", "gp", "turned",
            "g_turned", "ev_a", "ev_v", "pv_mm", "o_ev", "sel_mm", "out_mm", "x_done", "zero_q", "split"))
    SC = [(1, 384), (2, 0), (1, 0), (0, 0)]
    ORDER = [3, 1, 0, 2]
    DONE = [1, 2, 4, 4]
    OFF = [0, 512, 896, 1152]
    POFF = [0, P, 3 * P, 6 * P]
    with ExitStack() as own:
        qz = k.sb(own, "b_qz", [P, HB, S])
        kT = k.sb(own, "b_kT", [P, HB // 2, S])
        gate = k.sb(own, "b_gate", [P, 3, NT * HB * EB])
        gtop = k.sb(own, "b_gtop", [P, 2, NT * HB])
        gm = k.sb(own, "b_gm", [P, NT, HB, EB])
        tmp = k.sb(own, "b_tmp", [P, 2, EB * DB])
        val = k.sb(own, "b_val", [P, NT, HB, 2, DB])
        mx = k.sb(own, "b_mx", [P, HB, NT])
        rs = k.sb(own, "b_rs", [P, HB, NT])
        ri = k.sb(own, "b_ri", [P, HB, NT])
        prob = k.sb(own, "b_prob", [P, 2, 10 * P])
        pT = k.sb(own, "b_pT", [P, 10 * P])
        oT = k.sb(own, "b_oT", [P, S])
        gr = k.sb(own, "b_gr", [P, 2, NT, EB])
        gT = k.sb(own, "b_gT", [P, S], BF16)
        og = k.sb(own, "b_og", [P, 2, NJ, S])
        gp = k.gp
        block = own.enter_context(nc.Block())

        @block.gpsimd
        def _(g):
            g.memset(qz[:, :, :], 0.0).then_inc(zero_q, 1)
            for u in range(HB * NT):
                h, t = u // NT, u % NT
                g.wait_ge(val_sum, u + 1)
                g.tensor_copy(val[:, t, h, 1, :], val[:, t, h, 0, :]).then_inc(val_two, 1)

        @block.tensor
        def _(pe):
            norm_tensor(pe, k, n, k.xn)
            turned_wait(pe, n)
            for m in range(HB // 2):
                for i, w in enumerate((k.wqB, k.wkB)):
                    if m >= 2:
                        pe.wait_ge((q_ev, k_ev)[i], (2 * (m - 1), m - 1)[i])
                    for c in range(NC):
                        mm = pe.matmul(ps[:, 2 + 2 * i + m % 2, :], w[:, c, m * P:(m + 1) * P], k.xT[:, c, :],
                                       start=c == 0, stop=c == NC - 1)
                    mm.then_inc(qk_mm, 1)
            for t in range(NT):
                for c in range(NC):
                    mm = pe.matmul(ps[:, 6, t * HB * EB:(t + 1) * HB * EB], k.xT[:, c, t * P:(t + 1) * P],
                                   k.wgB[:, c, :], start=c == 0, stop=c == NC - 1)
            mm.then_inc(g_mm, 1)
            pe.wait_ge(k.ld_vx, 16 * NC)
            for u in range(HB * NT):
                h, t = u // NT, u % NT
                if u >= 2:
                    pe.wait_ge(val_mul, u - 1)
                for c in range(NC):
                    mm = pe.matmul(ps[:, u % 2, :], k.xT[:, c, t * P:(t + 1) * P], k.vxB[:, c, h, :],
                                   start=c == 0, stop=c == NC - 1)
                mm.then_inc(val_mm, 1)

            def scores(h):
                if h == 0:
                    pe.wait_ge(val_mul, HB * NT)
                    pe.wait_ge(q_ev, HB)
                    pe.wait_ge(k_ev, HB // 2)
                for o, t in enumerate(ORDER):
                    if h >= 1:
                        pe.wait_ge(exped, NT * (h - 1) + DONE[o])
                    bank, off = SC[t]
                    pe.matmul(ps[:, bank, off:off + (t + 1) * P], qz[:, h, t * P:(t + 1) * P],
                              kT[:, h // 2, 0:(t + 1) * P], start=True, stop=False)
                    mm = pe.matmul(ps[:, bank, off + t * P:off + (t + 1) * P], k.identb[:, :], k.causal[:, :],
                                   start=False, stop=True)
                    mm.then_inc(s_mm, 1)

            def turn(h):
                pe.wait_ge(exped, NT * (h + 1))
                for g, blocks in enumerate(([(t, 0) for t in range(4)], [(t, 1) for t in range(1, 4)],
                                            [(2, 2), (3, 2), (3, 3)])):
                    if g < 2 and h >= 1:
                        pe.wait_ge(ev_v, 6 * (h - 1) + 5 + g)
                    if g == 2:
                        pe.wait_ge(ev_a, 2 * h + 1)
                    for a, (t, i) in enumerate(blocks):
                        mm = pe.transpose(ps[:, 3 + g % 2, a * P:(a + 1) * P],
                                          prob[:, h % 2, POFF[t] + i * P:POFF[t] + (i + 1) * P], k.ident[:, :])
                    mm.then_inc(turned, 1)

            def gates(h):
                pe.wait_ge(gp_done, h + 1)
                pe.wait_ge(ev_v, 6 * h + 1)
                for t in range(NT):
                    mm = pe.transpose(ps[:, 4, 0:BANK // 2].bitcast(BF16)[:, t * P:(t + 1) * P], gp[:, t, :],
                                      k.identb[:, :])
                mm.then_inc(g_turned, 1)
                for j in range(NJ):
                    if j == 0:
                        pe.wait_ge(ev_a, 2 * h + 2)
                    pe.wait_ge(ev_v, 6 * h + (2, 2, 3, 4)[j])
                    pe.matmul(ps[:, 3 + j % 2, :], k.sel[:, j, :], gT[:, :], start=True, stop=True).then_inc(sel_mm, 1)

            def values(h):
                pe.wait_ge(ev_a, 2 * h + 2)
                pe.wait_ge(ev_v, 6 * h + 1)
                pe.wait_ge(val_two, NT * (h + 1))
                if h >= 1:
                    pe.wait_ge(o_ev, h)
                for i in range(NT):
                    mm = pe.matmul(ps[:, 5, i * P:S],
                                   val[:, i, h, :, :].rearrange("p a d -> p (a d)"),
                                   pT[:, OFF[i]:OFF[i] + S - i * P], start=i == 0, stop=i == NT - 1)
                mm.then_inc(pv_mm, 1)

            def out(h):
                pe.wait_ge(ev_v, 6 * (h + 1))
                for j in range(NJ):
                    for t in range(NT):
                        first = (h, j) == (0, 0)
                        mm = pe.matmul(ps[:, 6 + t // 2, (t % 2) * D:(t % 2 + 1) * D], og[:, h % 2, j, t * P:(t + 1) * P],
                                       k.oxB[:, h, j, :], start=first and t % 2 == 0,
                                       stop=(h, j) == (HB - 1, NJ - 1) and t % 2 == 1, skip_group_check=True)
                mm.then_inc(out_mm, 1)

            pe.wait_ge(g_exp, 1)
            pe.wait_ge(k.ld_ox, 16 * 4)
            scores(0)
            for h in range(HB):
                turn(h)
                if h + 1 < HB:
                    scores(h + 1)
                values(h)
                gates(h)
                if h >= 1:
                    out(h - 1)
            out(HB - 1)

        @block.scalar
        def _(act):
            norm_scalar(act, k, n)
            turned_scalar(act, k, n, k.xT)
            act.wait_ge(zero_q, 1)
            for m in range(HB // 2):
                act.wait_ge(qk_mm, 2 * m + 1)
                for a in range(2):
                    nc.scalar.mul(qz[DB * a:DB * a + DB, 2 * m + a, :], ps[DB * a:DB * a + DB, 2 + m % 2, :],
                                  SCALE_B).then_inc(q_ev, 1)
            act.wait_ge(g_mm, 1)
            nc.scalar.activation(gate[:, 0, :], ps[:, 6, 0:NT * HB * EB], ACT.Exp, scale=-1.0).then_inc(g_exp, 1)

            def probabilities(h):
                for o, t in enumerate(ORDER):
                    act.wait_ge(top, NT * h + DONE[o])
                    if h >= 2 and o == 0:
                        act.wait_ge(turned, 3 * (h - 1))
                    bank, off = SC[t]
                    nc.scalar.activation(prob[:, h % 2, POFF[t]:POFF[t] + (t + 1) * P],
                                         ps[:, bank, off:off + (t + 1) * P], ACT.Exp, bias=mx[:, h, t:t + 1],
                                         accum_out=rs[:, h, t:t + 1]).then_inc(exped, 1)

            def read_turned(h):
                for g in (0, 2):
                    act.wait_ge(turned, 3 * h + g + 1)
                    w = (4, 3, 3)[g] * P
                    nc.scalar.copy(pT[:, OFF[g]:OFF[g] + w], ps[:, 3 + g % 2, 0:w]).then_inc(ev_a, 1)

            probabilities(0)
            for h in range(HB):
                read_turned(h)
                if h + 1 < HB:
                    probabilities(h + 1)
                act.wait_ge(pv_mm, h + 1)
                if h >= 1:
                    act.wait_ge(ev_v, 6 * h)
                nc.scalar.copy(oT[:, :], ps[:, 5, :]).then_inc(o_ev, 1)

        @block.vector
        def _(v):
            norm_vector(v, k, n, k.x, k.xn)
            turned_vector(v, k, n, k.xT)
            for m in range(HB // 2):
                v.wait_ge(qk_mm, 2 * m + 2)
                v.tensor_copy(kT[:, m, :], ps[:, 4 + m % 2, :]).then_inc(k_ev, 1)
            v.wait_ge(g_exp, 1)
            v.tensor_scalar(gate[:, 1, :], gate[:, 0, :], 1.0, None, ALU.add).then_inc(g_one, 1)
            v.wait_ge(g_one, 1)
            v.reciprocal(gate[:, 2, :], gate[:, 1, :]).then_inc(g_sig, 1)
            v.wait_ge(g_sig, 1)
            g8 = [gate[:, i, :].rearrange("p (a e) -> p a e", e=EB) for i in range(3)]
            wide = [P, NT * HB, EB]
            v.tensor_reduce(gtop[:, 0, :], g8[2], AX_X, ALU.max).then_inc(g_top, 1)
            v.wait_ge(g_top, 1)
            v.tensor_tensor(g8[0], g8[2], gtop[:, 0, :].unsqueeze(2).to_broadcast(wide), ALU.is_equal).then_inc(g_eq, 1)
            v.wait_ge(g_eq, 1)
            v.tensor_tensor(g8[1], g8[0], k.desc[:, :].unsqueeze(1).to_broadcast(wide), ALU.mult).then_inc(g_key, 1)
            v.wait_ge(g_key, 1)
            v.tensor_reduce(gtop[:, 1, :], g8[1], AX_X, ALU.max).then_inc(g_first, 1)
            v.wait_ge(g_first, 1)
            v.tensor_tensor(g8[0], g8[1], gtop[:, 1, :].unsqueeze(2).to_broadcast(wide), ALU.is_equal).then_inc(g_pick, 1)
            v.wait_ge(g_pick, 1)
            gma = gm[:, :, :, :].rearrange("p t h e -> p (t h) e")
            v.tensor_tensor(gma, g8[0], g8[2], ALU.mult).then_inc(g_gm, 1)
            v.wait_ge(g_gm, 1)
            for u in range(HB * NT):
                h, t = u // NT, u % NT
                v.wait_ge(val_mm, u + 1)
                if u >= 2:
                    v.wait_ge(val_sum, u - 1)
                v.tensor_tensor(tmp[:, u % 2, :].rearrange("p (e d) -> p e d", e=EB),
                                ps[:, u % 2, :].rearrange("p (e d) -> p e d", e=EB),
                                gm[:, t, h, :].unsqueeze(2).to_broadcast([P, EB, DB]), ALU.mult).then_inc(val_mul, 1)
                v.wait_ge(val_mul, u + 1)
                v.tensor_reduce(val[:, t, h, 0, :], tmp[:, u % 2, :].rearrange("p (e d) -> p d e", e=EB), AX_X,
                                ALU.add).then_inc(val_sum, 1)

            def maxima(h):
                for o, t in enumerate(ORDER):
                    v.wait_ge(s_mm, NT * h + DONE[o])
                    bank, off = SC[t]
                    v.tensor_reduce(mx[:, h, t:t + 1], ps[:, bank, off:off + (t + 1) * P], AX_X, ALU.max,
                                    negate=True).then_inc(top, 1)

            def split_gates(h):
                gs = split
                v.wait_ge(exped, NT * (h + 1))
                v.reciprocal(ri[:, h, :], rs[:, h, :]).then_inc(rinv, 1)
                v.wait_ge(rinv, h + 1)
                v.tensor_tensor(gr[:, 0, :, :], gm[:, :, h, :], ri[:, h, :].unsqueeze(2).to_broadcast([P, NT, EB]),
                                ALU.mult).then_inc(gs, 1)
                if h >= 1:
                    v.wait_ge(g_turned, h)
                v.wait_ge(gs, 4 * h + 1)
                v.tensor_copy(gp[:, :, 0:EB], gr[:, 0, :, :]).then_inc(gs, 1)
                v.wait_ge(gs, 4 * h + 2)
                v.tensor_tensor(gr[:, 1, :, :], gr[:, 0, :, :], gp[:, :, 0:EB], ALU.subtract).then_inc(gs, 1)
                v.wait_ge(gs, 4 * h + 3)
                v.tensor_copy(gp[:, :, EB:2 * EB], gr[:, 1, :, :]).then_inc(gs, 1)
                v.wait_ge(gs, 4 * h + 4)
                v.tensor_tensor(gp[:, :, 2 * EB:3 * EB], gr[:, 1, :, :], gp[:, :, EB:2 * EB],
                                ALU.subtract).then_inc(gp_done, 1)

            maxima(0)
            for h in range(HB):
                v.wait_ge(turned, 3 * h + 2)
                v.tensor_copy(pT[:, OFF[1]:OFF[1] + 3 * P], ps[:, 4, 0:3 * P]).then_inc(ev_v, 1)
                split_gates(h)
                if h + 1 < HB:
                    maxima(h + 1)
                v.wait_ge(g_turned, h + 1)
                v.tensor_copy(gT[:, :], ps[:, 4, 0:BANK // 2].bitcast(BF16)).then_inc(ev_v, 1)
                v.wait_ge(o_ev, h + 1)
                if h >= 2:
                    v.wait_ge(out_mm, h - 1)
                for j in range(NJ):
                    v.wait_ge(sel_mm, NJ * h + j + 1)
                    v.tensor_tensor(og[:, h % 2, j, :], oT[:, :], ps[:, 3 + j % 2, :], ALU.mult).then_inc(ev_v, 1)
            v.wait_ge(out_mm, HB)
            for t in range(NT):
                v.tensor_tensor(k.x[:, t, :], k.x[:, t, :], ps[:, 6 + t // 2, (t % 2) * D:(t % 2 + 1) * D],
                                ALU.add).then_inc(x_done, 1)


def split3(v, sem, at, f, parts, rest):
    v.tensor_copy(parts[0], f).then_inc(sem, 1)
    v.wait_ge(sem, at + 1)
    v.tensor_tensor(rest, f, parts[0], ALU.subtract).then_inc(sem, 1)
    v.wait_ge(sem, at + 2)
    v.tensor_copy(parts[1], rest).then_inc(sem, 1)
    v.wait_ge(sem, at + 3)
    v.tensor_tensor(parts[2], rest, parts[1], ALU.subtract).then_inc(sem, 1)
    return at + 4


def project_c(k, A, b, vaug):
    nc, ps = k.nc, k.ps
    n = NormSems(k, "nc")
    ld_maskN = [k.sem(f"c_ld_maskN{i}") for i in range(2)]
    ld_maskT = [k.sem(f"c_ld_maskT{i}") for i in range(2)]
    (ld_ctxT, k_mm, k_ev, v_mm, v_ev, q_mm, q_ev, split_k, split_q, stored, biasN, biasT, tail) = (
        k.sem("c_" + x) for x in ("ld_ctxT", "k_mm", "k_ev", "v_mm", "v_ev", "q_mm", "q_ev",
                                  "split_k", "split_q", "stored", "biasN", "biasT", "tail"))
    with ExitStack() as own:
        kf = k.sb(own, "c_kf", [P, NC, SK])
        k3 = k.sb(own, "c_k3", [P, 3, NC, SK], BF16)
        qf = k.sb(own, "c_qf", [P, NC, S])
        q3 = k.sb(own, "c_q3", [P, 3, NC, S], BF16)
        rest = k.sb(own, "c_rest", [P, NC, SK])
        ctxT = k.sb(own, "c_ctxT", [P, NC, SK])
        rawN = k.sb(own, "c_rawN", [P, 2, SK], I32)
        rawT = k.sb(own, "c_rawT", [P, 2, 2, S], I32)
        block = own.enter_context(nc.Block())
        pairs = [(i, min(2, NKT - i)) for i in range(0, NKT, 2)]

        @block.gpsimd
        def _(g):
            g.memset(vaug[:, :, :, DC:DC + 1], 1.0).then_inc(tail, 1)
            g.memset(vaug[:, :, :, DC + 1:VW], 0.0).then_inc(tail, 1)
            for j, (i, w) in enumerate(pairs):
                g.wait_ge(ld_maskT[j % 2], 16 * (j // 2 + 1))
                g.tensor_scalar(k.maskT[0:KW[i], i:i + w, :], rawT[0:KW[i], j % 2, 0:w, :], 0.0, MASKED, ALU.is_equal,
                                ALU.mult).then_inc(biasT, 1)

        @block.tensor
        def _(pe):
            pe.wait_ge(ld_ctxT, 16)
            for m in range(NC):
                for i in range(NKC):
                    if m:
                        pe.wait_ge(k_ev, i + 1)
                    for c in range(NC):
                        mm = pe.matmul(ps[:, 2 + i, 0:KC[i]], k.wkC[:, c, m * P:(m + 1) * P],
                                       ctxT[:, c, i * BANK:i * BANK + KC[i]], start=c == 0, stop=c == NC - 1)
                    mm.then_inc(k_mm, 1)
            norm_tensor(pe, k, n, k.xn)
            for i in range(NKT):
                if i >= 2:
                    pe.wait_ge(v_ev, i - 1)
                for c in range(NC):
                    mm = pe.matmul(ps[0:KW[i], 6 + i % 2, 0:D], ctxT[:, c, i * P:i * P + KW[i]], k.wvC[:, c, :],
                                   start=c == 0, stop=c == NC - 1)
                mm.then_inc(v_mm, 1)
            turned_wait(pe, n)
            pe.wait_ge(k_ev, NC * NKC)
            for m in range(NC):
                for c in range(NC):
                    mm = pe.matmul(ps[:, 2 + m, :], k.wqC[:, c, m * P:(m + 1) * P], k.xT[:, c, :],
                                   start=c == 0, stop=c == NC - 1)
                mm.then_inc(q_mm, 1)

        @block.scalar
        def _(act):
            norm_scalar(act, k, n)
            for m in range(NC):
                for i in range(NKC):
                    act.wait_ge(k_mm, NKC * m + i + 1)
                    nc.scalar.activation(kf[:, m, i * BANK:i * BANK + KC[i]], ps[:, 2 + i, 0:KC[i]], ACT.Identity,
                                         bias=k.bkC[:, m:m + 1]).then_inc(k_ev, 1)
            turned_scalar(act, k, n, k.xT)
            for m in range(NC):
                act.wait_ge(q_mm, m + 1)
                nc.scalar.activation(qf[:, m, :], ps[:, 2 + m, :], ACT.Identity,
                                     bias=k.bqC[:, m:m + 1]).then_inc(q_ev, 1)

        @block.vector
        def _(v):
            norm_vector(v, k, n, k.x, k.xn)
            turned_vector(v, k, n, k.xT)
            for i in range(NKT):
                v.wait_ge(v_mm, i + 1)
                v.tensor_tensor(vaug[0:KW[i], i, :, 0:DC], ps[0:KW[i], 6 + i % 2, 0:D].rearrange("p (h d) -> p h d", d=DC),
                                k.bvC[0:KW[i], :].rearrange("p (h d) -> p h d", d=DC), ALU.add).then_inc(v_ev, 1)
            at = 0
            v.wait_ge(q_ev, NC)
            split3(v, split_q, 0, qf[:, :, :], [q3[:, i, :, :] for i in range(3)], rest[:, :, 0:S])
            v.wait_ge(split_q, 4)
            for m in range(NC):
                v.wait_ge(k_ev, NKC * (m + 1))
                at = split3(v, split_k, at, kf[:, m, :], [k3[:, i, m, :] for i in range(3)], rest[:, m, :])

            for t in range(NT):
                v.wait_ge(ld_maskN[t % 2], 16 * (t // 2 + 1))
                v.tensor_scalar(k.maskN[:, t, :], rawN[:, t % 2, :], 0.0, MASKED, ALU.is_equal,
                                ALU.mult).then_inc(biasN, 1)

        @block.sync
        def _(sp):
            sp.dma_start(ctxT[:, :, :], A["ctxT"][bass.ds(b, 1)].rearrange("a (c p) s -> p (a c) s", p=P)).then_inc(ld_ctxT, 16)
            for t in range(2):
                sp.dma_start(rawN[:, t % 2, :], A["mask"][bass.ds(b, 1), t * P:(t + 1) * P].rearrange(
                    "a p s -> p (a s)")).then_inc(ld_maskN[t % 2], 16)
            for j, (i, w) in enumerate(pairs):
                if j >= 2:
                    sp.wait_ge(biasT, j - 1)
                rows = KW[i + w - 1]
                sp.dma_start(rawT[0:rows, j % 2, 0:w, :], A["maskT"][bass.ds(b, 1), i * P:i * P + (w - 1) * P + rows].rearrange(
                    "a (w p) s -> p (a w) s", w=w)).then_inc(ld_maskT[j % 2], 16)
            sp.wait_ge(split_q, 4)
            for i in range(3):
                sp.dma_start(k.q_parts[i].rearrange("(c p) s -> p c s", p=P), q3[:, i, :, :]).then_inc(stored, 16)
            for m in range(NC):
                sp.wait_ge(split_k, 4 * (m + 1))
                for i in range(3):
                    sp.dma_start(k.k_parts[i, m * P:(m + 1) * P, :], k3[:, i, m, :]).then_inc(stored, 16)
            for t in range(2, NT):
                sp.wait_ge(biasN, t - 1)
                sp.dma_start(rawN[:, t % 2, :], A["mask"][bass.ds(b, 1), t * P:(t + 1) * P].rearrange(
                    "a p s -> p (a s)")).then_inc(ld_maskN[t % 2], 16)
            sp.wait_ge(stored, 16 * 3 * (1 + NC))


def attention_c(k, A, b, vaug):
    nc, ps = k.nc, k.ps
    ld_k = [k.sem(f"d_ld_k{i}") for i in range(NS)]
    ld_q = [k.sem(f"d_ld_q{i}") for i in range(NS)]
    (ld_m, mx_mm, mx_v, neg, split_m, m_turned, m_row, s_mm, exped, pv_mm, acc_ev, acc_turned, o_rec,
     o_nat, o_turned, oT_a, oT_v, f_mm, f_ev, xb_done, saved, ones) = (
        k.sem("d_" + x) for x in (
            "ld_m", "mx_mm", "mx_v", "neg", "split_m", "m_turned", "m_row", "s_mm", "exp", "pv_mm",
            "acc_ev", "acc_turned", "o_rec", "o_nat", "o_turned", "oT_a", "oT_v", "f_mm", "f_ev", "xb", "saved", "ones"))
    NU = NT * GH * NKC
    with ExitStack() as own:
        kS = k.sb(own, "kS", [P, NS, GH, SK + SK % 2], BF16)
        qS = k.sb(own, "qS", [P, NS, GH, S], BF16)
        mp = k.sb(own, "d_mp", [P, NT, GH, NKC])
        m1 = k.sb(own, "d_m1", [P, 2, NT * GH])
        m3 = k.sb(own, "d_m3", [P, NT, 3, GH], BF16)
        mrow = k.sb(own, "d_mrow", [3 * GH, S], BF16)
        prob = k.sb(own, "d_prob", [P, 2, GH, S])
        acc = k.sb(own, "d_acc", [P, S])
        rec = k.sb(own, "d_rec", [P, NT, GH])
        oN = k.sb(own, "d_oN", [P, NT, D])
        oT = k.sb(own, "d_oT", [P, NC, S])
        xb = k.sb(own, "d_xb", [P, NT, D])
        block = own.enter_context(nc.Block())

        @block.sync
        def _(sp):
            def load(g):
                if g >= NS:
                    sp.wait_ge(s_mm, 2 * NKT * (g - NS + 1))
                for r, (i, j) in enumerate(TERMS):
                    sp.dma_start(qS[r * DC:(r + 1) * DC, g % NS, :, :], k.q_parts[j, g * GH * DC:(g + 1) * GH * DC].rearrange(
                        "(h d) s -> d h s", d=DC)).then_inc(ld_q[g % NS], 16)
                for r, (i, j) in enumerate(TERMS):
                    sp.dma_start(kS[r * DC:(r + 1) * DC, g % NS, :, 0:SK], k.k_parts[i, g * GH * DC:(g + 1) * GH * DC].rearrange(
                        "(h d) s -> d h s", d=DC)).then_inc(ld_k[g % NS], 16)

            for g in range(NS):
                load(g)
            for g in range(NG):
                sp.wait_ge(m_row, g + 1)
                for i in range(3):
                    sp.dma_start(qS[KROWS + i:KROWS + i + 1, g % NS, :, :],
                                 mrow[i * GH:(i + 1) * GH, :]).then_inc(ld_m, 16)
                if g >= 1 and g + NS - 1 < NG:
                    load(g + NS - 1)
            sp.wait_ge(f_ev, NT)
            sp.dma_start(k.x_mid[bass.ds(b, 1)].rearrange("a (t p) d -> p (a t) d", p=P), k.x[:, :, :]).then_inc(saved, 16)
            sp.wait_ge(saved, 16)

        @block.gpsimd
        def _(g):
            for i in range(NS):
                g.memset(kS[KROWS:KROWS + 3, i, :, :].rearrange("p h s -> p (h s)").bitcast(F32), TWO_ONES).then_inc(ones, 1)
            g.wait_ge(ones, NS)
            g.tensor_tensor(xb[:, :, :], k.x[:, :, :], k.boC[:, :].unsqueeze(1).to_broadcast([P, NT, D]),
                            ALU.add).then_inc(xb_done, 1)

        @block.tensor
        def _(pe):
            def maxima(g, u):
                t, h, i = u // (GH * NKC), u // NKC % GH, u % NKC
                n = NU * g + u
                if u == 0:
                    pe.wait_ge(ld_q[g % NS], 16 * len(TERMS) * (g // NS + 1))
                    pe.wait_ge(ld_k[g % NS], 16 * len(TERMS) * (g // NS + 1))
                if n >= 2:
                    pe.wait_ge(mx_v, n - 1)
                pe.matmul(ps[:, 5 + n % 2, 0:KC[i]], qS[0:KROWS, g % NS, h, t * P:(t + 1) * P],
                          kS[0:KROWS, g % NS, h, i * BANK:i * BANK + KC[i]], start=True, stop=True).then_inc(mx_mm, 1)

            def turn_maxima(g):
                pe.wait_ge(split_m, 4 * (g + 1))
                if g >= 2:
                    pe.wait_ge(o_nat, g - 1)
                for t in range(NT):
                    mm = pe.transpose(ps[0:3 * GH, 7, 0:BANK // 2].bitcast(BF16)[:, t * P:(t + 1) * P],
                                      m3[:, t, :, :].rearrange("p a h -> p (a h)"), k.identb[:, :])
                mm.then_inc(m_turned, 1)

            def scores(g, i, a):
                w = KW[i]
                if i == 0 and a == 0:
                    pe.wait_ge(ld_m, 48 * (g + 1))
                    pe.wait_ge(ones, min(g + 1, NS))
                if g + i >= 1:
                    pe.wait_ge(exped, 2 * (NKT * g + i) - 1 + a)
                for j in range(2):
                    h = 2 * a + j
                    pe.matmul(ps[0:w, h, :], k.identb[0:w, 0:w], k.maskT[0:w, i, :], start=True, stop=False)
                    mm = pe.matmul(ps[0:w, h, :], kS[0:KROWS + 3, g % NS, h, i * P:i * P + w],
                                   qS[0:KROWS + 3, g % NS, h, :], start=False, stop=True)
                mm.then_inc(s_mm, 1)

            def values(g, i):
                w = KW[i]
                pe.wait_ge(exped, 2 * (NKT * g + i) + 2)
                if g >= 1 and i == 0:
                    pe.wait_ge(acc_ev, g)
                for h in range(GH):
                    mm = pe.matmul(ps[VW * h:VW * (h + 1), 4, :], vaug[0:w, i, GH * g + h, :],
                                   prob[0:w, i % 2, h, :], start=i == 0, stop=i == NKT - 1)
                mm.then_inc(pv_mm, 1)

            def turn_out(g):
                pe.wait_ge(acc_ev, g + 1)
                pe.wait_ge(m_row, min(g + 2, NG))
                if g >= 1:
                    pe.wait_ge(o_nat, g)
                for t in range(NT):
                    mm = pe.transpose(ps[:, 7, t * P:(t + 1) * P], acc[:, t * P:(t + 1) * P], k.ident[:, :])
                mm.then_inc(acc_turned, 1)

            for u in range(NU):
                maxima(0, u)
            turn_maxima(0)
            for g in range(NG):
                u = 0
                for i in range(NKT):
                    scores(g, i, 0)
                    scores(g, i, 1)
                    if i == 0 and g >= 1:
                        turn_out(g - 1)
                    if i >= 1:
                        values(g, i - 1)
                    if g + 1 < NG:
                        for _ in range(6):
                            if u < NU:
                                maxima(g + 1, u)
                                u += 1
                        if i == NKT - 1:
                            turn_maxima(g + 1)
                values(g, NKT - 1)
            turn_out(NG - 1)
            for t in range(NT):
                if t == 0:
                    pe.wait_ge(exped, 2 * NKT * NG)
                    pe.wait_ge(o_nat, NG)
                for c in range(NC):
                    mm = pe.transpose(ps[:, c, t * P:(t + 1) * P], oN[:, t, c * P:(c + 1) * P], k.ident[:, :])
            mm.then_inc(o_turned, 1)
            pe.wait_ge(oT_a, 1)
            pe.wait_ge(oT_v, 1)
            for t in range(NT):
                if t >= 2:
                    pe.wait_ge(f_ev, t - 1)
                for c in range(NC):
                    mm = pe.matmul(ps[:, 2 + t % 2, 0:D], oT[:, c, t * P:(t + 1) * P], k.woC[:, c, :],
                                   start=c == 0, stop=c == NC - 1)
                mm.then_inc(f_mm, 1)

        @block.scalar
        def _(act):
            for g in range(NG):
                for i in range(NKT):
                    w = KW[i]
                    for a in range(2):
                        act.wait_ge(s_mm, 2 * (NKT * g + i) + a + 1)
                        if NKT * g + i >= 2:
                            act.wait_ge(pv_mm, NKT * g + i - 1)
                        nc.scalar.activation(prob[0:w, i % 2, 2 * a:2 * a + 2, :], ps[0:w, 2 * a:2 * a + 2, :],
                                             ACT.Exp, scale=SCALE_C).then_inc(exped, 1)
                act.wait_ge(pv_mm, NKT * (g + 1))
                if g >= 1:
                    act.wait_ge(acc_turned, g)
                nc.scalar.copy(acc[:, :], ps[:, 4, :]).then_inc(acc_ev, 1)
            act.wait_ge(o_turned, 1)
            nc.scalar.copy(oT[:, 0, :], ps[:, 0, :]).then_inc(oT_a, 1)

        @block.vector
        def _(v):
            def maxima(g):
                for u in range(NU):
                    t, h, i = u // (GH * NKC), u // NKC % GH, u % NKC
                    n = NU * g + u
                    v.wait_ge(mx_mm, n + 1)
                    bank = ps[:, 5 + n % 2, 0:KC[i]]
                    v.tensor_tensor_reduce(bank, bank, k.maskN[:, t, i * BANK:i * BANK + KC[i]], 1.0, -3.0e38,
                                           ALU.add, ALU.max, mp[:, t, h, i:i + 1]).then_inc(mx_v, 1)
                v.wait_ge(mx_v, NU * (g + 1))
                if g >= 1:
                    v.wait_ge(split_m, 4 * g)
                v.tensor_reduce(m1[:, 0, :], mp[:, :, :, :].rearrange("p t h i -> p (t h) i"), AX_X, ALU.max,
                                negate=True).then_inc(neg, 1)
                v.wait_ge(neg, g + 1)
                if g >= 1:
                    v.wait_ge(m_turned, g)
                f = [m1[:, i, :].rearrange("p (t h) -> p t h", t=NT) for i in range(2)]
                split3(v, split_m, 4 * g, f[0], [m3[:, :, i, :] for i in range(3)], f[1])
                v.wait_ge(m_turned, g + 1)
                if g >= 1:
                    v.wait_ge(ld_m, 48 * g)
                v.tensor_copy(mrow[:, :], ps[0:3 * GH, 7, 0:BANK // 2].bitcast(BF16)).then_inc(m_row, 1)

            def outputs(g):
                v.wait_ge(acc_turned, g + 1)
                o = ps[:, 7, :].rearrange("p (t h c) -> p t h c", t=NT, h=GH)
                v.reciprocal(rec[:, :, :], o[:, :, :, DC]).then_inc(o_rec, 1)
                v.wait_ge(o_rec, g + 1)
                v.tensor_tensor(oN[:, :, GH * DC * g:GH * DC * (g + 1)].rearrange("p t (h c) -> p t h c", h=GH),
                                o[:, :, :, 0:DC], rec[:, :, :].unsqueeze(3).to_broadcast([P, NT, GH, DC]),
                                ALU.mult).then_inc(o_nat, 1)

            maxima(0)
            for g in range(NG):
                if g >= 1:
                    outputs(g - 1)
                if g + 1 < NG:
                    maxima(g + 1)
            outputs(NG - 1)
            v.wait_ge(o_turned, 1)
            v.tensor_copy(oT[:, 1, :], ps[:, 1, :]).then_inc(oT_v, 1)
            v.wait_ge(xb_done, 1)
            for t in range(NT):
                v.wait_ge(f_mm, t + 1)
                v.tensor_tensor(k.x[:, t, :], ps[:, 2 + t % 2, 0:D], xb[:, t, :], ALU.add).then_inc(f_ev, 1)


def route(k, A, b):
    nc, ps = k.nc, k.ps
    n = NormSems(k, "nd")
    (l_mm, l_top, l_sub, exped, top8, out8, picked, den, rden, weight, step, counted, slotted, saved) = (
        k.sem("r_" + x) for x in (
            "l_mm", "l_top", "l_sub", "exp", "top8", "out8", "picked", "den", "rden", "weight", "step", "counted",
            "slotted", "saved"))
    with ExitStack() as own:
        logit = k.sb(own, "r_logit", [P, NT, ED])
        lmax = k.sb(own, "r_lmax", [P, NT])
        e = k.sb(own, "r_e", [P, NT, ED])
        best = k.sb(own, "r_best", [P, NT, KD])
        rest = k.sb(own, "r_rest", [P, NT, ED])
        sel = k.sb(own, "r_sel", [P, NT, ED])
        selb = k.sb(own, "r_selb", [P, NT, ED], BF16)
        dn = k.sb(own, "r_dn", [P, 2, NT])
        w = k.sb(own, "r_w", [P, NT, ED])
        c0 = k.sb(own, "r_c0", [P, NT, ED])
        c1 = k.sb(own, "r_c1", [P, NT, ED])
        ok = k.sb(own, "r_ok", [P, NT, ED])
        pos = k.sb(own, "r_pos", [P, NT, ED])
        hot = k.sb(own, "r_hot", [P, NT, KD, ED])
        prod = k.sb(own, "r_prod", [P, NT, KD, ED])
        slotf = k.sb(own, "r_slotf", [P, NT * KD])
        slot = k.sb(own, "r_slot", [P, NT * KD], I32)
        wk = k.sb(own, "r_wk", [P, NT * KD])
        block = own.enter_context(nc.Block())

        @block.tensor
        def _(pe):
            norm_tensor(pe, k, n, k.xn)
            turned_wait(pe, n)
            for t in range(NT):
                for c in range(NC):
                    mm = pe.matmul(ps[:, 2, t * ED:(t + 1) * ED], k.xT[:, c, t * P:(t + 1) * P], k.wgD[:, c, :],
                                   start=c == 0, stop=c == NC - 1)
            mm.then_inc(l_mm, 1)
            pe.wait_ge(picked, 2)
            for t in range(NT + 1):
                for i in range(min(t, NT)):
                    mm = pe.matmul(ps[:, 3, t * ED:(t + 1) * ED], k.onesb[:, :], selb[:, i, :], start=i == 0,
                                   stop=t == NT and i == NT - 1)
                if t < NT:
                    mm = pe.matmul(ps[:, 3, t * ED:(t + 1) * ED], k.before[:, :], selb[:, t, :], start=t == 0, stop=True)
            mm.then_inc(counted, 1)

        @block.scalar
        def _(act):
            norm_scalar(act, k, n)
            turned_scalar(act, k, n, k.xT)
            act.wait_ge(l_sub, 1)
            nc.scalar.activation(e[:, :, :], logit[:, :, :], ACT.Exp).then_inc(exped, 1)

        @block.vector
        def _(v):
            norm_vector(v, k, n, k.x, k.xn)
            turned_vector(v, k, n, k.xT)
            wide = [P, NT, ED]
            v.wait_ge(l_mm, 1)
            lps = ps[:, 2, 0:NT * ED].rearrange("p (t e) -> p t e", e=ED)
            v.tensor_reduce(lmax[:, :], lps, AX_X, ALU.max).then_inc(l_top, 1)
            v.wait_ge(l_top, 1)
            v.tensor_tensor(logit[:, :, :], lps, lmax[:, :].unsqueeze(2).to_broadcast(wide), ALU.subtract).then_inc(l_sub, 1)
            v.wait_ge(exped, 1)
            for t in range(NT):
                v.max(best[:, t, :], e[:, t, :]).then_inc(top8, 1)
            for t in range(NT):
                v.wait_ge(top8, t + 1)
                v.match_replace(rest[:, t, :], best[:, t, :], e[:, t, :], -1.0).then_inc(out8, 1)
            v.wait_ge(out8, NT)
            v.tensor_scalar(sel[:, :, :], rest[:, :, :], 0.0, None, ALU.is_lt).then_inc(picked, 1)
            v.tensor_scalar(selb[:, :, :], rest[:, :, :], 0.0, None, ALU.is_lt).then_inc(picked, 1)
            v.tensor_reduce(dn[:, 0, :], best[:, :, :], AX_X, ALU.add).then_inc(den, 1)
            v.wait_ge(den, 1)
            v.reciprocal(dn[:, 1, :], dn[:, 0, :]).then_inc(rden, 1)
            v.wait_ge(rden, 1)
            v.tensor_tensor(w[:, :, :], e[:, :, :], dn[:, 1, :].unsqueeze(2).to_broadcast(wide), ALU.mult).then_inc(weight, 1)
            v.wait_ge(picked, 1)
            a, z, s, m = sel, c0, 1, 0
            while s < ED:
                v.tensor_tensor(z[:, :, s:], a[:, :, s:], a[:, :, 0:ED - s], ALU.add).then_inc(step, 1)
                v.tensor_copy(z[:, :, 0:s], a[:, :, 0:s]).then_inc(step, 1)
                m += 2
                v.wait_ge(step, m)
                a, z, s = z, (c1 if z is c0 else c0), 2 * s
            v.tensor_tensor(z[:, :, :], a[:, :, :], sel[:, :, :], ALU.mult).then_inc(step, 1)
            v.wait_ge(step, m + 1)
            four = [P, NT, KD, ED]
            v.tensor_tensor(hot[:, :, :, :], z[:, :, :].unsqueeze(2).to_broadcast(four),
                            k.number[:, :].unsqueeze(1).unsqueeze(3).to_broadcast(four), ALU.is_equal).then_inc(step, 1)
            v.wait_ge(counted, 1)
            pps = ps[:, 3, 0:NT * ED].rearrange("p (t e) -> p t e", e=ED)
            v.tensor_tensor(pos[:, :, :], pps, k.carry[:, :].unsqueeze(1).to_broadcast(wide), ALU.add).then_inc(step, 1)
            v.wait_ge(step, m + 3)
            v.tensor_tensor(k.carry[:, :], k.carry[:, :], ps[:, 3, NT * ED:(NT + 1) * ED], ALU.add).then_inc(step, 1)
            v.tensor_scalar(ok[:, :, :], pos[:, :, :], float(CAP), None, ALU.is_lt).then_inc(step, 1)
            v.tensor_tensor(c0[:, :, :] if z is not c0 else c1[:, :, :], pos[:, :, :],
                            k.base[:, :].unsqueeze(1).to_broadcast(wide), ALU.add).then_inc(step, 1)
            y = c0 if z is not c0 else c1
            v.wait_ge(step, m + 6)
            v.tensor_tensor(pos[:, :, :], y[:, :, :], ok[:, :, :], ALU.mult).then_inc(step, 1)
            v.wait_ge(step, m + 7)
            v.tensor_scalar(y[:, :, :], pos[:, :, :], float(NSLOT), None, ALU.add).then_inc(step, 1)
            v.wait_ge(step, m + 8)
            v.tensor_tensor(prod[:, :, :, :], hot[:, :, :, :], y[:, :, :].unsqueeze(2).to_broadcast(four),
                            ALU.mult).then_inc(step, 1)
            v.wait_ge(step, m + 9)
            v.tensor_reduce(slotf[:, :], prod[:, :, :, :].rearrange("p t k e -> p (t k) e"), AX_X, ALU.add).then_inc(step, 1)
            v.wait_ge(step, m + 10)
            v.tensor_copy(slot[:, :], slotf[:, :]).then_inc(slotted, 1)
            v.tensor_tensor(prod[:, :, :, :], hot[:, :, :, :], w[:, :, :].unsqueeze(2).to_broadcast(four),
                            ALU.mult).then_inc(step, 1)
            v.wait_ge(step, m + 11)
            v.tensor_reduce(wk[:, :], prod[:, :, :, :].rearrange("p t k e -> p (t k) e"), AX_X, ALU.add).then_inc(slotted, 1)

        @block.gpsimd
        def _(g):
            g.wait_ge(slotted, 1)
            g.wait_ge(k.zeroed, 16 * ZFILL)
            for t in range(NT):
                for i in range(KD):
                    j = t * KD + i
                    g.indirect_dma_start(out=k.table_in[:, :], out_offset=bass.IndirectOffsetOnAxis(
                        ap=slot[:, j:j + 1], axis=0), in_=k.xn[:, t, :], in_offset=None,
                        bounds_check=NSLOT - 1, oob_is_err=False).then_inc(k.scattered, 16)
            g.wait_ge(k.scattered, (b + 1) * (16 * NT * KD))

        @block.sync
        def _(sp):
            sp.wait_ge(slotted, 2)
            sp.dma_start(k.slots[bass.ds(b, 1)].rearrange("a p j -> p (a j)"), slot[:, :]).then_inc(saved, 16)
            sp.dma_start(k.choice_w[bass.ds(b, 1)].rearrange("a p j -> p (a j)"), wk[:, :]).then_inc(saved, 16)
            sp.wait_ge(saved, 32)


def experts(k, A):
    nc, ps = k.nc, k.ps
    ld = [k.sem(f"e_ld{i}") for i in range(3)]
    (turned, bT_ev, g_mm, u_mm, silu, h_done, d_mm, o_ev, zero_row, zero_stored) = (
        k.sem("e_" + x) for x in ("turned", "bT_ev", "g_mm", "u_mm", "silu", "h", "d_mm", "o_ev", "zero_row", "zero_stored"))
    stored = [k.sem(f"e_stored{i}") for i in range(2)]
    FH = FD // 2
    with ExitStack() as own:
        up = k.sb(own, "e_up", [P, 3, NC, 2 * FD])
        down = k.sb(own, "e_down", [FH, 3, 2, D])
        buf = k.sb(own, "e_buf", [P, 3, 2, D])
        bT = k.sb(own, "e_bT", [P, 2, NC, CAP])
        sg = k.sb(own, "e_sg", [FH, 2, 2, CAP])
        hT = k.sb(own, "e_hT", [FH, 2, 2, CAP])
        o = k.sb(own, "e_o", [P, 2, 2, D])
        zrow = k.sb(own, "e_zrow", [1, D])
        block = own.enter_context(nc.Block())

        @block.sync
        def _(sp):
            for e in range(ED):
                if e >= 3:
                    sp.wait_ge(d_mm, e - 2)
                i = e % 3
                sp.dma_start(buf[:, i], k.table_in[e * CAP:(e + 1) * CAP].rearrange("(s p) d -> p s d", p=P)).then_inc(ld[i], 16)
                sp.dma_start(up[:, i], A["D_up"][e].rearrange("(c p) f -> p c f", p=P)).then_inc(ld[i], 16)
                sp.dma_start(down[:, i], A["D_down"][e].rearrange("(j f) d -> f j d", f=FH)).then_inc(ld[i], 16)

        @block.tensor
        def _(pe):
            def turn(e):
                pe.wait_ge(ld[e % 3], 48 * (e // 3 + 1))
                if e >= 2:
                    pe.wait_ge(bT_ev, e - 1)
                for c in range(NC):
                    for s in range(2):
                        mm = pe.transpose(ps[:, e % 2, c * CAP + s * P:c * CAP + (s + 1) * P],
                                          buf[:, e % 3, s, c * P:(c + 1) * P], k.ident[:, :])
                mm.then_inc(turned, 1)

            def out_of(e):
                pe.wait_ge(h_done, e + 1)
                if e >= 2:
                    pe.wait_ge(o_ev, e - 1)
                for s in range(2):
                    for j in range(2):
                        mm = pe.matmul(ps[:, 6 + e % 2, s * D:(s + 1) * D], hT[:, e % 2, j, s * P:(s + 1) * P],
                                       down[:, e % 3, j, :], start=j == 0, stop=j == 1)
                mm.then_inc(d_mm, 1)

            turn(0)
            for e in range(ED):
                if e + 1 < ED:
                    turn(e + 1)
                pe.wait_ge(bT_ev, e + 1)
                if e >= 2:
                    pe.wait_ge(h_done, e - 1)
                for part, done in ((0, g_mm), (1, u_mm)):
                    for j in range(2):
                        for c in range(NC):
                            mm = pe.matmul(ps[0:FH, 2 + 2 * part + e % 2, j * CAP:(j + 1) * CAP],
                                           up[:, e % 3, c, part * FD + j * FH:part * FD + (j + 1) * FH],
                                           bT[:, e % 2, c, :], start=c == 0, stop=c == NC - 1)
                    mm.then_inc(done, 1)
                if e >= 1:
                    out_of(e - 1)
            out_of(ED - 1)

        @block.scalar
        def _(act):
            act.wait_ge(zero_row, 1)
            act.dma_start(k.table_out[NSLOT:NSLOT + 1, :], zrow[:, :]).then_inc(zero_stored, 16)

            def store(e):
                act.wait_ge(o_ev, e + 1)
                act.dma_start(k.table_out[e * CAP:(e + 1) * CAP].rearrange("(s p) d -> p s d", p=P),
                              o[:, e % 2]).then_inc(stored[e % 2], 16)

            for e in range(ED):
                if e >= 2:
                    store(e - 2)
                act.wait_ge(turned, e + 1)
                if e >= 2:
                    act.wait_ge(u_mm, e - 1)
                nc.scalar.copy(bT[:, e % 2].rearrange("p c s -> p (c s)"), ps[:, e % 2, :]).then_inc(bT_ev, 1)
                act.wait_ge(g_mm, e + 1)
                if e >= 2:
                    act.wait_ge(h_done, e - 1)
                nc.scalar.activation(sg[:, e % 2].rearrange("p c s -> p (c s)"), ps[0:FH, 2 + e % 2, :],
                                     ACT.Silu).then_inc(silu, 1)
            store(ED - 2)
            store(ED - 1)
            for i in range(2):
                act.wait_ge(stored[i], 16 * (ED // 2))
            act.wait_ge(zero_stored, 16)

        @block.vector
        def _(v):
            v.memset(zrow[:, :], 0.0).then_inc(zero_row, 1)

            def read_out(e):
                v.wait_ge(d_mm, e + 1)
                if e >= 2:
                    v.wait_ge(stored[e % 2], 16 * (e // 2))
                v.tensor_copy(o[:, e % 2].rearrange("p s d -> p (s d)"), ps[:, 6 + e % 2, :]).then_inc(o_ev, 1)

            for e in range(ED):
                v.wait_ge(silu, e + 1)
                v.wait_ge(u_mm, e + 1)
                if e >= 2:
                    v.wait_ge(d_mm, e - 1)
                v.tensor_tensor(hT[:, e % 2].rearrange("p c s -> p (c s)"), sg[:, e % 2].rearrange("p c s -> p (c s)"),
                                ps[0:FH, 4 + e % 2, :], ALU.mult).then_inc(h_done, 1)
                if e >= 1:
                    read_out(e - 1)
            read_out(ED - 1)


def combine(k, out):
    nc = k.nc
    NTT = NB * NT
    ld_x = [k.sem(f"g_x{i}") for i in range(2)]
    stored = [k.sem(f"g_out{i}") for i in range(2)]
    ld_w, acc = k.sem("g_ld_w"), k.sem("g_acc")
    with ExitStack() as own:
        slot = k.sb(own, "g_slot", [P, NB, NT * KD], I32)
        wk = k.sb(own, "g_wk", [P, NB, NT * KD])
        rows = k.sb(own, "g_rows", [P, 2, KD, D])
        x = k.sb(own, "g_x", [P, 2, D])
        block = own.enter_context(nc.Block())
        xt = k.x_mid.rearrange("b (t p) d -> (b t) p d", p=P)
        ot = out.rearrange("b (t p) d -> (b t) p d", p=P)

        @block.sync
        def _(sp):
            sp.dma_start(slot[:, :, :], k.slots.rearrange("b p j -> p b j")).then_inc(ld_w, 16)
            sp.dma_start(wk[:, :, :], k.choice_w.rearrange("b p j -> p b j")).then_inc(ld_w, 16)
            for t in range(NTT + 1):
                if t < NTT:
                    if t >= 2:
                        sp.wait_ge(stored[t % 2], 16 * (t // 2))
                    sp.dma_start(x[:, t % 2, :], xt[t]).then_inc(ld_x[t % 2], 16)
                if t >= 1:
                    sp.wait_ge(acc, KD * t)
                    sp.dma_start(ot[t - 1], x[:, (t - 1) % 2, :]).then_inc(stored[(t - 1) % 2], 16)
            for i in range(2):
                sp.wait_ge(stored[i], 16 * (NTT // 2))

        @block.gpsimd
        def _(g):
            g.wait_ge(ld_w, 32)
            for t in range(NTT):
                if t >= 2:
                    g.wait_ge(acc, KD * (t - 1))
                for i in range(KD):
                    j = (t % NT) * KD + i
                    g.indirect_dma_start(out=rows[:, t % 2, i, :], out_offset=None, in_=k.table_out[:, :],
                                         in_offset=bass.IndirectOffsetOnAxis(ap=slot[:, t // NT, j:j + 1], axis=0),
                                         bounds_check=NSLOT, oob_is_err=False).then_inc(k.gathered[t % 2], 16)

        @block.vector
        def _(v):
            v.wait_ge(ld_w, 32)
            for t in range(NTT):
                v.wait_ge(ld_x[t % 2], 16 * (t // 2 + 1))
                v.wait_ge(k.gathered[t % 2], 16 * KD * (t // 2 + 1))
                for i in range(KD):
                    j = (t % NT) * KD + i
                    if i:
                        v.wait_ge(acc, KD * t + i)
                    v.scalar_tensor_tensor(out=x[:, t % 2, :], in0=rows[:, t % 2, i, :], scalar=wk[:, t // NT, j:j + 1],
                                           in1=x[:, t % 2, :], op0=ALU.mult, op1=ALU.add).then_inc(acc, 1)


class Row(Build):

    def __init__(self, nc, ctx):
        super().__init__(nc, ctx)

        def sb(name, shape, dt=F32):
            return self.sb(ctx, name, shape, dt)

        def dram(name, shape, dt):
            return nc.dram_tensor(name, shape, dt, kind="Internal").ap()

        self.ps = ctx.enter_context(nc.psum_tensor("ps", [P, 8, BANK], F32))
        self.ident = sb("ident", [P, P])
        self.identb = sb("identb", [P, P], BF16)
        self.causal = sb("causal", [P, P], BF16)
        self.sel = sb("sel", [P, NJ, P], BF16)
        self.eps = sb("eps", [P, 1])
        self.desc = sb("desc", [P, EB])
        self.stats = sb("stats", [P, NT, 6])
        self.mv = sb("mv", [P, NT, 2])
        self.std = sb("std", [P, NT])
        self.rstd = sb("rstd", [P, NT])
        self.x = sb("x", [P, NT, D])
        self.xn = sb("xn", [P, NT, D])
        self.xT = sb("xT", [P, NC, S])
        self.gp = sb("gp", [P, NT, P], BF16)
        self.wqA, self.wkTA, self.wvA = (sb(x, [P, NC, D]) for x in ("wqA", "wkTA", "wvA"))
        self.bqA, self.bkA, self.bqC, self.bkC = (sb(x, [P, NC]) for x in ("bqA", "bkA", "bqC", "bkC"))
        self.bvA, self.bvC, self.boC = (sb(x, [P, D]) for x in ("bvA", "bvC", "boC"))
        self.wqB, self.wkB = (sb(x, [P, NC, HB * DB]) for x in ("wqB", "wkB"))
        self.wgB = sb("wgB", [P, NC, HB * EB])
        self.wqC, self.wkC, self.wvC, self.woC = (sb(x, [P, NC, D]) for x in ("wqC", "wkC", "wvC", "woC"))
        self.q_parts = dram("q_parts", [3, D, S], BF16)
        self.k_parts = dram("k_parts", [3, D, SK], BF16)
        self.x_mid = dram("x_mid", [NB, S, D], F32)
        self.table_in = dram("table_in", [NSLOT, D], F32)
        self.table_out = dram("table_out", [NSLOT + 1, D], F32)
        self.slots = dram("slots", [NB, P, NT * KD], I32)
        self.choice_w = dram("choice_w", [NB, P, NT * KD], F32)
        self.onesb = sb("onesb", [P, P], BF16)
        self.before = sb("before", [P, P], BF16)
        self.number = sb("number", [P, KD])
        self.base = sb("base", [P, ED])
        self.carry = sb("carry", [P, ED])
        self.wgD = sb("wgD", [P, NC, ED])

        self.zeroed = ctx.enter_context(nc.semaphore("zeroed"))
        self.scattered = ctx.enter_context(nc.semaphore("scattered"))
        self.gathered = [ctx.enter_context(nc.semaphore(f"gathered{i}")) for i in range(2)]

    def weights(self, A):
        for dst, src in ((self.wqA, "A_wq"), (self.wkTA, "A_wkT"), (self.wvA, "A_wv"), (self.wqB, "B_wq"),
                         (self.wkB, "B_wk"), (self.wgB, "B_wg"), (self.wqC, "C_wq"), (self.wkC, "C_wk"),
                         (self.wvC, "C_wv"), (self.woC, "C_wo"), (self.wgD, "D_wg")):
            yield dst[:, :, :], A[src].rearrange("(c p) n -> p c n", p=P)
        for dst, src in ((self.bqA, "A_bq"), (self.bkA, "A_bk"), (self.bqC, "C_bq"), (self.bkC, "C_bk")):
            yield dst[:, :], A[src]
        for dst, src in ((self.bvA, "A_bv"), (self.bvC, "C_bv"), (self.boC, "C_bo")):
            yield dst[:, :], A[src].partition_broadcast(P)


def program(nc, A, out):
    with ExitStack() as whole:
        k = Row(nc, whole)
        with k.semaphores():
            setup(k, A)
        with nc.Fori(0, NB) as b:
            with k.semaphores(), ExitStack() as second:
                k.vxB = k.sb(second, "vxB", [P, NC, HB, EB * DB])
                k.oxB = k.sb(second, "oxB", [P, HB, NJ, D])
                attention_a(k, A, b)
                attention_b(k, A, b)
            with k.semaphores():
                with ExitStack() as third:
                    k.maskN = k.sb(third, "maskN", [P, NT, SK], BF16)
                    k.maskT = k.sb(third, "maskT", [P, NKT, S], BF16)
                    vaug = k.sb(third, "vaug", [P, NKT, HC, VW])
                    project_c(k, A, b, vaug)
                    attention_c(k, A, b, vaug)
                route(k, A, b)
        with k.semaphores():
            experts(k, A)
            combine(k, out)


def layouts(i):
    import numpy as _np

    c = _np.ascontiguousarray
    vx, ox = _np.asarray(i["L0_ffn_value_experts"]), _np.asarray(i["L0_ffn_output_experts"])
    ctx, mask = _np.asarray(i["ctx_1024"]), _np.asarray(i["mask_Bx1xSxS2_ik1"])[:, 0]
    T = lambda x: _np.asarray(x).T
    cols = lambda x: _np.asarray(x).reshape(-1, 128).T
    a = {
        "x": i["x"], "ctx": ctx, "ctxT": ctx.transpose(0, 2, 1), "mask": mask, "maskT": mask.transpose(0, 2, 1),
        "A_wq": i["L0_xattn_Wq"], "A_wkT": T(i["L0_xattn_Wk"]), "A_wv": i["L0_xattn_Wv"],
        "A_bq": cols(i["L0_xattn_bq"]), "A_bk": cols(i["L0_xattn_bk"]), "A_bv": i["L0_xattn_bv"],
        "B_wq": i["L0_ffn_w_q"], "B_wk": i["L0_ffn_w_k"], "B_wg": i["L0_ffn_w_gate"],
        "B_vx": vx.transpose(2, 1, 0, 3).reshape(256, 8, 512),
        "B_ox": ox.transpose(1, 0, 2, 3).reshape(8, 4, 2, 64, 256),
        "C_wq": T(i["L1_xattn_wq_w"]), "C_wk": T(i["L1_xattn_wk_w"]), "C_wv": T(i["L1_xattn_wv_w"]),
        "C_wo": T(i["L1_xattn_fo_w"]), "C_bq": cols(i["L1_xattn_wq_b"]), "C_bk": cols(i["L1_xattn_wk_b"]),
        "C_bv": i["L1_xattn_wv_b"], "C_bo": i["L1_xattn_fo_b"],
        "D_wg": T(i["L1_ffn_gate_weight"]),
        "D_up": _np.asarray(i["L1_ffn_gate_up_proj"]).transpose(0, 2, 1),
        "D_down": _np.asarray(i["L1_ffn_down_proj"]).transpose(0, 2, 1),
    }
    return {n: c(_np.asarray(x)) for n, x in a.items()}


def kernel(**inputs):
    import concourse.bacc as _bacc
    from concourse.bass_utils import run_bass_kernel_spmd as _run

    nc = _bacc.Bacc("TRN2", target_bir_lowering=False, num_devices=1)
    arrays, A = {}, {}
    for name, a in layouts(inputs).items():
        arrays[f"in_{name}"] = a
        A[name] = nc.dram_tensor(f"in_{name}", a.shape, mybir.dt.from_np(a.dtype), kind="ExternalInput").ap()
    out = nc.dram_tensor("out_0", (NB, S, D), F32, kind="ExternalOutput").ap()
    program(nc, A, out)
    r = _run(nc, [arrays], core_ids=[0])
    return r.results[0]["out_0"]
```

```python
from contextlib import ExitStack, contextmanager

import numpy as np

import concourse.bass as bass
from concourse import mybir

ALU = mybir.AluOpType
ACT = mybir.ActivationFunctionType
AX_X = mybir.AxisListType.X
F32 = mybir.dt.float32
BF16 = mybir.dt.bfloat16
I32 = mybir.dt.int32

P = 128
NB, S, D = 4, 512, 256
SK = 1601
NT = S // P
NC = D // P
NKT = -(-SK // P)
KW = [min(P, SK - P * i) for i in range(NKT)]
BANK = 512
NKC = -(-SK // BANK)
KC = [min(BANK, SK - BANK * i) for i in range(NKC)]
EPS = 1e-5
SCALE_A = float(D) ** -0.5

HB, DB, EB = 8, 64, 8
SCALE_B = float(DB) ** -0.5
NJ = EB // 2

HC, DC = 16, 16
SCALE_C = float(D) ** -0.5
NG, GH = 4, 4
NS = 3
VW = 32
TERMS = [(0, 0), (0, 1), (0, 2), (1, 0), (1, 1), (2, 0)]
KROWS = len(TERMS) * DC
MASKED = -1e20

ED, KD = 32, 8
CAP, FD = 256, 192
NSLOT = ED * CAP
NE = 6
ZFILL = NSLOT // S
TWO_ONES = float(np.array(0x3F803F80, np.uint32).view(np.float32))


class Build:

    def __init__(self, nc, ctx):
        self.nc, self.ctx = nc, ctx
        self.sems = []

    def sb(self, ctx, name, shape, dt=F32):
        return ctx.enter_context(self.nc.sbuf_tensor(name, shape, dt))

    def sem(self, name):
        s = self.ctx.enter_context(self.nc.semaphore(name))
        self.sems.append(s)
        return s


    @contextmanager
    def semaphores(self):
        self.sems = []
        with ExitStack() as self.ctx:
            yield
            numbers = sorted(s.num for s in self.sems)
            self.nc.sync.sem_clear(range(numbers[0], numbers[-1] + 1))
            self.nc.all_engine_barrier()


class NormSems:

    def __init__(self, k, layer):
        self.stats = k.sem(f"{layer}_stats")
        self.aggr = k.sem(f"{layer}_aggr")
        self.std = k.sem(f"{layer}_std")
        self.rstd = k.sem(f"{layer}_rstd")
        self.normed = k.sem(f"{layer}_normed")
        self.turned = k.sem(f"{layer}_turned")
        self.xT_a = k.sem(f"{layer}_xT_a")
        self.xT_v = k.sem(f"{layer}_xT_v")


def norm_vector(v, k, n, x, xn):
    for t in range(NT):
        v.bn_stats(k.stats[:, t, :], x[:, t, :]).then_inc(n.stats, 1)
    for t in range(NT):
        v.wait_ge(n.stats, t + 1)
        v.bn_aggr(k.mv[:, t, :], k.stats[:, t, :]).then_inc(n.aggr, 1)
    v.wait_ge(n.std, 1)
    v.reciprocal(k.rstd[:, :], k.std[:, :]).then_inc(n.rstd, 1)
    v.wait_ge(n.rstd, 1)
    for t in range(NT):
        v.tensor_scalar(xn[:, t, :], x[:, t, :], k.mv[:, t, 0:1], k.rstd[:, t:t + 1],
                        ALU.subtract, ALU.mult).then_inc(n.normed, 1)


def norm_scalar(act, k, n):
    act.wait_ge(n.aggr, NT)
    k.nc.scalar.activation(k.std[:, :], k.mv[:, :, 1], ACT.Sqrt, bias=k.eps[:, 0:1]).then_inc(n.std, 1)


def norm_tensor(pe, k, n, xn):
    for t in range(NT):
        pe.wait_ge(n.normed, t + 1)
        for c in range(NC):
            mm = pe.transpose(k.ps[:, c, t * P:(t + 1) * P], xn[:, t, c * P:(c + 1) * P], k.ident[:, :])
    mm.then_inc(n.turned, 1)


def turned_scalar(act, k, n, xT):
    act.wait_ge(n.turned, 1)
    k.nc.scalar.copy(xT[:, 0, :], k.ps[:, 0, :]).then_inc(n.xT_a, 1)


def turned_vector(v, k, n, xT):
    v.wait_ge(n.turned, 1)
    v.tensor_copy(xT[:, 1, :], k.ps[:, 1, :]).then_inc(n.xT_v, 1)


def turned_wait(eng, n):
    eng.wait_ge(n.xT_a, 1)
    eng.wait_ge(n.xT_v, 1)


def setup(k, A):
    nc = k.nc
    ones_done, sel_done, loaded, eps_done = (k.sem(x) for x in ("set_zero", "set_sel", "set_weights", "set_eps"))
    zeros_done = k.sem("set_zeros")
    with nc.Block(no_gpsimd_drain=True) as block:

        @block.gpsimd
        def _(g):
            g.wait_ge(zeros_done, 2)
            for i in range(ZFILL):
                g.dma_start(k.table_in.rearrange("(i p t) d -> i p t d", i=ZFILL, p=P)[i], k.xr[:, :, :]).then_inc(k.scattered, 16)
            g.memset(k.ident[:, :], 0.0).then_inc(ones_done, 1)
            g.memset(k.identb[:, :], 0.0).then_inc(ones_done, 1)
            g.memset(k.causal[:, :], 0.0).then_inc(ones_done, 1)
            g.memset(k.sel[:, :, :], 0.0).then_inc(ones_done, 1)
            g.memset(k.onesb[:, :], 1.0).then_inc(ones_done, 1)
            g.memset(k.before[:, :], 0.0).then_inc(ones_done, 1)
            g.wait_ge(ones_done, 6)
            g.affine_select(out=k.before[:, :], in_=k.before[:, :], compare_op=ALU.is_ge, fill=1.0, base=0,
                            pattern=[[-1, P]], channel_multiplier=1).then_inc(sel_done, 1)
            for m in (k.ident, k.identb):
                g.affine_select(out=m[:, :], in_=m[:, :], compare_op=ALU.not_equal, fill=1.0, base=0,
                                pattern=[[-1, P]], channel_multiplier=1).then_inc(sel_done, 1)
            g.affine_select(out=k.causal[:, :], in_=k.causal[:, :], compare_op=ALU.is_ge, fill=MASKED, base=0,
                            pattern=[[-1, P]], channel_multiplier=1).then_inc(sel_done, 1)
            for part in range(3):
                g.wait_ge(sel_done, 4 + part)
                v = k.sel[:, :, :].rearrange("p j (a i) -> p j a i", a=2)
                g.affine_select(out=v, in_=v, compare_op=ALU.not_equal, fill=1.0, base=-EB * part,
                                pattern=[[-2, NJ], [-1, 2], [0, DB]], channel_multiplier=1).then_inc(sel_done, 1)
            g.wait_ge(sel_done, 7)

        @block.vector
        def _(v):
            v.memset(k.xr[:, :, :], 0.0).then_inc(zeros_done, 1)
            v.memset(k.slot[:, :], NSLOT).then_inc(zeros_done, 1)
            v.memset(k.eps[:, :], EPS).then_inc(eps_done, 1)
            for e in range(EB):
                v.memset(k.desc[:, e:e + 1], float(EB - e)).then_inc(eps_done, 1)
            v.memset(k.gp[:, :, :], 0.0).then_inc(eps_done, 1)
            for i in range(KD):
                v.memset(k.number[:, i:i + 1], float(i + 1)).then_inc(eps_done, 1)
            for e in range(ED):
                v.memset(k.base[:, e:e + 1], float(CAP * e - NSLOT)).then_inc(eps_done, 1)
            v.memset(k.carry[:, :], 0.0).then_inc(eps_done, 1)

        @block.sync
        def _(sp):
            n = 0
            for dst, src in k.weights(A):
                sp.dma_start(dst, src).then_inc(loaded, 16)
                n += 1
            sp.wait_ge(loaded, 16 * n)


def scatter_rows(g, k):
    for t in range(NT):
        for i in range(KD):
            j = t * KD + i
            g.indirect_dma_start(out=k.table_in[:, :], out_offset=bass.IndirectOffsetOnAxis(
                ap=k.slot[:, j:j + 1], axis=0), in_=k.xr[:, t, :], in_offset=None,
                bounds_check=NSLOT - 1, oob_is_err=False).then_inc(k.scattered, 16)


def attention_a(k, A, b):
    k.ld_vx, k.ld_ox = k.sem("ld_vx"), k.sem("ld_ox")
    nc, ps = k.nc, k.ps
    n = NormSems(k, "na")
    (ld_x, ld_ctxT, ld_ctx, q_mm, q_ev, qk_mm, qk_ev, kb_mm, kb_ev, s_mm, top, top2, bias, exped, turned,
     pt_v, pt_a, pv_mm, o_ev, f_mm, f_ev, rsum, xb_done) = (
        k.sem("a_" + x) for x in (
            "ld_x", "ld_ctxT", "ld_ctx", "q_mm", "q_ev", "qk_mm", "qk_ev", "kb_mm", "kb_ev", "s_mm", "top", "top2",
            "bias", "exp", "turned", "pt_v", "pt_a", "pv_mm", "o_ev", "f_mm", "f_ev", "rsum", "xb"))
    with ExitStack() as own:
        ctxN = k.sb(own, "ctxN", [P, NKT, D])
        qT = k.sb(own, "a_qT", [P, NC, S])
        qk = k.sb(own, "a_qk", [P, NC, S])
        kb = k.sb(own, "a_kb", [P, NT])
        mx = k.sb(own, "a_mx", [P, 3, NT])
        rs = k.sb(own, "a_rs", [P, 2, NT])
        prob = k.sb(own, "a_prob", [P, 2, SK])
        pT = k.sb(own, "a_pT", [P, NKT, P])
        oT = k.sb(own, "a_oT", [P, NC, P])
        xb = k.sb(own, "a_xb", [P, NT, D])
        ctxT = k.sb(own, "a_ctxT", [P, NC, SK])
        block = own.enter_context(nc.Block())

        @block.sync
        def _(sp):
            sp.dma_start(k.x[:, :, :], A["x"][bass.ds(b, 1)].rearrange("a (t p) d -> p (a t) d", p=P)).then_inc(ld_x, 16)
            sp.dma_start(ctxT[:, :, :], A["ctxT"][bass.ds(b, 1)].rearrange("a (c p) s -> p (a c) s", p=P)).then_inc(ld_ctxT, 16)
            sp.dma_start(ctxN[:, 0:NKT - 1, :], A["ctx"][bass.ds(b, 1), 0:P * (NKT - 1)].rearrange(
                "a (t p) d -> p (a t) d", p=P)).then_inc(ld_ctx, 16)
            sp.dma_start(ctxN[0:KW[-1], NKT - 1, :], A["ctx"][bass.ds(b, 1), P * (NKT - 1):SK].rearrange(
                "a p d -> p (a d)")).then_inc(ld_ctx, 16)
            for c in range(NC):
                sp.dma_start(k.vxB[:, c], A["B_vx"][c * P:(c + 1) * P].rearrange("p h n -> p h n")).then_inc(k.ld_vx, 16)
            for a in range(2):
                for h in range(0, HB, 4):
                    sp.dma_start(k.oxB[a * DB:(a + 1) * DB, h:h + 4], A["B_ox"][h:h + 4, :, a].rearrange(
                        "h j p n -> p h j n")).then_inc(k.ld_ox, 16)

        @block.gpsimd
        def _(g):
            g.wait_ge(ld_x, 16)
            g.tensor_tensor(xb[:, :, :], k.x[:, :, :], k.bvA[:, :].unsqueeze(1).to_broadcast([P, NT, D]),
                            ALU.add).then_inc(xb_done, 1)
            scatter_rows(g, k)

        @block.tensor
        def _(pe):
            norm_tensor(pe, k, n, k.xn)
            turned_wait(pe, n)
            for m in range(NC):
                for c in range(NC):
                    mm = pe.matmul(ps[:, 2 + m, :], k.wqA[:, c, m * P:(m + 1) * P], k.xT[:, c, :],
                                   start=c == 0, stop=c == NC - 1)
                mm.then_inc(q_mm, 1)
            pe.wait_ge(q_ev, NC)
            for m in range(NC):
                for c in range(NC):
                    mm = pe.matmul(ps[:, 4 + m, :], k.wkTA[:, c, m * P:(m + 1) * P], qT[:, c, :],
                                   start=c == 0, stop=c == NC - 1)
                mm.then_inc(qk_mm, 1)
            for t in range(NT):
                for c in range(NC):
                    mm = pe.matmul(ps[:, 6, t:t + 1], qT[:, c, t * P:(t + 1) * P], k.bkA[:, c:c + 1],
                                   start=c == 0, stop=c == NC - 1)
            mm.then_inc(kb_mm, 1)

            def scores(t):
                if t == 0:
                    pe.wait_ge(qk_ev, NC)
                    pe.wait_ge(ld_ctxT, 16)
                else:
                    pe.wait_ge(exped, t)
                for i in range(NKC):
                    for c in range(NC):
                        mm = pe.matmul(ps[:, i, 0:KC[i]], qk[:, c, t * P:(t + 1) * P],
                                       ctxT[:, c, i * BANK:i * BANK + KC[i]], start=c == 0, stop=c == NC - 1)
                mm.then_inc(s_mm, 1)

            def turn(t):
                pe.wait_ge(exped, t + 1)
                for g in range(NKC):
                    if (t, g) == (0, 0):
                        pe.wait_ge(qk_ev, NC)
                    if g % 2 == 0 and 2 * t + g // 2 > 0:
                        pe.wait_ge(pt_v, 2 * t + g // 2)
                    if g % 2 == 1 and 2 * t + g // 2 > 0:
                        pe.wait_ge(pt_a, 2 * t + g // 2)
                    for i in range(4 * g, min(4 * g + 4, NKT)):
                        mm = pe.transpose(ps[0:KW[i], 4 + g % 2, (i - 4 * g) * P:(i - 4 * g + 1) * P],
                                          prob[:, t % 2, i * P:i * P + KW[i]], k.ident[:, :])
                    mm.then_inc(turned, 1)

            def context(t):
                pe.wait_ge(pt_v, 2 * t + 2)
                pe.wait_ge(pt_a, 2 * t + 2)
                if t == 0:
                    pe.wait_ge(ld_ctx, 32)
                    pe.wait_ge(kb_ev, 1)
                else:
                    pe.wait_ge(o_ev, t)
                for m in range(NC):
                    for i in range(NKT):
                        mm = pe.matmul(ps[:, 6, m * P:(m + 1) * P], ctxN[0:KW[i], i, m * P:(m + 1) * P],
                                       pT[0:KW[i], i, :], start=i == 0, stop=i == NKT - 1)
                mm.then_inc(pv_mm, 1)

            def project(t):
                pe.wait_ge(o_ev, t + 1)
                if t >= 1:
                    pe.wait_ge(f_ev, t)
                for c in range(NC):
                    mm = pe.matmul(ps[:, 7, 0:D], oT[:, c, :], k.wvA[:, c, :], start=c == 0, stop=c == NC - 1)
                mm.then_inc(f_mm, 1)

            for i in range(NT + 2):
                if i < NT:
                    scores(i)
                if i >= 2:
                    project(i - 2)
                if 1 <= i <= NT:
                    turn(i - 1)
                    context(i - 1)

        @block.scalar
        def _(act):
            norm_scalar(act, k, n)
            turned_scalar(act, k, n, k.xT)
            for m in range(NC):
                act.wait_ge(q_mm, m + 1)
                nc.scalar.activation(qT[:, m, :], ps[:, 2 + m, :], ACT.Identity,
                                     bias=k.bqA[:, m:m + 1]).then_inc(q_ev, 1)
            for i in range(NT + 1):
                if i < NT:
                    act.wait_ge(bias, i + 1)
                    if i >= 2:
                        act.wait_ge(turned, NKC * (i - 1))
                    nc.scalar.activation(prob[:, i % 2, :], ps[:, 0:4, :].rearrange("p a n -> p (a n)")[:, 0:SK],
                                         ACT.Exp, bias=mx[:, 2, i:i + 1], scale=SCALE_A,
                                         accum_out=rs[:, 0, i:i + 1]).then_inc(exped, 1)
                if i >= 1:
                    t = i - 1
                    for g in (1, 3):
                        act.wait_ge(turned, NKC * t + g + 1)
                        w = min(4, NKT - 4 * g)
                        rows = P if w == 4 else KW[-1]
                        nc.scalar.copy(pT[0:rows, 4 * g:4 * g + w, :],
                                       ps[0:rows, 4 + g % 2, 0:w * P].rearrange("p (a n) -> p a n", n=P)).then_inc(pt_a, 1)
                    act.wait_ge(pv_mm, t + 1)
                    nc.scalar.copy(oT[:, :, :].rearrange("p c n -> p (c n)"), ps[:, 6, 0:D]).then_inc(o_ev, 1)

        @block.vector
        def _(v):
            v.wait_ge(ld_x, 16)
            norm_vector(v, k, n, k.x, k.xn)
            turned_vector(v, k, n, k.xT)
            for m in range(NC):
                v.wait_ge(qk_mm, m + 1)
                v.tensor_copy(qk[:, m, :], ps[:, 4 + m, :]).then_inc(qk_ev, 1)
            v.wait_ge(kb_mm, 1)
            v.tensor_copy(kb[:, :], ps[:, 6, 0:NT]).then_inc(kb_ev, 1)
            v.wait_ge(kb_ev, 1)

            def finish(t):
                v.wait_ge(exped, t + 1)
                v.reciprocal(rs[:, 1, t:t + 1], rs[:, 0, t:t + 1]).then_inc(rsum, 1)
                v.wait_ge(rsum, t + 1)
                v.wait_ge(f_mm, t + 1)
                v.wait_ge(xb_done, 1)
                v.scalar_tensor_tensor(out=k.x[:, t, :], in0=ps[:, 7, 0:D], scalar=rs[:, 1, t:t + 1],
                                       in1=xb[:, t, :], op0=ALU.mult, op1=ALU.add).then_inc(f_ev, 1)

            for i in range(NT + 2):
                if i < NT:
                    v.wait_ge(s_mm, i + 1)
                    v.tensor_reduce(mx[:, 0, i:i + 1], ps[:, 0:4, :].rearrange("p a n -> p (a n)")[:, 0:SK],
                                    AX_X, ALU.max).then_inc(top, 1)
                    v.wait_ge(top, i + 1)
                    v.tensor_tensor(mx[:, 1, i:i + 1], mx[:, 0, i:i + 1], kb[:, i:i + 1], ALU.add).then_inc(top2, 1)
                    v.wait_ge(top2, i + 1)
                    v.tensor_scalar(mx[:, 2, i:i + 1], mx[:, 1, i:i + 1], kb[:, i:i + 1], -SCALE_A, ALU.subtract,
                                    ALU.mult).then_inc(bias, 1)
                if i >= 2:
                    finish(i - 2)
                if 1 <= i <= NT:
                    t = i - 1
                    for g in (0, 2):
                        v.wait_ge(turned, NKC * t + g + 1)
                        v.tensor_copy(pT[:, 4 * g:4 * g + 4, :],
                                      ps[:, 4 + g % 2, :].rearrange("p (a n) -> p a n", n=P)).then_inc(pt_v, 1)


def attention_b(k, A, b):
    nc, ps = k.nc, k.ps
    n = NormSems(k, "nb")
    (qk_mm, q_ev, k_ev, g_mm, g_exp, g_one, g_sig, g_top, g_eq, g_key, g_first, g_pick, g_gm, val_mm, val_mul,
     val_sum, val_two, s_mm, top, exped, rinv, gp_done, turned, g_turned, ev_a, ev_v, pv_mm, o_ev, sel_mm, out_mm, x_done, zero_q, split) = (
        k.sem("b_" + x) for x in (
            "qk_mm", "q_ev", "k_ev", "g_mm", "g_exp", "g_one", "g_sig", "g_top", "g_eq", "g_key", "g_first",
            "g_pick", "g_gm", "val_mm", "val_mul", "val_sum", "val_two", "s_mm", "top", "exp", "rinv", "gp", "turned",
            "g_turned", "ev_a", "ev_v", "pv_mm", "o_ev", "sel_mm", "out_mm", "x_done", "zero_q", "split"))
    SC = [(1, 384), (2, 0), (1, 0), (0, 0)]
    ORDER = [3, 1, 0, 2]
    DONE = [1, 2, 4, 4]
    OFF = [0, 512, 896, 1152]
    POFF = [0, P, 3 * P, 6 * P]
    with ExitStack() as own:
        qz = k.sb(own, "b_qz", [P, HB, S])
        kT = k.sb(own, "b_kT", [P, HB // 2, S])
        gate = k.sb(own, "b_gate", [P, 3, NT * HB * EB])
        gtop = k.sb(own, "b_gtop", [P, 2, NT * HB])
        gm = k.sb(own, "b_gm", [P, NT, HB, EB])
        tmp = k.sb(own, "b_tmp", [P, 2, EB * DB])
        val = k.sb(own, "b_val", [P, NT, HB, 2, DB])
        mx = k.sb(own, "b_mx", [P, HB, NT])
        rs = k.sb(own, "b_rs", [P, HB, NT])
        ri = k.sb(own, "b_ri", [P, HB, NT])
        prob = k.sb(own, "b_prob", [P, 2, 10 * P])
        pT = k.sb(own, "b_pT", [P, 10 * P])
        oT = k.sb(own, "b_oT", [P, S])
        gr = k.sb(own, "b_gr", [P, 2, NT, EB])
        gT = k.sb(own, "b_gT", [P, S], BF16)
        og = k.sb(own, "b_og", [P, 2, NJ, S])
        gp = k.gp
        block = own.enter_context(nc.Block())

        @block.gpsimd
        def _(g):
            g.memset(qz[:, :, :], 0.0).then_inc(zero_q, 1)
            for u in range(HB * NT):
                h, t = u // NT, u % NT
                g.wait_ge(val_sum, u + 1)
                g.tensor_copy(val[:, t, h, 1, :], val[:, t, h, 0, :]).then_inc(val_two, 1)

        @block.tensor
        def _(pe):
            norm_tensor(pe, k, n, k.xn)
            turned_wait(pe, n)
            for m in range(HB // 2):
                for i, w in enumerate((k.wqB, k.wkB)):
                    if m >= 2:
                        pe.wait_ge((q_ev, k_ev)[i], (2 * (m - 1), m - 1)[i])
                    for c in range(NC):
                        mm = pe.matmul(ps[:, 2 + 2 * i + m % 2, :], w[:, c, m * P:(m + 1) * P], k.xT[:, c, :],
                                       start=c == 0, stop=c == NC - 1)
                    mm.then_inc(qk_mm, 1)
            for t in range(NT):
                for c in range(NC):
                    mm = pe.matmul(ps[:, 6, t * HB * EB:(t + 1) * HB * EB], k.xT[:, c, t * P:(t + 1) * P],
                                   k.wgB[:, c, :], start=c == 0, stop=c == NC - 1)
            mm.then_inc(g_mm, 1)
            pe.wait_ge(k.ld_vx, 16 * NC)
            for u in range(HB * NT):
                h, t = u // NT, u % NT
                if u >= 2:
                    pe.wait_ge(val_mul, u - 1)
                for c in range(NC):
                    mm = pe.matmul(ps[:, u % 2, :], k.xT[:, c, t * P:(t + 1) * P], k.vxB[:, c, h, :],
                                   start=c == 0, stop=c == NC - 1)
                mm.then_inc(val_mm, 1)

            def scores(h):
                if h == 0:
                    pe.wait_ge(val_mul, HB * NT)
                    pe.wait_ge(q_ev, HB)
                    pe.wait_ge(k_ev, HB // 2)
                for o, t in enumerate(ORDER):
                    if h >= 1:
                        pe.wait_ge(exped, NT * (h - 1) + DONE[o])
                    bank, off = SC[t]
                    pe.matmul(ps[:, bank, off:off + (t + 1) * P], qz[:, h, t * P:(t + 1) * P],
                              kT[:, h // 2, 0:(t + 1) * P], start=True, stop=False)
                    mm = pe.matmul(ps[:, bank, off + t * P:off + (t + 1) * P], k.identb[:, :], k.causal[:, :],
                                   start=False, stop=True)
                    mm.then_inc(s_mm, 1)

            def turn(h):
                pe.wait_ge(exped, NT * (h + 1))
                for g, blocks in enumerate(([(t, 0) for t in range(4)], [(t, 1) for t in range(1, 4)],
                                            [(2, 2), (3, 2), (3, 3)])):
                    if g < 2 and h >= 1:
                        pe.wait_ge(ev_v, 6 * (h - 1) + 5 + g)
                    if g == 2:
                        pe.wait_ge(ev_a, 2 * h + 1)
                    for a, (t, i) in enumerate(blocks):
                        mm = pe.transpose(ps[:, 3 + g % 2, a * P:(a + 1) * P],
                                          prob[:, h % 2, POFF[t] + i * P:POFF[t] + (i + 1) * P], k.ident[:, :])
                    mm.then_inc(turned, 1)

            def gates(h):
                pe.wait_ge(gp_done, h + 1)
                pe.wait_ge(ev_v, 6 * h + 1)
                for t in range(NT):
                    mm = pe.transpose(ps[:, 4, 0:BANK // 2].bitcast(BF16)[:, t * P:(t + 1) * P], gp[:, t, :],
                                      k.identb[:, :])
                mm.then_inc(g_turned, 1)
                for j in range(NJ):
                    if j == 0:
                        pe.wait_ge(ev_a, 2 * h + 2)
                    pe.wait_ge(ev_v, 6 * h + (2, 2, 3, 4)[j])
                    pe.matmul(ps[:, 3 + j % 2, :], k.sel[:, j, :], gT[:, :], start=True, stop=True).then_inc(sel_mm, 1)

            def values(h):
                pe.wait_ge(ev_a, 2 * h + 2)
                pe.wait_ge(ev_v, 6 * h + 1)
                pe.wait_ge(val_two, NT * (h + 1))
                if h >= 1:
                    pe.wait_ge(o_ev, h)
                for i in range(NT):
                    mm = pe.matmul(ps[:, 5, i * P:S],
                                   val[:, i, h, :, :].rearrange("p a d -> p (a d)"),
                                   pT[:, OFF[i]:OFF[i] + S - i * P], start=i == 0, stop=i == NT - 1)
                mm.then_inc(pv_mm, 1)

            def out(h):
                pe.wait_ge(ev_v, 6 * (h + 1))
                for j in range(NJ):
                    for t in range(NT):
                        first = (h, j) == (0, 0)
                        mm = pe.matmul(ps[:, 6 + t // 2, (t % 2) * D:(t % 2 + 1) * D], og[:, h % 2, j, t * P:(t + 1) * P],
                                       k.oxB[:, h, j, :], start=first and t % 2 == 0,
                                       stop=(h, j) == (HB - 1, NJ - 1) and t % 2 == 1, skip_group_check=True)
                mm.then_inc(out_mm, 1)

            pe.wait_ge(g_exp, 1)
            pe.wait_ge(k.ld_ox, 16 * 4)
            scores(0)
            for h in range(HB):
                turn(h)
                if h + 1 < HB:
                    scores(h + 1)
                values(h)
                gates(h)
                if h >= 1:
                    out(h - 1)
            out(HB - 1)

        @block.scalar
        def _(act):
            norm_scalar(act, k, n)
            turned_scalar(act, k, n, k.xT)
            act.wait_ge(zero_q, 1)
            for m in range(HB // 2):
                act.wait_ge(qk_mm, 2 * m + 1)
                for a in range(2):
                    nc.scalar.mul(qz[DB * a:DB * a + DB, 2 * m + a, :], ps[DB * a:DB * a + DB, 2 + m % 2, :],
                                  SCALE_B).then_inc(q_ev, 1)
            act.wait_ge(g_mm, 1)
            nc.scalar.activation(gate[:, 0, :], ps[:, 6, 0:NT * HB * EB], ACT.Exp, scale=-1.0).then_inc(g_exp, 1)

            def probabilities(h):
                for o, t in enumerate(ORDER):
                    act.wait_ge(top, NT * h + DONE[o])
                    if h >= 2 and o == 0:
                        act.wait_ge(turned, 3 * (h - 1))
                    bank, off = SC[t]
                    nc.scalar.activation(prob[:, h % 2, POFF[t]:POFF[t] + (t + 1) * P],
                                         ps[:, bank, off:off + (t + 1) * P], ACT.Exp, bias=mx[:, h, t:t + 1],
                                         accum_out=rs[:, h, t:t + 1]).then_inc(exped, 1)

            def read_turned(h):
                for g in (0, 2):
                    act.wait_ge(turned, 3 * h + g + 1)
                    w = (4, 3, 3)[g] * P
                    nc.scalar.copy(pT[:, OFF[g]:OFF[g] + w], ps[:, 3 + g % 2, 0:w]).then_inc(ev_a, 1)

            probabilities(0)
            for h in range(HB):
                read_turned(h)
                if h + 1 < HB:
                    probabilities(h + 1)
                act.wait_ge(pv_mm, h + 1)
                if h >= 1:
                    act.wait_ge(ev_v, 6 * h)
                nc.scalar.copy(oT[:, :], ps[:, 5, :]).then_inc(o_ev, 1)

        @block.vector
        def _(v):
            norm_vector(v, k, n, k.x, k.xn)
            turned_vector(v, k, n, k.xT)
            for m in range(HB // 2):
                v.wait_ge(qk_mm, 2 * m + 2)
                v.tensor_copy(kT[:, m, :], ps[:, 4 + m % 2, :]).then_inc(k_ev, 1)
            v.wait_ge(g_exp, 1)
            v.tensor_scalar(gate[:, 1, :], gate[:, 0, :], 1.0, None, ALU.add).then_inc(g_one, 1)
            v.wait_ge(g_one, 1)
            v.reciprocal(gate[:, 2, :], gate[:, 1, :]).then_inc(g_sig, 1)
            v.wait_ge(g_sig, 1)
            g8 = [gate[:, i, :].rearrange("p (a e) -> p a e", e=EB) for i in range(3)]
            wide = [P, NT * HB, EB]
            v.tensor_reduce(gtop[:, 0, :], g8[2], AX_X, ALU.max).then_inc(g_top, 1)
            v.wait_ge(g_top, 1)
            v.tensor_tensor(g8[0], g8[2], gtop[:, 0, :].unsqueeze(2).to_broadcast(wide), ALU.is_equal).then_inc(g_eq, 1)
            v.wait_ge(g_eq, 1)
            v.tensor_tensor(g8[1], g8[0], k.desc[:, :].unsqueeze(1).to_broadcast(wide), ALU.mult).then_inc(g_key, 1)
            v.wait_ge(g_key, 1)
            v.tensor_reduce(gtop[:, 1, :], g8[1], AX_X, ALU.max).then_inc(g_first, 1)
            v.wait_ge(g_first, 1)
            v.tensor_tensor(g8[0], g8[1], gtop[:, 1, :].unsqueeze(2).to_broadcast(wide), ALU.is_equal).then_inc(g_pick, 1)
            v.wait_ge(g_pick, 1)
            gma = gm[:, :, :, :].rearrange("p t h e -> p (t h) e")
            v.tensor_tensor(gma, g8[0], g8[2], ALU.mult).then_inc(g_gm, 1)
            v.wait_ge(g_gm, 1)
            for u in range(HB * NT):
                h, t = u // NT, u % NT
                v.wait_ge(val_mm, u + 1)
                if u >= 2:
                    v.wait_ge(val_sum, u - 1)
                v.tensor_tensor(tmp[:, u % 2, :].rearrange("p (e d) -> p e d", e=EB),
                                ps[:, u % 2, :].rearrange("p (e d) -> p e d", e=EB),
                                gm[:, t, h, :].unsqueeze(2).to_broadcast([P, EB, DB]), ALU.mult).then_inc(val_mul, 1)
                v.wait_ge(val_mul, u + 1)
                v.tensor_reduce(val[:, t, h, 0, :], tmp[:, u % 2, :].rearrange("p (e d) -> p d e", e=EB), AX_X,
                                ALU.add).then_inc(val_sum, 1)

            def maxima(h):
                for o, t in enumerate(ORDER):
                    v.wait_ge(s_mm, NT * h + DONE[o])
                    bank, off = SC[t]
                    v.tensor_reduce(mx[:, h, t:t + 1], ps[:, bank, off:off + (t + 1) * P], AX_X, ALU.max,
                                    negate=True).then_inc(top, 1)

            def split_gates(h):
                gs = split
                v.wait_ge(exped, NT * (h + 1))
                v.reciprocal(ri[:, h, :], rs[:, h, :]).then_inc(rinv, 1)
                v.wait_ge(rinv, h + 1)
                v.tensor_tensor(gr[:, 0, :, :], gm[:, :, h, :], ri[:, h, :].unsqueeze(2).to_broadcast([P, NT, EB]),
                                ALU.mult).then_inc(gs, 1)
                if h >= 1:
                    v.wait_ge(g_turned, h)
                v.wait_ge(gs, 4 * h + 1)
                v.tensor_copy(gp[:, :, 0:EB], gr[:, 0, :, :]).then_inc(gs, 1)
                v.wait_ge(gs, 4 * h + 2)
                v.tensor_tensor(gr[:, 1, :, :], gr[:, 0, :, :], gp[:, :, 0:EB], ALU.subtract).then_inc(gs, 1)
                v.wait_ge(gs, 4 * h + 3)
                v.tensor_copy(gp[:, :, EB:2 * EB], gr[:, 1, :, :]).then_inc(gs, 1)
                v.wait_ge(gs, 4 * h + 4)
                v.tensor_tensor(gp[:, :, 2 * EB:3 * EB], gr[:, 1, :, :], gp[:, :, EB:2 * EB],
                                ALU.subtract).then_inc(gp_done, 1)

            maxima(0)
            for h in range(HB):
                v.wait_ge(turned, 3 * h + 2)
                v.tensor_copy(pT[:, OFF[1]:OFF[1] + 3 * P], ps[:, 4, 0:3 * P]).then_inc(ev_v, 1)
                split_gates(h)
                if h + 1 < HB:
                    maxima(h + 1)
                v.wait_ge(g_turned, h + 1)
                v.tensor_copy(gT[:, :], ps[:, 4, 0:BANK // 2].bitcast(BF16)).then_inc(ev_v, 1)
                v.wait_ge(o_ev, h + 1)
                if h >= 2:
                    v.wait_ge(out_mm, h - 1)
                for j in range(NJ):
                    v.wait_ge(sel_mm, NJ * h + j + 1)
                    v.tensor_tensor(og[:, h % 2, j, :], oT[:, :], ps[:, 3 + j % 2, :], ALU.mult).then_inc(ev_v, 1)
            v.wait_ge(out_mm, HB)
            for t in range(NT):
                v.tensor_tensor(k.x[:, t, :], k.x[:, t, :], ps[:, 6 + t // 2, (t % 2) * D:(t % 2 + 1) * D],
                                ALU.add).then_inc(x_done, 1)


def split3(v, sem, at, f, parts, rest):
    v.tensor_copy(parts[0], f).then_inc(sem, 1)
    v.wait_ge(sem, at + 1)
    v.tensor_tensor(rest, f, parts[0], ALU.subtract).then_inc(sem, 1)
    v.wait_ge(sem, at + 2)
    v.tensor_copy(parts[1], rest).then_inc(sem, 1)
    v.wait_ge(sem, at + 3)
    v.tensor_tensor(parts[2], rest, parts[1], ALU.subtract).then_inc(sem, 1)
    return at + 4


def context_c(k, A, b):
    nc, ps = k.nc, k.ps
    ld_ctxT = [k.sem(f"x_ld_ctxT{i}") for i in range(2)]
    (k_mm, k_ev, v_mm, v_ev, split_k, stored) = (
        k.sem("x_" + x) for x in ("k_mm", "k_ev", "v_mm", "v_ev", "split_k", "stored"))
    with ExitStack() as own:
        kf = k.sb(own, "x_kf", [P, NC, SK])
        k3 = k.sb(own, "x_k3", [P, 2, 3, NC, SK], BF16)
        rest = k.sb(own, "x_rest", [P, 2, SK])
        vf = k.sb(own, "x_vf", [P, 2, NKT, D])
        ctxT = k.sb(own, "x_ctxT", [P, 2, NC, SK])
        block = own.enter_context(nc.Block())

        @block.sync
        def _(sp):
            for r in range(2):
                sp.dma_start(ctxT[:, r], A["ctxT"][bass.ds(2 * b + r, 1)].rearrange("a (c p) s -> p (a c) s", p=P)).then_inc(ld_ctxT[r], 16)
            for r in range(2):
                for m in range(NC):
                    sp.wait_ge(split_k, 4 * (NC * r + m + 1))
                    sp.dma_start(k.k_parts[bass.ds(2 * b + r, 1), :, m * P:(m + 1) * P, :].rearrange("a i p s -> p (a i) s"),
                                 k3[:, r, :, m, :]).then_inc(stored, 16)
                sp.wait_ge(v_ev, NKT * (r + 1))
                sp.dma_start(k.v_all[bass.ds(2 * b + r, 1), :, 0:NKT - 1].rearrange("a p t d -> p (a t) d"),
                             vf[:, r, 0:NKT - 1]).then_inc(stored, 16)
                sp.dma_start(k.v_all[bass.ds(2 * b + r, 1), 0:KW[-1], NKT - 1].rearrange("a p d -> p (a d)"),
                             vf[0:KW[-1], r, NKT - 1]).then_inc(stored, 16)
            sp.wait_ge(stored, 16 * 2 * (NC + 2))

        @block.tensor
        def _(pe):
            for r in range(2):
                pe.wait_ge(ld_ctxT[r], 16)
                for m in range(NC):
                    for i in range(NKC):
                        if r + m:
                            pe.wait_ge(k_ev, NKC * (NC * r + m - 1) + i + 1)
                        for c in range(NC):
                            mm = pe.matmul(ps[:, i, 0:KC[i]], k.wkC[:, c, m * P:(m + 1) * P],
                                           ctxT[:, r, c, i * BANK:i * BANK + KC[i]], start=c == 0, stop=c == NC - 1)
                        mm.then_inc(k_mm, 1)
                for i in range(NKT):
                    n = NKT * r + i
                    if n >= 4:
                        pe.wait_ge(v_ev, n - 3)
                    for c in range(NC):
                        mm = pe.matmul(ps[0:KW[i], 4 + n % 4, 0:D], ctxT[:, r, c, i * P:i * P + KW[i]], k.wvC[:, c, :],
                                       start=c == 0, stop=c == NC - 1)
                    mm.then_inc(v_mm, 1)

        @block.scalar
        def _(act):
            for r in range(2):
                for m in range(NC):
                    if r:
                        act.wait_ge(split_k, 4 * (m + 1) - 2)
                    for i in range(NKC):
                        act.wait_ge(k_mm, NKC * (NC * r + m) + i + 1)
                        nc.scalar.activation(kf[:, m, i * BANK:i * BANK + KC[i]], ps[:, i, 0:KC[i]], ACT.Identity,
                                             bias=k.bkC[:, m:m + 1]).then_inc(k_ev, 1)

        @block.vector
        def _(v):
            at = 0
            for r in range(2):
                for m in range(NC):
                    v.wait_ge(k_ev, NKC * (NC * r + m + 1))
                    if at >= 8:
                        v.wait_ge(split_k, at - 4)
                    at = split3(v, split_k, at, kf[:, m, :], [k3[:, r, i, m, :] for i in range(3)], rest[:, m % 2, :])
                for i in range(NKT):
                    n = NKT * r + i
                    v.wait_ge(v_mm, n + 1)
                    v.tensor_tensor(vf[0:KW[i], r, i, :], ps[0:KW[i], 4 + n % 4, 0:D], k.bvC[0:KW[i], :], ALU.add).then_inc(v_ev, 1)


def attention_c(k, A, b):
    nc, ps = k.nc, k.ps
    n = NormSems(k, "nc")
    ld_maskN = [k.sem(f"c_ld_maskN{i}") for i in range(2)]
    ld_maskT = [k.sem(f"c_ld_maskT{i}") for i in range(2)]
    (ld_v, v_ev, q_mm, q_ev, split_q, stored, biasN, biasT, tail) = (
        k.sem("c_" + x) for x in ("ld_v", "v_ev", "q_mm", "q_ev", "split_q", "stored", "biasN", "biasT", "tail"))
    ld_k = [k.sem(f"d_ld_k{i}") for i in range(NS)]
    ld_q = [k.sem(f"d_ld_q{i}") for i in range(NS)]
    (ld_m, mx_mm, mx_v, neg, split_m, m_turned, m_row, s_mm, exped, pv_mm, acc_ev, acc_turned, o_rec,
     o_nat, o_turned, oT_a, oT_v, f_mm, f_ev, xb_done, saved, ones) = (
        k.sem("d_" + x) for x in (
            "ld_m", "mx_mm", "mx_v", "neg", "split_m", "m_turned", "m_row", "s_mm", "exp", "pv_mm",
            "acc_ev", "acc_turned", "o_rec", "o_nat", "o_turned", "oT_a", "oT_v", "f_mm", "f_ev", "xb", "saved", "ones"))
    NU = NT * GH * NKC
    with ExitStack() as own:
        kS = k.sb(own, "kS", [P, NS, GH, SK + SK % 2], BF16)
        qS = k.sb(own, "qS", [P, NS, GH, S], BF16)
        mp = k.sb(own, "d_mp", [P, NT, GH, NKC])
        m1 = k.sb(own, "d_m1", [P, 2, NT * GH])
        m3 = k.sb(own, "d_m3", [P, NT, 3, GH], BF16)
        mrow = k.sb(own, "d_mrow", [3 * GH, S], BF16)
        prob = k.sb(own, "d_prob", [P, 2, GH, S])
        acc = k.sb(own, "d_acc", [P, S])
        rec = k.sb(own, "d_rec", [P, NT, GH])
        oN = k.sb(own, "d_oN", [P, NT, D])
        oT = k.sb(own, "d_oT", [P, NC, S])
        xb = k.sb(own, "d_xb", [P, NT, D])
        maskN = k.sb(own, "maskN", [P, NT, SK], BF16)
        maskT = k.sb(own, "maskT", [P, NKT, S], BF16)
        vaug = k.sb(own, "vaug", [P, NKT, HC, VW])
        q3 = k.sb(own, "c_q3", [P, 3, NC, S], BF16)
        rawN = k.sb(own, "c_rawN", [P, 2, SK], I32)
        rawT = k.sb(own, "c_rawT", [P, 2, 2, S], I32)
        qf, rest = oT, oN[:, :, :].rearrange("p t d -> p (t d)").rearrange("p (c s) -> p c s", c=NC)
        vf = prob[:, :, :, :].rearrange("p a h s -> p (a h s)")[:, 0:NKT * D].rearrange("p (t d) -> p t d", d=D)
        block = own.enter_context(nc.Block())
        pairs = [(i, min(2, NKT - i)) for i in range(0, NKT, 2)]

        def load_q(eng, g):
            for r, (i, j) in enumerate(TERMS):
                eng.dma_start(qS[r * DC:(r + 1) * DC, g % NS, :, :], k.q_parts[j, g * GH * DC:(g + 1) * GH * DC].rearrange(
                    "(h d) s -> d h s", d=DC)).then_inc(ld_q[g % NS], 16)

        @block.sync
        def _(sp):
            def load_k(g):
                for r, (i, j) in enumerate(TERMS):
                    sp.dma_start(kS[r * DC:(r + 1) * DC, g % NS, :, 0:SK], k.k_parts[bass.ds(b, 1), i, g * GH * DC:(g + 1) * GH * DC].rearrange(
                        "a (h d) s -> d (a h) s", d=DC)).then_inc(ld_k[g % NS], 16)

            def load_maskN(t):
                sp.dma_start(rawN[:, t % 2, :], A["mask"][bass.ds(b, 1), t * P:(t + 1) * P].rearrange(
                    "a p s -> p (a s)")).then_inc(ld_maskN[t % 2], 16)

            load_maskN(0)
            load_k(0)
            sp.wait_ge(stored, 16)
            load_maskN(1)
            sp.dma_start(vf[:, 0:NKT - 1, :], k.v_all[bass.ds(b, 1), :, 0:NKT - 1, :].rearrange("a p t d -> p (a t) d")).then_inc(ld_v, 16)
            sp.dma_start(vf[0:KW[-1], NKT - 1, :], k.v_all[bass.ds(b, 1), 0:KW[-1], NKT - 1, :].rearrange("a p d -> p (a d)")).then_inc(ld_v, 16)
            for t in range(2, NT):
                sp.wait_ge(biasN, t - 1)
                load_maskN(t)
            for j, (i, w) in enumerate(pairs):
                if j >= 2:
                    sp.wait_ge(biasT, j - 1)
                rows = KW[i + w - 1]
                sp.dma_start(rawT[0:rows, j % 2, 0:w, :], A["maskT"][bass.ds(b, 1), i * P:i * P + (w - 1) * P + rows].rearrange(
                    "a (w p) s -> p (a w) s", w=w)).then_inc(ld_maskT[j % 2], 16)
            for g in range(1, NS):
                load_k(g)
                load_q(sp, g)
            for g in range(NG):
                sp.wait_ge(m_row, g + 1)
                for i in range(3):
                    sp.dma_start(qS[KROWS + i:KROWS + i + 1, g % NS, :, :],
                                 mrow[i * GH:(i + 1) * GH, :]).then_inc(ld_m, 16)
                if g >= 1 and g + NS - 1 < NG:
                    sp.wait_ge(s_mm, 2 * NKT * g)
                    load_k(g + NS - 1)
                    load_q(sp, g + NS - 1)
            sp.wait_ge(f_ev, NT)
            sp.dma_start(k.x_mid[bass.ds(b, 1)].rearrange("a (t p) d -> p (a t) d", p=P), k.x[:, :, :]).then_inc(saved, 16)
            sp.wait_ge(saved, 16)

        @block.gpsimd
        def _(g):
            for i in range(NS):
                g.memset(kS[KROWS:KROWS + 3, i, :, :].rearrange("p h s -> p (h s)").bitcast(F32), TWO_ONES).then_inc(ones, 1)
            g.wait_ge(ones, NS)
            g.tensor_tensor(xb[:, :, :], k.x[:, :, :], k.boC[:, :].unsqueeze(1).to_broadcast([P, NT, D]),
                            ALU.add).then_inc(xb_done, 1)
            g.memset(vaug[:, :, :, DC:DC + 1], 1.0).then_inc(tail, 1)
            g.memset(vaug[:, :, :, DC + 1:VW], 0.0).then_inc(tail, 1)
            for j, (i, w) in enumerate(pairs):
                g.wait_ge(ld_maskT[j % 2], 16 * (j // 2 + 1))
                g.tensor_scalar(maskT[0:KW[i], i:i + w, :], rawT[0:KW[i], j % 2, 0:w, :], 0.0, MASKED, ALU.is_equal,
                                ALU.mult).then_inc(biasT, 1)

        @block.tensor
        def _(pe):
            def maxima(g, u):
                t, h, i = u // (GH * NKC), u // NKC % GH, u % NKC
                n = NU * g + u
                if u == 0:
                    pe.wait_ge(ld_q[g % NS], 16 * len(TERMS) * (g // NS + 1))
                    pe.wait_ge(ld_k[g % NS], 16 * len(TERMS) * (g // NS + 1))
                if n >= 2:
                    pe.wait_ge(mx_v, n - 1)
                pe.matmul(ps[:, 5 + n % 2, 0:KC[i]], qS[0:KROWS, g % NS, h, t * P:(t + 1) * P],
                          kS[0:KROWS, g % NS, h, i * BANK:i * BANK + KC[i]], start=True, stop=True).then_inc(mx_mm, 1)

            def turn_maxima(g):
                pe.wait_ge(split_m, 4 * (g + 1))
                if g >= 2:
                    pe.wait_ge(o_nat, g - 1)
                for t in range(NT):
                    mm = pe.transpose(ps[0:3 * GH, 7, 0:BANK // 2].bitcast(BF16)[:, t * P:(t + 1) * P],
                                      m3[:, t, :, :].rearrange("p a h -> p (a h)"), k.identb[:, :])
                mm.then_inc(m_turned, 1)

            def scores(g, i, a, between):
                w = KW[i]
                if g == 0 and a == 0 and i % 2 == 0:
                    pe.wait_ge(biasT, i // 2 + 1)
                if i == 0 and a == 0:
                    pe.wait_ge(ld_m, 48 * (g + 1))
                    pe.wait_ge(ones, min(g + 1, NS))
                if g + i >= 1:
                    pe.wait_ge(exped, 2 * (NKT * g + i) - 1 + a)
                for j in range(2):
                    h = 2 * a + j
                    pe.matmul(ps[0:w, h, :], k.identb[0:w, 0:w], maskT[0:w, i, :], start=True, stop=False)
                    mm = pe.matmul(ps[0:w, h, :], kS[0:KROWS + 3, g % NS, h, i * P:i * P + w],
                                   qS[0:KROWS + 3, g % NS, h, :], start=False, stop=True)
                    if j:
                        mm.then_inc(s_mm, 1)
                    between()

            def values(g, i, between):
                w = KW[i]
                pe.wait_ge(exped, 2 * (NKT * g + i) + 2)
                if g == 0 and i == 0:
                    pe.wait_ge(tail, 2)
                    pe.wait_ge(v_ev, 2)
                if g >= 1 and i == 0:
                    pe.wait_ge(acc_ev, g)
                for h in range(GH):
                    mm = pe.matmul(ps[VW * h:VW * (h + 1), 4, :], vaug[0:w, i, GH * g + h, :],
                                   prob[0:w, i % 2, h, :], start=i == 0, stop=i == NKT - 1)
                    if h % 2:
                        between()
                mm.then_inc(pv_mm, 1)

            def turn_out(g):
                pe.wait_ge(acc_ev, g + 1)
                pe.wait_ge(m_row, min(g + 2, NG))
                if g >= 1:
                    pe.wait_ge(o_nat, g)
                for t in range(NT):
                    mm = pe.transpose(ps[:, 7, t * P:(t + 1) * P], acc[:, t * P:(t + 1) * P], k.ident[:, :])
                mm.then_inc(acc_turned, 1)

            norm_tensor(pe, k, n, k.xn)
            turned_wait(pe, n)
            for m in range(NC):
                for c in range(NC):
                    mm = pe.matmul(ps[:, 2 + m, :], k.wqC[:, c, m * P:(m + 1) * P], k.xT[:, c, :],
                                   start=c == 0, stop=c == NC - 1)
                mm.then_inc(q_mm, 1)
            for u in range(NU):
                maxima(0, u)
            turn_maxima(0)
            for g in range(NG):
                chunks = iter(range(NU if g + 1 < NG else 0))

                def maximum():
                    u = next(chunks, None)
                    if u is not None:
                        maxima(g + 1, u)

                for i in range(NKT):
                    scores(g, i, 0, maximum)
                    scores(g, i, 1, maximum)
                    if i == 1 and g >= 1:
                        turn_out(g - 1)
                    if i >= 1:
                        values(g, i - 1, maximum)
                    if i == NKT - 1 and g + 1 < NG:
                        turn_maxima(g + 1)
                values(g, NKT - 1, maximum)
            turn_out(NG - 1)
            for t in range(NT):
                if t == 0:
                    pe.wait_ge(exped, 2 * NKT * NG)
                    pe.wait_ge(o_nat, NG)
                for c in range(NC):
                    mm = pe.transpose(ps[:, c, t * P:(t + 1) * P], oN[:, t, c * P:(c + 1) * P], k.ident[:, :])
            mm.then_inc(o_turned, 1)
            pe.wait_ge(oT_a, 1)
            pe.wait_ge(oT_v, 1)
            for t in range(NT):
                if t >= 2:
                    pe.wait_ge(f_ev, t - 1)
                for c in range(NC):
                    mm = pe.matmul(ps[:, 2 + t % 2, 0:D], oT[:, c, t * P:(t + 1) * P], k.woC[:, c, :],
                                   start=c == 0, stop=c == NC - 1)
                mm.then_inc(f_mm, 1)

        @block.scalar
        def _(act):
            norm_scalar(act, k, n)
            turned_scalar(act, k, n, k.xT)
            for m in range(NC):
                act.wait_ge(q_mm, m + 1)
                nc.scalar.activation(qf[:, m, :], ps[:, 2 + m, :], ACT.Identity,
                                     bias=k.bqC[:, m:m + 1]).then_inc(q_ev, 1)
            act.wait_ge(split_q, 4)
            act.dma_start(k.q_parts.rearrange("i (c p) s -> p i c s", p=P), q3[:, :, :, :]).then_inc(stored, 16)
            act.wait_ge(stored, 16)
            load_q(act, 0)
            act.wait_ge(ld_v, 32)
            act.wait_ge(tail, 2)
            nc.scalar.copy(vaug[:, 0:NKT - 1, :, 0:DC], vf[:, 0:NKT - 1, :].rearrange("p t (h d) -> p t h d", d=DC)).then_inc(v_ev, 1)
            nc.scalar.copy(vaug[0:KW[-1], NKT - 1, :, 0:DC], vf[0:KW[-1], NKT - 1, :].rearrange("p (h d) -> p h d", d=DC)).then_inc(v_ev, 1)
            act.wait_ge(v_ev, 2)
            for g in range(NG):
                for i in range(NKT):
                    w = KW[i]
                    for a in range(2):
                        act.wait_ge(s_mm, 2 * (NKT * g + i) + a + 1)
                        if NKT * g + i >= 2:
                            act.wait_ge(pv_mm, NKT * g + i - 1)
                        nc.scalar.activation(prob[0:w, i % 2, 2 * a:2 * a + 2, :], ps[0:w, 2 * a:2 * a + 2, :],
                                             ACT.Exp, scale=SCALE_C).then_inc(exped, 1)
                act.wait_ge(pv_mm, NKT * (g + 1))
                if g >= 1:
                    act.wait_ge(acc_turned, g)
                nc.scalar.copy(acc[:, :], ps[:, 4, :]).then_inc(acc_ev, 1)
            act.wait_ge(o_turned, 1)
            nc.scalar.copy(oT[:, 0, :], ps[:, 0, :]).then_inc(oT_a, 1)

        @block.vector
        def _(v):
            def maxima(g):
                for u in range(NU):
                    if u == 8 and g >= 2:
                        outputs(g - 2)
                    t, h, i = u // (GH * NKC), u // NKC % GH, u % NKC
                    n = NU * g + u
                    v.wait_ge(mx_mm, n + 1)
                    bank = ps[:, 5 + n % 2, 0:KC[i]]
                    v.tensor_tensor_reduce(bank, bank, maskN[:, t, i * BANK:i * BANK + KC[i]], 1.0, -3.0e38,
                                           ALU.add, ALU.max, mp[:, t, h, i:i + 1]).then_inc(mx_v, 1)
                v.wait_ge(mx_v, NU * (g + 1))
                if g >= 1:
                    v.wait_ge(split_m, 4 * g)
                v.tensor_reduce(m1[:, 0, :], mp[:, :, :, :].rearrange("p t h i -> p (t h) i"), AX_X, ALU.max,
                                negate=True).then_inc(neg, 1)
                v.wait_ge(neg, g + 1)
                if g >= 1:
                    v.wait_ge(m_turned, g)
                f = [m1[:, i, :].rearrange("p (t h) -> p t h", t=NT) for i in range(2)]
                split3(v, split_m, 4 * g, f[0], [m3[:, :, i, :] for i in range(3)], f[1])
                v.wait_ge(m_turned, g + 1)
                if g >= 1:
                    v.wait_ge(ld_m, 48 * g)
                v.tensor_copy(mrow[:, :], ps[0:3 * GH, 7, 0:BANK // 2].bitcast(BF16)).then_inc(m_row, 1)

            def outputs(g):
                v.wait_ge(acc_turned, g + 1)
                o = ps[:, 7, :].rearrange("p (t h c) -> p t h c", t=NT, h=GH)
                v.reciprocal(rec[:, :, :], o[:, :, :, DC]).then_inc(o_rec, 1)
                v.wait_ge(o_rec, g + 1)
                v.tensor_tensor(oN[:, :, GH * DC * g:GH * DC * (g + 1)].rearrange("p t (h c) -> p t h c", h=GH),
                                o[:, :, :, 0:DC], rec[:, :, :].unsqueeze(3).to_broadcast([P, NT, GH, DC]),
                                ALU.mult).then_inc(o_nat, 1)

            norm_vector(v, k, n, k.x, k.xn)
            turned_vector(v, k, n, k.xT)

            def bias(t):
                v.wait_ge(ld_maskN[t % 2], 16 * (t // 2 + 1))
                v.tensor_scalar(maskN[:, t, :], rawN[:, t % 2, :], 0.0, MASKED, ALU.is_equal,
                                ALU.mult).then_inc(biasN, 1)

            bias(0)
            v.wait_ge(q_ev, NC)
            split3(v, split_q, 0, qf[:, :, :], [q3[:, i, :, :] for i in range(3)], rest)
            for t in range(1, NT):
                bias(t)
            v.wait_ge(biasN, NT)
            v.wait_ge(split_q, 4)
            maxima(0)
            for g in range(NG):
                if g + 1 < NG:
                    maxima(g + 1)
            outputs(NG - 2)
            outputs(NG - 1)
            v.wait_ge(o_turned, 1)
            v.tensor_copy(oT[:, 1, :], ps[:, 1, :]).then_inc(oT_v, 1)
            v.wait_ge(xb_done, 1)
            for t in range(NT):
                v.wait_ge(f_mm, t + 1)
                v.tensor_tensor(k.x[:, t, :], ps[:, 2 + t % 2, 0:D], xb[:, t, :], ALU.add).then_inc(f_ev, 1)


def route(k, A, b):
    nc, ps = k.nc, k.ps
    n = NormSems(k, "nd")
    (l_mm, l_top, l_sub, exped, top8, out8, picked, den, rden, weight, step, counted, slotted, saved) = (
        k.sem("r_" + x) for x in (
            "l_mm", "l_top", "l_sub", "exp", "top8", "out8", "picked", "den", "rden", "weight", "step", "counted",
            "slotted", "saved"))
    with ExitStack() as own:
        logit = k.sb(own, "r_logit", [P, NT, ED])
        lmax = k.sb(own, "r_lmax", [P, NT])
        e = k.sb(own, "r_e", [P, NT, ED])
        best = k.sb(own, "r_best", [P, NT, KD])
        rest = k.sb(own, "r_rest", [P, NT, ED])
        sel = k.sb(own, "r_sel", [P, NT, ED])
        selb = k.sb(own, "r_selb", [P, NT, ED], BF16)
        dn = k.sb(own, "r_dn", [P, 2, NT])
        w = k.sb(own, "r_w", [P, NT, ED])
        c0 = k.sb(own, "r_c0", [P, NT, ED])
        c1 = k.sb(own, "r_c1", [P, NT, ED])
        ok = k.sb(own, "r_ok", [P, NT, ED])
        pos = k.sb(own, "r_pos", [P, NT, ED])
        hot = k.sb(own, "r_hot", [P, NT, KD, ED])
        prod = k.sb(own, "r_prod", [P, NT, KD, ED])
        slotf = k.sb(own, "r_slotf", [P, NT * KD])
        wk = k.sb(own, "r_wk", [P, NT * KD])
        block = own.enter_context(nc.Block())

        @block.tensor
        def _(pe):
            norm_tensor(pe, k, n, k.xr)
            turned_wait(pe, n)
            for t in range(NT):
                for c in range(NC):
                    mm = pe.matmul(ps[:, 2, t * ED:(t + 1) * ED], k.xT[:, c, t * P:(t + 1) * P], k.wgD[:, c, :],
                                   start=c == 0, stop=c == NC - 1)
            mm.then_inc(l_mm, 1)
            pe.wait_ge(picked, 2)
            for t in range(NT + 1):
                for i in range(min(t, NT)):
                    mm = pe.matmul(ps[:, 3, t * ED:(t + 1) * ED], k.onesb[:, :], selb[:, i, :], start=i == 0,
                                   stop=t == NT and i == NT - 1)
                if t < NT:
                    mm = pe.matmul(ps[:, 3, t * ED:(t + 1) * ED], k.before[:, :], selb[:, t, :], start=t == 0, stop=True)
            mm.then_inc(counted, 1)

        @block.scalar
        def _(act):
            norm_scalar(act, k, n)
            turned_scalar(act, k, n, k.xT)
            act.wait_ge(l_sub, 1)
            nc.scalar.activation(e[:, :, :], logit[:, :, :], ACT.Exp).then_inc(exped, 1)

        @block.vector
        def _(v):
            norm_vector(v, k, n, k.x, k.xr)
            turned_vector(v, k, n, k.xT)
            wide = [P, NT, ED]
            v.wait_ge(l_mm, 1)
            lps = ps[:, 2, 0:NT * ED].rearrange("p (t e) -> p t e", e=ED)
            v.tensor_reduce(lmax[:, :], lps, AX_X, ALU.max).then_inc(l_top, 1)
            v.wait_ge(l_top, 1)
            v.tensor_tensor(logit[:, :, :], lps, lmax[:, :].unsqueeze(2).to_broadcast(wide), ALU.subtract).then_inc(l_sub, 1)
            v.wait_ge(exped, 1)
            for t in range(NT):
                v.max(best[:, t, :], e[:, t, :]).then_inc(top8, 1)
            for t in range(NT):
                v.wait_ge(top8, t + 1)
                v.match_replace(rest[:, t, :], best[:, t, :], e[:, t, :], -1.0).then_inc(out8, 1)
            v.wait_ge(out8, NT)
            v.tensor_scalar(sel[:, :, :], rest[:, :, :], 0.0, None, ALU.is_lt).then_inc(picked, 1)
            v.tensor_scalar(selb[:, :, :], rest[:, :, :], 0.0, None, ALU.is_lt).then_inc(picked, 1)
            v.tensor_reduce(dn[:, 0, :], best[:, :, :], AX_X, ALU.add).then_inc(den, 1)
            v.wait_ge(den, 1)
            v.reciprocal(dn[:, 1, :], dn[:, 0, :]).then_inc(rden, 1)
            v.wait_ge(rden, 1)
            v.tensor_tensor(w[:, :, :], e[:, :, :], dn[:, 1, :].unsqueeze(2).to_broadcast(wide), ALU.mult).then_inc(weight, 1)
            v.wait_ge(picked, 1)
            a, z, s, m = sel, c0, 1, 0
            while s < ED:
                v.tensor_tensor(z[:, :, s:], a[:, :, s:], a[:, :, 0:ED - s], ALU.add).then_inc(step, 1)
                v.tensor_copy(z[:, :, 0:s], a[:, :, 0:s]).then_inc(step, 1)
                m += 2
                v.wait_ge(step, m)
                a, z, s = z, (c1 if z is c0 else c0), 2 * s
            v.tensor_tensor(z[:, :, :], a[:, :, :], sel[:, :, :], ALU.mult).then_inc(step, 1)
            v.wait_ge(step, m + 1)
            four = [P, NT, KD, ED]
            v.tensor_tensor(hot[:, :, :, :], z[:, :, :].unsqueeze(2).to_broadcast(four),
                            k.number[:, :].unsqueeze(1).unsqueeze(3).to_broadcast(four), ALU.is_equal).then_inc(step, 1)
            v.wait_ge(counted, 1)
            pps = ps[:, 3, 0:NT * ED].rearrange("p (t e) -> p t e", e=ED)
            v.tensor_tensor(pos[:, :, :], pps, k.carry[:, :].unsqueeze(1).to_broadcast(wide), ALU.add).then_inc(step, 1)
            v.wait_ge(step, m + 3)
            v.tensor_tensor(k.carry[:, :], k.carry[:, :], ps[:, 3, NT * ED:(NT + 1) * ED], ALU.add).then_inc(step, 1)
            v.tensor_scalar(ok[:, :, :], pos[:, :, :], float(CAP), None, ALU.is_lt).then_inc(step, 1)
            v.tensor_tensor(c0[:, :, :] if z is not c0 else c1[:, :, :], pos[:, :, :],
                            k.base[:, :].unsqueeze(1).to_broadcast(wide), ALU.add).then_inc(step, 1)
            y = c0 if z is not c0 else c1
            v.wait_ge(step, m + 6)
            v.tensor_tensor(pos[:, :, :], y[:, :, :], ok[:, :, :], ALU.mult).then_inc(step, 1)
            v.wait_ge(step, m + 7)
            v.tensor_scalar(y[:, :, :], pos[:, :, :], float(NSLOT), None, ALU.add).then_inc(step, 1)
            v.wait_ge(step, m + 8)
            v.tensor_tensor(prod[:, :, :, :], hot[:, :, :, :], y[:, :, :].unsqueeze(2).to_broadcast(four),
                            ALU.mult).then_inc(step, 1)
            v.wait_ge(step, m + 9)
            v.tensor_reduce(slotf[:, :], prod[:, :, :, :].rearrange("p t k e -> p (t k) e"), AX_X, ALU.add).then_inc(step, 1)
            v.wait_ge(step, m + 10)
            v.tensor_copy(k.slot[:, :], slotf[:, :]).then_inc(slotted, 1)
            v.tensor_tensor(prod[:, :, :, :], hot[:, :, :, :], w[:, :, :].unsqueeze(2).to_broadcast(four),
                            ALU.mult).then_inc(step, 1)
            v.wait_ge(step, m + 11)
            v.tensor_reduce(wk[:, :], prod[:, :, :, :].rearrange("p t k e -> p (t k) e"), AX_X, ALU.add).then_inc(slotted, 1)

        @block.sync
        def _(sp):
            sp.wait_ge(slotted, 2)
            sp.dma_start(k.slots[bass.ds(b, 1)].rearrange("a p j -> p (a j)"), k.slot[:, :]).then_inc(saved, 16)
            sp.dma_start(k.choice_w[bass.ds(b, 1)].rearrange("a p j -> p (a j)"), wk[:, :]).then_inc(saved, 16)
            sp.wait_ge(saved, 32)


def experts(k, A):
    nc, ps = k.nc, k.ps
    ld = [k.sem(f"e_ld{i}") for i in range(NE)]
    (turned, bT_ev, g_mm, u_mm, silu, h_done, d_mm, o_ev, zero_row, zero_stored) = (
        k.sem("e_" + x) for x in ("turned", "bT_ev", "g_mm", "u_mm", "silu", "h", "d_mm", "o_ev", "zero_row", "zero_stored"))
    stored = [k.sem(f"e_stored{i}") for i in range(2)]
    FH = FD // 2
    with ExitStack() as own:
        up = k.sb(own, "e_up", [P, NE, NC, 2 * FD])
        down = k.sb(own, "e_down", [FH, NE, 2, D])
        buf = k.sb(own, "e_buf", [P, NE, 2, D])
        bT = k.sb(own, "e_bT", [P, 2, NC, CAP])
        sg = k.sb(own, "e_sg", [FH, 2, 2, CAP])
        hT = k.sb(own, "e_hT", [FH, 2, 2, CAP])
        o = k.sb(own, "e_o", [P, 2, 2, D])
        zrow = k.sb(own, "e_zrow", [1, D])
        block = own.enter_context(nc.Block())

        @block.gpsimd
        def _(g):
            scatter_rows(g, k)

        @block.sync
        def _(sp):
            for e in range(ED):
                if e >= NE:
                    sp.wait_ge(d_mm, e - NE + 1)
                i = e % NE
                sp.dma_start(up[:, i], A["D_up"][e]).then_inc(ld[i], 16)
                sp.dma_start(down[:, i], A["D_down"][e]).then_inc(ld[i], 16)
                if e == 0:
                    sp.wait_ge(k.scattered, 16 * ZFILL + 16 * NT * KD * (NB + 1))
                sp.dma_start(buf[:, i], k.table_in[e * CAP:(e + 1) * CAP].rearrange("(p s) d -> p s d", p=P)).then_inc(ld[i], 16)

        @block.tensor
        def _(pe):
            def turn(e):
                pe.wait_ge(ld[e % NE], 48 * (e // NE + 1))
                if e >= 2:
                    pe.wait_ge(bT_ev, e - 1)
                for c in range(NC):
                    for s in range(2):
                        mm = pe.transpose(ps[:, e % 2, c * CAP + s * P:c * CAP + (s + 1) * P],
                                          buf[:, e % NE, s, c * P:(c + 1) * P], k.ident[:, :])
                mm.then_inc(turned, 1)

            def out_of(e):
                pe.wait_ge(h_done, e + 1)
                if e >= 2:
                    pe.wait_ge(o_ev, e - 1)
                for s in range(2):
                    for j in range(2):
                        mm = pe.matmul(ps[:, 6 + e % 2, s * D:(s + 1) * D], hT[:, e % 2, j, s * P:(s + 1) * P],
                                       down[:, e % NE, j, :], start=j == 0, stop=j == 1)
                mm.then_inc(d_mm, 1)

            turn(0)
            for e in range(ED):
                if e + 1 < ED:
                    turn(e + 1)
                pe.wait_ge(bT_ev, e + 1)
                if e >= 2:
                    pe.wait_ge(h_done, e - 1)
                for part, done in ((0, g_mm), (1, u_mm)):
                    for j in range(2):
                        for c in range(NC):
                            mm = pe.matmul(ps[0:FH, 2 + 2 * part + e % 2, j * CAP:(j + 1) * CAP],
                                           up[:, e % NE, c, part * FD + j * FH:part * FD + (j + 1) * FH],
                                           bT[:, e % 2, c, :], start=c == 0, stop=c == NC - 1)
                    mm.then_inc(done, 1)
                if e >= 1:
                    out_of(e - 1)
            out_of(ED - 1)

        @block.scalar
        def _(act):
            act.wait_ge(zero_row, 1)
            act.dma_start(k.table_out[NSLOT:NSLOT + 1, :], zrow[:, :]).then_inc(zero_stored, 16)

            def store(e):
                act.wait_ge(o_ev, e + 1)
                act.dma_start(k.table_out[e * CAP:(e + 1) * CAP].rearrange("(p s) d -> p s d", p=P),
                              o[:, e % 2]).then_inc(stored[e % 2], 16)

            for e in range(ED):
                act.wait_ge(turned, e + 1)
                if e >= 2:
                    act.wait_ge(u_mm, e - 1)
                nc.scalar.copy(bT[:, e % 2].rearrange("p c s -> p (c s)"), ps[:, e % 2, :]).then_inc(bT_ev, 1)
                if e >= 2:
                    store(e - 2)
                act.wait_ge(g_mm, e + 1)
                if e >= 2:
                    act.wait_ge(h_done, e - 1)
                nc.scalar.activation(sg[:, e % 2].rearrange("p c s -> p (c s)"), ps[0:FH, 2 + e % 2, :],
                                     ACT.Silu).then_inc(silu, 1)
            store(ED - 2)
            store(ED - 1)
            for i in range(2):
                act.wait_ge(stored[i], 16 * (ED // 2))
            act.wait_ge(zero_stored, 16)

        @block.vector
        def _(v):
            v.memset(zrow[:, :], 0.0).then_inc(zero_row, 1)

            def read_out(e):
                v.wait_ge(d_mm, e + 1)
                if e >= 2:
                    v.wait_ge(stored[e % 2], 16 * (e // 2))
                v.tensor_copy(o[:, e % 2].rearrange("p s d -> p (s d)"), ps[:, 6 + e % 2, :]).then_inc(o_ev, 1)

            for e in range(ED):
                v.wait_ge(silu, e + 1)
                v.wait_ge(u_mm, e + 1)
                if e >= 2:
                    v.wait_ge(d_mm, e - 1)
                v.tensor_tensor(hT[:, e % 2].rearrange("p c s -> p (c s)"), sg[:, e % 2].rearrange("p c s -> p (c s)"),
                                ps[0:FH, 4 + e % 2, :], ALU.mult).then_inc(h_done, 1)
                if e >= 1:
                    read_out(e - 1)
            read_out(ED - 1)


def combine(k, out):
    nc = k.nc
    NTT = NB * NT
    ld_x = [k.sem(f"g_x{i}") for i in range(2)]
    stored = [k.sem(f"g_out{i}") for i in range(2)]
    ld_w, acc = k.sem("g_ld_w"), k.sem("g_acc")
    with ExitStack() as own:
        slot = k.sb(own, "g_slot", [P, NB, NT * KD], I32)
        wk = k.sb(own, "g_wk", [P, NB, NT * KD])
        rows = k.sb(own, "g_rows", [P, 2, KD, D])
        x = k.sb(own, "g_x", [P, 2, D])
        block = own.enter_context(nc.Block())
        xt = k.x_mid.rearrange("b (t p) d -> (b t) p d", p=P)
        ot = out.rearrange("b (t p) d -> (b t) p d", p=P)

        @block.sync
        def _(sp):
            sp.dma_start(slot[:, :, :], k.slots.rearrange("b p j -> p b j")).then_inc(ld_w, 16)
            sp.dma_start(wk[:, :, :], k.choice_w.rearrange("b p j -> p b j")).then_inc(ld_w, 16)
            for t in range(NTT + 1):
                if t < NTT:
                    if t >= 2:
                        sp.wait_ge(stored[t % 2], 16 * (t // 2))
                    sp.dma_start(x[:, t % 2, :], xt[t]).then_inc(ld_x[t % 2], 16)
                if t >= 1:
                    sp.wait_ge(acc, KD * t)
                    sp.dma_start(ot[t - 1], x[:, (t - 1) % 2, :]).then_inc(stored[(t - 1) % 2], 16)
            for i in range(2):
                sp.wait_ge(stored[i], 16 * (NTT // 2))

        @block.gpsimd
        def _(g):
            g.wait_ge(ld_w, 32)
            for t in range(NTT):
                if t >= 2:
                    g.wait_ge(acc, KD * (t - 1))
                for i in range(KD):
                    j = (t % NT) * KD + i
                    g.indirect_dma_start(out=rows[:, t % 2, i, :], out_offset=None, in_=k.table_out[:, :],
                                         in_offset=bass.IndirectOffsetOnAxis(ap=slot[:, t // NT, j:j + 1], axis=0),
                                         bounds_check=NSLOT, oob_is_err=False).then_inc(k.gathered[t % 2], 16)

        @block.vector
        def _(v):
            v.wait_ge(ld_w, 32)
            for t in range(NTT):
                v.wait_ge(ld_x[t % 2], 16 * (t // 2 + 1))
                v.wait_ge(k.gathered[t % 2], 16 * KD * (t // 2 + 1))
                for i in range(KD):
                    j = (t % NT) * KD + i
                    if i:
                        v.wait_ge(acc, KD * t + i)
                    v.scalar_tensor_tensor(out=x[:, t % 2, :], in0=rows[:, t % 2, i, :], scalar=wk[:, t // NT, j:j + 1],
                                           in1=x[:, t % 2, :], op0=ALU.mult, op1=ALU.add).then_inc(acc, 1)


class Row(Build):

    def __init__(self, nc, ctx):
        super().__init__(nc, ctx)

        def sb(name, shape, dt=F32):
            return self.sb(ctx, name, shape, dt)

        def dram(name, shape, dt):
            return nc.dram_tensor(name, shape, dt, kind="Internal").ap()

        self.ps = ctx.enter_context(nc.psum_tensor("ps", [P, 8, BANK], F32))
        self.ident = sb("ident", [P, P])
        self.identb = sb("identb", [P, P], BF16)
        self.causal = sb("causal", [P, P], BF16)
        self.sel = sb("sel", [P, NJ, P], BF16)
        self.eps = sb("eps", [P, 1])
        self.desc = sb("desc", [P, EB])
        self.stats = sb("stats", [P, NT, 6])
        self.mv = sb("mv", [P, NT, 2])
        self.std = sb("std", [P, NT])
        self.rstd = sb("rstd", [P, NT])
        self.x = sb("x", [P, NT, D])
        self.xn = sb("xn", [P, NT, D])
        self.xT = sb("xT", [P, NC, S])
        self.gp = sb("gp", [P, NT, P], BF16)
        self.wqA, self.wkTA, self.wvA = (sb(x, [P, NC, D]) for x in ("wqA", "wkTA", "wvA"))
        self.bqA, self.bkA, self.bqC, self.bkC = (sb(x, [P, NC]) for x in ("bqA", "bkA", "bqC", "bkC"))
        self.bvA, self.bvC, self.boC = (sb(x, [P, D]) for x in ("bvA", "bvC", "boC"))
        self.wqB, self.wkB = (sb(x, [P, NC, HB * DB]) for x in ("wqB", "wkB"))
        self.wgB = sb("wgB", [P, NC, HB * EB])
        self.wqC, self.wkC, self.wvC, self.woC = (sb(x, [P, NC, D]) for x in ("wqC", "wkC", "wvC", "woC"))
        self.q_parts = dram("q_parts", [3, D, S], BF16)
        self.k_parts = dram("k_parts", [NB, 3, D, SK], BF16)
        self.v_all = dram("v_all", [NB, P, NKT, D], F32)
        self.x_mid = dram("x_mid", [NB, S, D], F32)
        self.table_in = dram("table_in", [NSLOT, D], F32)
        self.table_out = dram("table_out", [NSLOT + 1, D], F32)
        self.slots = dram("slots", [NB, P, NT * KD], I32)
        self.choice_w = dram("choice_w", [NB, P, NT * KD], F32)
        self.onesb = sb("onesb", [P, P], BF16)
        self.before = sb("before", [P, P], BF16)
        self.number = sb("number", [P, KD])
        self.base = sb("base", [P, ED])
        self.carry = sb("carry", [P, ED])
        self.wgD = sb("wgD", [P, NC, ED])

        self.xr = sb("xr", [P, NT, D])
        self.slot = sb("slot", [P, NT * KD], I32)
        self.scattered = ctx.enter_context(nc.semaphore("scattered"))
        self.gathered = [ctx.enter_context(nc.semaphore(f"gathered{i}")) for i in range(2)]

    def weights(self, A):
        for dst, src in ((self.wqA, "A_wq"), (self.wkTA, "A_wkT"), (self.wvA, "A_wv"), (self.wqB, "B_wq"),
                         (self.wkB, "B_wk"), (self.wgB, "B_wg"), (self.wqC, "C_wq"), (self.wkC, "C_wk"),
                         (self.wvC, "C_wv"), (self.woC, "C_wo"), (self.wgD, "D_wg")):
            yield dst[:, :, :], A[src].rearrange("(c p) n -> p c n", p=P)
        for dst, src in ((self.bqA, "A_bq"), (self.bkA, "A_bk"), (self.bqC, "C_bq"), (self.bkC, "C_bk")):
            yield dst[:, :], A[src]
        for dst, src in ((self.bvA, "A_bv"), (self.bvC, "C_bv"), (self.boC, "C_bo")):
            yield dst[:, :], A[src].partition_broadcast(P)


def program(nc, A, out):
    with ExitStack() as whole:
        k = Row(nc, whole)
        with k.semaphores():
            setup(k, A)
        with nc.Fori(0, NB // 2) as b:
            with k.semaphores():
                context_c(k, A, b)
        with nc.Fori(0, NB) as b:
            with k.semaphores(), ExitStack() as second:
                k.vxB = k.sb(second, "vxB", [P, NC, HB, EB * DB])
                k.oxB = k.sb(second, "oxB", [P, HB, NJ, D])
                attention_a(k, A, b)
                attention_b(k, A, b)
            with k.semaphores():
                attention_c(k, A, b)
                route(k, A, b)
        with k.semaphores():
            experts(k, A)
            combine(k, out)


def layouts(i):
    import numpy as _np

    c = _np.ascontiguousarray
    vx, ox = _np.asarray(i["L0_ffn_value_experts"]), _np.asarray(i["L0_ffn_output_experts"])
    ctx, mask = _np.asarray(i["ctx_1024"]), _np.asarray(i["mask_Bx1xSxS2_ik1"])[:, 0]
    T = lambda x: _np.asarray(x).T
    cols = lambda x: _np.asarray(x).reshape(-1, 128).T
    a = {
        "x": i["x"], "ctx": ctx, "ctxT": ctx.transpose(0, 2, 1), "mask": mask, "maskT": mask.transpose(0, 2, 1),
        "A_wq": i["L0_xattn_Wq"], "A_wkT": T(i["L0_xattn_Wk"]), "A_wv": i["L0_xattn_Wv"],
        "A_bq": cols(i["L0_xattn_bq"]), "A_bk": cols(i["L0_xattn_bk"]), "A_bv": i["L0_xattn_bv"],
        "B_wq": i["L0_ffn_w_q"], "B_wk": i["L0_ffn_w_k"], "B_wg": i["L0_ffn_w_gate"],
        "B_vx": vx.transpose(2, 1, 0, 3).reshape(256, 8, 512),
        "B_ox": ox.transpose(1, 0, 2, 3).reshape(8, 4, 2, 64, 256),
        "C_wq": T(i["L1_xattn_wq_w"]), "C_wk": T(i["L1_xattn_wk_w"]), "C_wv": T(i["L1_xattn_wv_w"]),
        "C_wo": T(i["L1_xattn_fo_w"]), "C_bq": cols(i["L1_xattn_wq_b"]), "C_bk": cols(i["L1_xattn_wk_b"]),
        "C_bv": i["L1_xattn_wv_b"], "C_bo": i["L1_xattn_fo_b"],
        "D_wg": T(i["L1_ffn_gate_weight"]),
        "D_up": _np.asarray(i["L1_ffn_gate_up_proj"]).transpose(0, 2, 1).reshape(32, 2, 128, 384).transpose(0, 2, 1, 3),
        "D_down": _np.asarray(i["L1_ffn_down_proj"]).transpose(0, 2, 1).reshape(32, 2, 96, 256).transpose(0, 2, 1, 3),
    }
    return {n: c(_np.asarray(x)) for n, x in a.items()}


def kernel(**inputs):
    import concourse.bacc as _bacc
    from concourse.bass_utils import run_bass_kernel_spmd as _run

    nc = _bacc.Bacc("TRN2", target_bir_lowering=False, num_devices=1)
    arrays, A = {}, {}
    for name, a in layouts(inputs).items():
        arrays[f"in_{name}"] = a
        A[name] = nc.dram_tensor(f"in_{name}", a.shape, mybir.dt.from_np(a.dtype), kind="ExternalInput").ap()
    out = nc.dram_tensor("out_0", (NB, S, D), F32, kind="ExternalOutput").ap()
    program(nc, A, out)
    r = _run(nc, [arrays], core_ids=[0])
    return r.results[0]["out_0"]
```

```python
from contextlib import ExitStack, contextmanager

import numpy as np

import concourse.bass as bass
from concourse import mybir

ALU = mybir.AluOpType
ACT = mybir.ActivationFunctionType
AX_X = mybir.AxisListType.X
F32 = mybir.dt.float32
BF16 = mybir.dt.bfloat16
I32 = mybir.dt.int32

P = 128
NB, S, D = 4, 512, 256
SK = 1601
NT = S // P
NC = D // P
NKT = -(-SK // P)
KW = [min(P, SK - P * i) for i in range(NKT)]
BANK = 512
NKC = -(-SK // BANK)
KC = [min(BANK, SK - BANK * i) for i in range(NKC)]
MC = [402, 400, 400, 399]
MO = [0, 402, 802, 1202]
EPS = 1e-5
SCALE_A = float(D) ** -0.5

HB, DB, EB = 8, 64, 8
SCALE_B = float(DB) ** -0.5
NJ = EB // 2

HC, DC = 16, 16
SCALE_C = float(D) ** -0.5
NG, GH = 4, 4
NS = 3
VW = 32
TERMS = [(0, 0), (0, 1), (0, 2), (1, 0), (1, 1), (2, 0)]
KROWS = len(TERMS) * DC
MASKED = -1e20

ED, KD = 32, 8
CAP, FD = 256, 192
NSLOT = ED * CAP
NTOK = NB * S
SPARE = S + NTOK
WEIGHT, TOKEN = D, D + ED
ROW = TOKEN + 1
NE = 6
NO = 4
AHEAD = 5
FIRST_WEIGHTS = 4
ZFILL = NSLOT // S
TWO_ONES = float(np.array(0x3F803F80, np.uint32).view(np.float32))


class Build:

    def __init__(self, nc, ctx):
        self.nc, self.ctx = nc, ctx
        self.sems = []

    def sb(self, ctx, name, shape, dt=F32):
        return ctx.enter_context(self.nc.sbuf_tensor(name, shape, dt))

    def sem(self, name):
        s = self.ctx.enter_context(self.nc.semaphore(name))
        self.sems.append(s)
        return s


    @contextmanager
    def semaphores(self):
        self.sems = []
        with ExitStack() as self.ctx:
            yield
            numbers = sorted(s.num for s in self.sems)
            self.nc.sync.sem_clear(range(numbers[0], numbers[-1] + 1))
            self.nc.all_engine_barrier()


class NormMemory:

    def __init__(self, sb, name):
        self.stats = sb(f"{name}_stats", [P, NT, 6])
        self.mv = sb(f"{name}_mv", [P, NT, 2])
        self.var = sb(f"{name}_var", [P, NT])
        self.rstd = sb(f"{name}_rstd", [P, NT])
        self.minus_half = sb(f"{name}_minus_half", [P, NT])


class NormSems:

    def __init__(self, k, layer):
        self.memory = k.norm_memory[layer == "nd"]
        self.stats = k.sem(f"{layer}_stats")
        self.aggr = k.sem(f"{layer}_aggr")
        self.var = k.sem(f"{layer}_var")
        self.rstd = k.sem(f"{layer}_rstd")
        self.normed = k.sem(f"{layer}_normed")
        self.turned = k.sem(f"{layer}_turned")
        self.xT_a = k.sem(f"{layer}_xT_a")
        self.xT_v = k.sem(f"{layer}_xT_v")


def norm_vector(v, n, x, xn):
    statistics(v, n, x)
    normalise(v, n, x, xn)


def statistics(v, n, x):
    m = n.memory
    for t in range(NT):
        v.bn_stats(m.stats[:, t, :], x[:, t, :]).then_inc(n.stats, 1)
    for t in range(NT):
        v.wait_ge(n.stats, t + 1)
        v.bn_aggr(m.mv[:, t, :], m.stats[:, t, :]).then_inc(n.aggr, 1)


def normalise(v, n, x, xn):
    m = n.memory
    v.wait_ge(n.rstd, 1)
    for t in range(NT):
        v.tensor_scalar(xn[:, t, :], x[:, t, :], m.mv[:, t, 0:1], m.rstd[:, t:t + 1],
                        ALU.subtract, ALU.mult).then_inc(n.normed, 1)


def norm_gpsimd(g, n):
    m = n.memory
    g.wait_ge(n.aggr, NT)
    g.tensor_scalar(m.var[:, :], m.mv[:, :, 1], EPS, None, ALU.add).then_inc(n.var, 1)
    g.wait_ge(n.var, 1)
    g.tensor_tensor(m.rstd[:, :], m.var[:, :], m.minus_half[:, :], ALU.pow).then_inc(n.rstd, 1)
    g.wait_ge(n.rstd, 1)


def norm_tensor(pe, k, n, xn, bank=0):
    for t in range(NT):
        pe.wait_ge(n.normed, t + 1)
        for c in range(NC):
            mm = pe.transpose(k.ps[:, bank + c, t * P:(t + 1) * P], xn[:, t, c * P:(c + 1) * P], k.ident[:, :])
    mm.then_inc(n.turned, 1)


def turned_scalar(act, k, n, xT, bank=0):
    act.wait_ge(n.turned, 1)
    k.nc.scalar.copy(xT[:, 0, :], k.ps[:, bank, :]).then_inc(n.xT_a, 1)


def turned_vector(v, k, n, xT, bank=0):
    v.wait_ge(n.turned, 1)
    v.tensor_copy(xT[:, 1, :], k.ps[:, bank + 1, :]).then_inc(n.xT_v, 1)


def turned_wait(eng, n):
    eng.wait_ge(n.xT_a, 1)
    eng.wait_ge(n.xT_v, 1)


def setup(k, A):
    nc = k.nc
    ones_done, sel_done, loaded, eps_done = (k.sem(x) for x in ("set_zero", "set_sel", "set_weights", "set_eps"))
    zeros_done, numbered = k.sem("set_zeros"), k.sem("set_numbers")
    with nc.Block(no_gpsimd_drain=True) as block:

        @block.gpsimd
        def _(g):
            number = k.xr[:, :, TOKEN:ROW].bitcast(I32)
            for half in range(2):
                g.iota(number[half * P // 2:(half + 1) * P // 2], pattern=[[1, NT], [0, 1]], base=SPARE,
                       channel_multiplier=NT).then_inc(numbered, 1)
                g.wait_ge(numbered, half + 1)
            g.iota(k.token[:, :], pattern=[[P, NT]], base=0, channel_multiplier=1).then_inc(numbered, 1)
            g.wait_ge(numbered, 3)
            g.wait_ge(zeros_done, 1)
            g.dma_start(k.total[SPARE:SPARE + CAP, :].rearrange("(t p) d -> p t d", p=P),
                        k.xr[:, 0:CAP // P, 0:D]).then_inc(k.scattered, 16)
            g.memset(k.ident[:, :], 0.0).then_inc(ones_done, 1)
            g.memset(k.identb[:, :], 0.0).then_inc(ones_done, 1)
            g.memset(k.causal[:, :], 0.0).then_inc(ones_done, 1)
            g.memset(k.sel[:, :, :], 0.0).then_inc(ones_done, 1)
            g.memset(k.onesb[:, :], 1.0).then_inc(ones_done, 1)
            g.memset(k.before[:, :], 0.0).then_inc(ones_done, 1)
            g.wait_ge(ones_done, 6)
            g.affine_select(out=k.before[:, :], in_=k.before[:, :], compare_op=ALU.is_ge, fill=1.0, base=0,
                            pattern=[[-1, P]], channel_multiplier=1).then_inc(sel_done, 1)
            for m in (k.ident, k.identb):
                g.affine_select(out=m[:, :], in_=m[:, :], compare_op=ALU.not_equal, fill=1.0, base=0,
                                pattern=[[-1, P]], channel_multiplier=1).then_inc(sel_done, 1)
            g.affine_select(out=k.causal[:, :], in_=k.causal[:, :], compare_op=ALU.is_ge, fill=MASKED, base=0,
                            pattern=[[-1, P]], channel_multiplier=1).then_inc(sel_done, 1)
            for part in range(3):
                g.wait_ge(sel_done, 4 + part)
                v = k.sel[:, :, :].rearrange("p j (a i) -> p j a i", a=2)
                g.affine_select(out=v, in_=v, compare_op=ALU.not_equal, fill=1.0, base=-EB * part,
                                pattern=[[-2, NJ], [-1, 2], [0, DB]], channel_multiplier=1).then_inc(sel_done, 1)
            g.wait_ge(sel_done, 7)

        @block.vector
        def _(v):
            v.memset(k.xr[:, :, 0:TOKEN], 0.0).then_inc(zeros_done, 1)
            for m in k.norm_memory:
                v.memset(m.minus_half[:, :], -0.5).then_inc(eps_done, 1)
            v.memset(k.live[:, :], 0.0).then_inc(eps_done, 1)
            for e in range(EB):
                v.memset(k.desc[:, e:e + 1], float(EB - e)).then_inc(eps_done, 1)
            v.memset(k.gp[:, :, :], 0.0).then_inc(eps_done, 1)
            for e in range(ED):
                v.memset(k.base[:, e:e + 1], float(CAP * e - NSLOT)).then_inc(eps_done, 1)
            v.memset(k.carry[:, :], 0.0).then_inc(eps_done, 1)

        @block.sync
        def _(sp):
            weights = list(k.weights(A))
            for i, (dst, src) in enumerate(weights):
                sp.dma_start(dst, src).then_inc(loaded if i < FIRST_WEIGHTS else k.loaded, 16)
            k.late_weights = len(weights) - FIRST_WEIGHTS
            sp.wait_ge(loaded, 16 * FIRST_WEIGHTS)


class Slots:

    def __init__(self, k, own, name):
        self.step = k.sem(f"{name}_step")
        self.c = [k.sb(own, f"{name}_c{i}", [P, NT, ED]) for i in range(2)]
        self.hot = k.sb(own, f"{name}_hot", [P, NT, KD, ED])
        self.prod = k.sb(own, f"{name}_prod", [P, NT, KD, ED])


def find_slots(g, k, u):
    n = 0

    def step(instruction):
        nonlocal n
        instruction.then_inc(u.step, 1)
        n += 1

    a, z, s = k.chosen, u.c[0], 1
    while s < ED:
        step(g.tensor_tensor(z[:, :, s:], a[:, :, s:], a[:, :, 0:ED - s], ALU.add))
        step(g.tensor_copy(z[:, :, 0:s], a[:, :, 0:s]))
        g.wait_ge(u.step, n)
        a, z, s = z, (u.c[1] if z is u.c[0] else u.c[0]), 2 * s
    step(g.tensor_tensor(z[:, :, :], a[:, :, :], k.chosen[:, :, :], ALU.mult))
    g.wait_ge(u.step, n)
    four = [P, NT, KD, ED]
    for i in range(KD):
        step(g.tensor_scalar(u.hot[:, :, i, :], z[:, :, :], float(i + 1), None, ALU.is_equal))
    g.wait_ge(u.step, n)
    step(g.tensor_tensor(u.prod[:, :, :, :], u.hot[:, :, :, :], k.place[:, :, :].unsqueeze(2).to_broadcast(four),
                         ALU.mult))
    g.wait_ge(u.step, n)
    w = ED
    while w > 1:
        w //= 2
        step(g.tensor_tensor(u.prod[:, :, :, 0:w], u.prod[:, :, :, 0:w], u.prod[:, :, :, w:2 * w], ALU.add))
        g.wait_ge(u.step, n)
    step(g.tensor_scalar(k.slot[:, :].rearrange("p (t k) -> p t k", k=KD), u.prod[:, :, :, 0], float(NSLOT), None, ALU.add))
    return n


def scatter_rows(g, k, choices, done):
    for i in choices:
        for t in range(NT):
            j = t * KD + i
            g.indirect_dma_start(out=k.table[:, :], out_offset=bass.IndirectOffsetOnAxis(
                ap=k.slot[:, j:j + 1], axis=0), in_=k.xr[:, t, :], in_offset=None,
                bounds_check=NSLOT - 1, oob_is_err=False).then_inc(done, 16)


class Route:

    def __init__(self, k, own, name):
        self.k = k
        self.n = NormSems(k, "nd")
        (self.l_mm, self.l_top, self.l_sub, self.exped, self.top8, self.out8, self.picked, self.den, self.rden,
         self.weight, self.counted, self.placed, self.carried, self.filled, self.shifted, self.token, self.moved,
         self.alive, self.kept) = (
            k.sem(f"{name}_{x}") for x in (
                "l_mm", "l_top", "l_sub", "exped", "top8", "out8", "picked", "den", "rden", "weight", "counted",
                "placed", "carried", "filled", "shifted", "token", "moved", "alive", "kept"))
        self.x = k.xr[:, :, 0:D]
        self.xT = k.sb(own, f"{name}_xT", [P, NC, S])
        self.lmax = k.sb(own, f"{name}_lmax", [P, NT])
        self.dn = k.sb(own, f"{name}_dn", [P, 2, NT])
        self.best = k.sb(own, f"{name}_best", [P, NT, KD])
        self.selb = k.sb(own, f"{name}_selb", [P, NT, ED], BF16)
        self.logit, self.e, self.rest, self.ok, self.pos, self.far = (
            k.sb(own, f"{name}_{x}", [P, NT, ED]) for x in ("logit", "e", "rest", "ok", "pos", "far"))

    def keep(self, sp, b):
        total = self.k.total[0:SPARE].rearrange("(b t p) d -> b p t d", b=NB + 1, p=P)
        sp.dma_start(total[bass.ds(b, 1)].rearrange("a p t d -> p (a t) d"), self.x).then_inc(self.kept, 16)

    def normalise(self, v):
        v.wait_ge(self.kept, 16)
        normalise(v, self.n, self.x, self.x)

    def turn(self, pe):
        norm_tensor(pe, self.k, self.n, self.x, bank=6)

    def logits(self, pe):
        k = self.k
        turned_wait(pe, self.n)
        for t in range(NT):
            for c in range(NC):
                mm = pe.matmul(k.ps[:, 7, t * ED:(t + 1) * ED], self.xT[:, c, t * P:(t + 1) * P], k.wgD[:, c, :],
                               start=c == 0, stop=c == NC - 1)
        mm.then_inc(self.l_mm, 1)

    def shift(self, v):
        ps = self.k.ps[:, 7, 0:NT * ED].rearrange("p (t e) -> p t e", e=ED)
        v.wait_ge(self.l_mm, 1)
        v.tensor_reduce(self.lmax[:, :], ps, AX_X, ALU.max).then_inc(self.l_top, 1)
        v.wait_ge(self.l_top, 1)
        v.tensor_tensor(self.logit[:, :, :], ps, self.lmax[:, :].unsqueeze(2).to_broadcast([P, NT, ED]),
                        ALU.subtract).then_inc(self.l_sub, 1)

    def exponentials(self, act):
        act.wait_ge(self.l_sub, 1)
        self.k.nc.scalar.activation(self.e[:, :, :], self.logit[:, :, :], ACT.Exp).then_inc(self.exped, 1)

    def choose(self, v):
        k = self.k
        v.wait_ge(self.exped, 1)
        for t in range(NT):
            v.max(self.best[:, t, :], self.e[:, t, :]).then_inc(self.top8, 1)
        for t in range(NT):
            v.wait_ge(self.top8, t + 1)
            v.match_replace(self.rest[:, t, :], self.best[:, t, :], self.e[:, t, :], -1.0).then_inc(self.out8, 1)
        v.wait_ge(self.out8, NT)
        for chosen in (self.selb, k.chosen):
            v.tensor_scalar(chosen[:, :, :], self.rest[:, :, :], 0.0, k.live[:, 0:1], ALU.is_lt,
                            ALU.mult).then_inc(self.picked, 1)
        v.tensor_reduce(self.dn[:, 0, :], self.best[:, :, :], AX_X, ALU.add).then_inc(self.den, 1)
        v.wait_ge(self.den, 1)
        v.reciprocal(self.dn[:, 1, :], self.dn[:, 0, :]).then_inc(self.rden, 1)
        v.wait_ge(self.rden, 1)
        v.tensor_tensor(k.xr[:, :, WEIGHT:TOKEN], self.e[:, :, :], self.dn[:, 1, :].unsqueeze(2).to_broadcast([P, NT, ED]),
                        ALU.mult).then_inc(self.weight, 1)

    def counts(self, pe):
        k = self.k
        at = lambda t: k.ps[:, 7, (NT + t) * ED:(NT + t + 1) * ED]
        pe.wait_ge(self.picked, 1)
        for t in range(NT + 1):
            for i in range(min(t, NT)):
                mm = pe.matmul(at(t), k.onesb[:, :], self.selb[:, i, :], start=i == 0, stop=t == NT and i == NT - 1)
            if t < NT:
                mm = pe.matmul(at(t), k.before[:, :], self.selb[:, t, :], start=t == 0, stop=True)
        mm.then_inc(self.counted, 1)

    def places(self, v):
        k = self.k
        wide = [P, NT, ED]
        v.wait_ge(self.counted, 1)
        ps = k.ps[:, 7, NT * ED:2 * NT * ED].rearrange("p (t e) -> p t e", e=ED)
        v.tensor_tensor(self.pos[:, :, :], ps, k.carry[:, :].unsqueeze(1).to_broadcast(wide), ALU.add).then_inc(self.placed, 1)
        v.wait_ge(self.placed, 1)
        v.tensor_tensor(k.carry[:, :], k.carry[:, :], k.ps[:, 7, 2 * NT * ED:(2 * NT + 1) * ED], ALU.add).then_inc(self.carried, 1)
        v.tensor_scalar(self.ok[:, :, :], self.pos[:, :, :], float(CAP), None, ALU.is_lt).then_inc(self.filled, 1)
        v.tensor_tensor(self.far[:, :, :], self.pos[:, :, :], k.base[:, :].unsqueeze(1).to_broadcast(wide),
                        ALU.add).then_inc(self.shifted, 1)
        v.wait_ge(self.filled, 1)
        v.wait_ge(self.shifted, 1)
        v.tensor_tensor(k.place[:, :, :], self.far[:, :, :], self.ok[:, :, :], ALU.mult).then_inc(self.placed, 1)
        v.wait_ge(self.picked, 2)
        v.memset(k.live[:, :], 1.0).then_inc(self.alive, 1)

    def tokens(self, g):
        k = self.k
        g.tensor_copy(k.xr[:, :, TOKEN].bitcast(I32), k.token[:, :]).then_inc(self.token, 1)
        g.wait_ge(self.token, 1)
        g.tensor_scalar(k.token[:, :], k.token[:, :], float(S), None, ALU.add).then_inc(self.moved, 1)
        g.wait_ge(self.moved, 1)


def attention_a(k, A, b):
    k.ld_vx, k.ld_ox = k.sem("ld_vx"), k.sem("ld_ox")
    nc, ps = k.nc, k.ps
    n = NormSems(k, "na")
    (ld_x, ld_ctxT, ld_ctx, q_mm, q_ev, qk_mm, qk_ev, kb_mm, kb_ev, s_mm, top, top2, bias, exped, turned,
     pt_v, pt_a, pv_mm, o_ev, f_mm, f_ev, rsum, xb_done) = (
        k.sem("a_" + x) for x in (
            "ld_x", "ld_ctxT", "ld_ctx", "q_mm", "q_ev", "qk_mm", "qk_ev", "kb_mm", "kb_ev", "s_mm", "top", "top2",
            "bias", "exp", "turned", "pt_v", "pt_a", "pv_mm", "o_ev", "f_mm", "f_ev", "rsum", "xb"))
    with ExitStack() as own:
        slots = Slots(k, own, "a_slots")
        r = Route(k, own, "ar")
        ctxN = k.sb(own, "ctxN", [P, NKT, D])
        qT = k.sb(own, "a_qT", [P, NC, S])
        qk = k.sb(own, "a_qk", [P, NC, S])
        kb = k.sb(own, "a_kb", [P, NT])
        mx = k.sb(own, "a_mx", [P, 3, NT])
        rs = k.sb(own, "a_rs", [P, 2, NT])
        prob = k.sb(own, "a_prob", [P, 2, SK])
        pT = k.sb(own, "a_pT", [P, NKT, P])
        oT = k.sb(own, "a_oT", [P, NC, P])
        xb = k.sb(own, "a_xb", [P, NT, D])
        ctxT = k.sb(own, "a_ctxT", [P, NC, SK])
        block = own.enter_context(nc.Block())

        @block.sync
        def _(sp):
            sp.dma_start(k.x[:, :, :], A["x"][bass.ds(b, 1)].rearrange("a (t p) d -> p (a t) d", p=P)).then_inc(ld_x, 16)
            r.keep(sp, b)
            sp.dma_start(ctxT[:, :, :], A["ctxT"][bass.ds(b, 1)].rearrange("a (c p) s -> p (a c) s", p=P)).then_inc(ld_ctxT, 16)
            sp.dma_start(ctxN[:, 0:NKT - 1, :], A["ctx"][bass.ds(b, 1), 0:P * (NKT - 1)].rearrange(
                "a (t p) d -> p (a t) d", p=P)).then_inc(ld_ctx, 16)
            sp.dma_start(ctxN[0:KW[-1], NKT - 1, :], A["ctx"][bass.ds(b, 1), P * (NKT - 1):SK].rearrange(
                "a p d -> p (a d)")).then_inc(ld_ctx, 16)
            for c in range(NC):
                sp.dma_start(k.vxB[:, c], A["B_vx"][c * P:(c + 1) * P].rearrange("p h n -> p h n")).then_inc(k.ld_vx, 16)
            for a in range(2):
                for h in range(0, HB, 4):
                    sp.dma_start(k.oxB[a * DB:(a + 1) * DB, h:h + 4], A["B_ox"][h:h + 4, :, a].rearrange(
                        "h j p n -> p h j n")).then_inc(k.ld_ox, 16)

        @block.gpsimd
        def _(g):
            norm_gpsimd(g, r.n)
            norm_gpsimd(g, n)
            g.wait_ge(ld_x, 16)
            g.tensor_tensor(xb[:, :, :], k.x[:, :, :], k.bvA[:, :].unsqueeze(1).to_broadcast([P, NT, D]),
                            ALU.add).then_inc(xb_done, 1)
            r.tokens(g)
            g.wait_ge(r.placed, 2)
            g.wait_ge(slots.step, find_slots(g, k, slots))

        @block.tensor
        def _(pe):
            norm_tensor(pe, k, n, k.xn)
            r.turn(pe)
            turned_wait(pe, n)
            for m in range(NC):
                for c in range(NC):
                    mm = pe.matmul(ps[:, 2 + m, :], k.wqA[:, c, m * P:(m + 1) * P], k.xT[:, c, :],
                                   start=c == 0, stop=c == NC - 1)
                mm.then_inc(q_mm, 1)
            r.logits(pe)
            pe.wait_ge(q_ev, NC)
            for m in range(NC):
                for c in range(NC):
                    mm = pe.matmul(ps[:, 4 + m, :], k.wkTA[:, c, m * P:(m + 1) * P], qT[:, c, :],
                                   start=c == 0, stop=c == NC - 1)
                mm.then_inc(qk_mm, 1)
            for t in range(NT):
                for c in range(NC):
                    mm = pe.matmul(ps[:, 6, t:t + 1], qT[:, c, t * P:(t + 1) * P], k.bkA[:, c:c + 1],
                                   start=c == 0, stop=c == NC - 1)
            mm.then_inc(kb_mm, 1)

            def scores(t):
                if t == 0:
                    pe.wait_ge(qk_ev, NC)
                    pe.wait_ge(ld_ctxT, 16)
                else:
                    pe.wait_ge(exped, t)
                for i in range(NKC):
                    for c in range(NC):
                        mm = pe.matmul(ps[:, i, 0:KC[i]], qk[:, c, t * P:(t + 1) * P],
                                       ctxT[:, c, i * BANK:i * BANK + KC[i]], start=c == 0, stop=c == NC - 1)
                mm.then_inc(s_mm, 1)

            def turn(t, g):
                if g == 0:
                    pe.wait_ge(exped, t + 1)
                if (t, g) == (0, 0):
                    pe.wait_ge(qk_ev, NC)
                if g % 2 == 0 and 2 * t + g // 2 > 0:
                    pe.wait_ge(pt_v, 2 * t + g // 2)
                if g % 2 == 1 and 2 * t + g // 2 > 0:
                    pe.wait_ge(pt_a, 2 * t + g // 2)
                for i in range(4 * g, min(4 * g + 4, NKT)):
                    mm = pe.transpose(ps[0:KW[i], 4 + g % 2, (i - 4 * g) * P:(i - 4 * g + 1) * P],
                                      prob[:, t % 2, i * P:i * P + KW[i]], k.ident[:, :])
                mm.then_inc(turned, 1)

            def context(t, g):
                pe.wait_ge((pt_v, pt_a)[g % 2], 2 * t + g // 2 + 1)
                if g == 0:
                    if t == 0:
                        pe.wait_ge(ld_ctx, 32)
                        pe.wait_ge(kb_ev, 1)
                    else:
                        pe.wait_ge(o_ev, t)
                for m in range(NC):
                    for i in range(4 * g, min(4 * g + 4, NKT)):
                        mm = pe.matmul(ps[:, 6, m * P:(m + 1) * P], ctxN[0:KW[i], i, m * P:(m + 1) * P],
                                       pT[0:KW[i], i, :], start=i == 0 and m == 0, stop=i == NKT - 1 and m == NC - 1,
                                       skip_group_check=True)
                if g == NKC - 1:
                    mm.then_inc(pv_mm, 1)

            def project(t):
                pe.wait_ge(o_ev, t + 1)
                if t == 0:
                    pe.wait_ge(r.carried, 1)
                if t >= 1:
                    pe.wait_ge(f_ev, t)
                for c in range(NC):
                    mm = pe.matmul(ps[:, 7, 0:D], oT[:, c, :], k.wvA[:, c, :], start=c == 0, stop=c == NC - 1)
                mm.then_inc(f_mm, 1)

            for i in range(NT + 2):
                if 1 <= i <= NT:
                    turn(i - 1, 0)
                    turn(i - 1, 1)
                if i < NT:
                    scores(i)
                if i == 0:
                    r.counts(pe)
                if i >= 2:
                    project(i - 2)
                if 1 <= i <= NT:
                    turn(i - 1, 2)
                    context(i - 1, 0)
                    context(i - 1, 1)
                    turn(i - 1, 3)
                    context(i - 1, 2)
                    context(i - 1, 3)

        @block.scalar
        def _(act):
            turned_scalar(act, k, n, k.xT)
            turned_scalar(act, k, r.n, r.xT, bank=6)
            for m in range(NC):
                act.wait_ge(q_mm, m + 1)
                nc.scalar.activation(qT[:, m, :], ps[:, 2 + m, :], ACT.Identity,
                                     bias=k.bqA[:, m:m + 1]).then_inc(q_ev, 1)
            r.exponentials(act)
            def turned_probabilities(t, g):
                act.wait_ge(turned, NKC * t + g + 1)
                w = min(4, NKT - 4 * g)
                rows = P if w == 4 else KW[-1]
                nc.scalar.copy(pT[0:rows, 4 * g:4 * g + w, :],
                               ps[0:rows, 4 + g % 2, 0:w * P].rearrange("p (a n) -> p a n", n=P)).then_inc(pt_a, 1)

            for i in range(NT + 1):
                if i >= 1:
                    turned_probabilities(i - 1, 1)
                if i < NT:
                    act.wait_ge(bias, i + 1)
                    if i >= 2:
                        act.wait_ge(turned, NKC * (i - 1))
                    nc.scalar.activation(prob[:, i % 2, :], ps[:, 0:4, :].rearrange("p a n -> p (a n)")[:, 0:SK],
                                         ACT.Exp, bias=mx[:, 2, i:i + 1], scale=SCALE_A,
                                         accum_out=rs[:, 0, i:i + 1]).then_inc(exped, 1)
                if i >= 1:
                    turned_probabilities(i - 1, 3)
                    act.wait_ge(pv_mm, i)
                    nc.scalar.copy(oT[:, :, :].rearrange("p c n -> p (c n)"), ps[:, 6, 0:D]).then_inc(o_ev, 1)

        @block.vector
        def _(v):
            statistics(v, r.n, r.x)
            v.wait_ge(ld_x, 16)
            norm_vector(v, n, k.x, k.xn)
            r.normalise(v)
            turned_vector(v, k, n, k.xT)
            turned_vector(v, k, r.n, r.xT, bank=6)
            r.shift(v)
            for m in range(NC):
                v.wait_ge(qk_mm, m + 1)
                v.tensor_copy(qk[:, m, :], ps[:, 4 + m, :]).then_inc(qk_ev, 1)
            v.wait_ge(kb_mm, 1)
            v.tensor_copy(kb[:, :], ps[:, 6, 0:NT]).then_inc(kb_ev, 1)
            v.wait_ge(kb_ev, 1)
            r.choose(v)

            def finish(t):
                v.wait_ge(exped, t + 1)
                v.reciprocal(rs[:, 1, t:t + 1], rs[:, 0, t:t + 1]).then_inc(rsum, 1)
                v.wait_ge(rsum, t + 1)
                v.wait_ge(f_mm, t + 1)
                v.wait_ge(xb_done, 1)
                v.scalar_tensor_tensor(out=k.x[:, t, :], in0=ps[:, 7, 0:D], scalar=rs[:, 1, t:t + 1],
                                       in1=xb[:, t, :], op0=ALU.mult, op1=ALU.add).then_inc(f_ev, 1)

            def turned_probabilities(t, g):
                v.wait_ge(turned, NKC * t + g + 1)
                v.tensor_copy(pT[:, 4 * g:4 * g + 4, :],
                              ps[:, 4 + g % 2, :].rearrange("p (a n) -> p a n", n=P)).then_inc(pt_v, 1)

            for i in range(NT + 2):
                if 1 <= i <= NT:
                    turned_probabilities(i - 1, 0)
                if i < NT:
                    v.wait_ge(s_mm, i + 1)
                    v.tensor_reduce(mx[:, 0, i:i + 1], ps[:, 0:4, :].rearrange("p a n -> p (a n)")[:, 0:SK],
                                    AX_X, ALU.max).then_inc(top, 1)
                    v.wait_ge(top, i + 1)
                    v.tensor_tensor(mx[:, 1, i:i + 1], mx[:, 0, i:i + 1], kb[:, i:i + 1], ALU.add).then_inc(top2, 1)
                    v.wait_ge(top2, i + 1)
                    v.tensor_scalar(mx[:, 2, i:i + 1], mx[:, 1, i:i + 1], kb[:, i:i + 1], -SCALE_A, ALU.subtract,
                                    ALU.mult).then_inc(bias, 1)
                if i == 0:
                    r.places(v)
                if 1 <= i <= NT:
                    turned_probabilities(i - 1, 2)
                if i >= 2:
                    finish(i - 2)


def attention_b(k, A, b):
    nc, ps = k.nc, k.ps
    n = NormSems(k, "nb")
    (qk_mm, q_ev, k_ev, g_mm, g_exp, g_one, g_sig, g_top, g_eq, g_key, g_first, g_pick, g_gm, val_mm, val_mul,
     val_sum, val_two, s_mm, top, exped, rinv, gp_done, turned, g_turned, ev_a, ev_v, pv_mm, o_ev, sel_mm, out_mm, x_done, zero_q, split) = (
        k.sem("b_" + x) for x in (
            "qk_mm", "q_ev", "k_ev", "g_mm", "g_exp", "g_one", "g_sig", "g_top", "g_eq", "g_key", "g_first",
            "g_pick", "g_gm", "val_mm", "val_mul", "val_sum", "val_two", "s_mm", "top", "exp", "rinv", "gp", "turned",
            "g_turned", "ev_a", "ev_v", "pv_mm", "o_ev", "sel_mm", "out_mm", "x_done", "zero_q", "split"))
    EARLY = HB * NT - 6
    SC = [(1, 384), (2, 0), (1, 0), (0, 0)]
    ORDER = [3, 1, 0, 2]
    DONE = [1, 2, 4, 4]
    OFF = [0, 512, 896, 1152]
    POFF = [0, P, 3 * P, 6 * P]
    with ExitStack() as own:
        qz = k.sb(own, "b_qz", [P, HB, S])
        kT = k.sb(own, "b_kT", [P, HB // 2, S])
        gate = k.sb(own, "b_gate", [P, 3, NT * HB * EB])
        gtop = k.sb(own, "b_gtop", [P, 2, NT * HB])
        gm = k.sb(own, "b_gm", [P, NT, HB, EB])
        tmp = k.sb(own, "b_tmp", [P, 2, EB * DB])
        val = k.sb(own, "b_val", [P, NT, HB, 2, DB])
        mx = k.sb(own, "b_mx", [P, HB, NT])
        rs = k.sb(own, "b_rs", [P, HB, NT])
        ri = k.sb(own, "b_ri", [P, HB, NT])
        prob = k.sb(own, "b_prob", [P, 2, 10 * P])
        pT = k.sb(own, "b_pT", [P, 10 * P])
        oT = k.sb(own, "b_oT", [P, S])
        gr = k.sb(own, "b_gr", [P, 2, NT, EB])
        gT = k.sb(own, "b_gT", [P, S], BF16)
        og = k.sb(own, "b_og", [P, 2, NJ, S])
        gp = k.gp
        block = own.enter_context(nc.Block())

        @block.gpsimd
        def _(g):
            norm_gpsimd(g, n)
            g.memset(qz[:, :, :], 0.0).then_inc(zero_q, 1)
            scatter_rows(g, k, range(KD), k.scattered)
            for u in range(HB * NT):
                h, t = u // NT, u % NT
                g.wait_ge(val_sum, u + 1)
                g.tensor_copy(val[:, t, h, 1, :], val[:, t, h, 0, :]).then_inc(val_two, 1)

        @block.tensor
        def _(pe):
            norm_tensor(pe, k, n, k.xn)
            turned_wait(pe, n)
            for t in range(NT):
                for c in range(NC):
                    mm = pe.matmul(ps[:, 6, t * HB * EB:(t + 1) * HB * EB], k.xT[:, c, t * P:(t + 1) * P],
                                   k.wgB[:, c, :], start=c == 0, stop=c == NC - 1)
            mm.then_inc(g_mm, 1)
            for m in range(HB // 2):
                for i, w in enumerate((k.wqB, k.wkB)):
                    if m >= 2:
                        pe.wait_ge((q_ev, k_ev)[i], (2 * (m - 1), m - 1)[i])
                    for c in range(NC):
                        mm = pe.matmul(ps[:, 2 + 2 * i + m % 2, :], w[:, c, m * P:(m + 1) * P], k.xT[:, c, :],
                                       start=c == 0, stop=c == NC - 1)
                    mm.then_inc(qk_mm, 1)
            def scores(h):
                if h == 0:
                    pe.wait_ge(q_ev, HB)
                    pe.wait_ge(k_ev, HB // 2)
                for o, t in enumerate(ORDER):
                    if h >= 1:
                        pe.wait_ge(exped, NT * (h - 1) + DONE[o])
                    bank, off = SC[t]
                    pe.matmul(ps[:, bank, off:off + (t + 1) * P], qz[:, h, t * P:(t + 1) * P],
                              kT[:, h // 2, 0:(t + 1) * P], start=True, stop=False)
                    mm = pe.matmul(ps[:, bank, off + t * P:off + (t + 1) * P], k.identb[:, :], k.causal[:, :],
                                   start=False, stop=True)
                    mm.then_inc(s_mm, 1)

            def turn(h):
                pe.wait_ge(exped, NT * (h + 1))
                for g, blocks in enumerate(([(t, 0) for t in range(4)], [(t, 1) for t in range(1, 4)],
                                            [(2, 2), (3, 2), (3, 3)])):
                    if g < 2 and h >= 1:
                        pe.wait_ge(ev_v, 6 * (h - 1) + 5 + g)
                    if g == 2:
                        pe.wait_ge(ev_a, 2 * h + 1)
                    for a, (t, i) in enumerate(blocks):
                        mm = pe.transpose(ps[:, 3 + g % 2, a * P:(a + 1) * P],
                                          prob[:, h % 2, POFF[t] + i * P:POFF[t] + (i + 1) * P], k.ident[:, :])
                    mm.then_inc(turned, 1)
                    if g == 1:
                        out(h - 1, 0)

            def gates(h):
                pe.wait_ge(gp_done, h + 1)
                pe.wait_ge(ev_v, 6 * h + 1)
                for t in range(NT):
                    mm = pe.transpose(ps[:, 4, 0:BANK // 2].bitcast(BF16)[:, t * P:(t + 1) * P], gp[:, t, :],
                                      k.identb[:, :])
                mm.then_inc(g_turned, 1)
                out(h - 1, 2)
                for j in range(NJ):
                    if j == 2:
                        out(h - 1, 3)
                    if j == 0:
                        pe.wait_ge(ev_a, 2 * h + 2)
                    pe.wait_ge(ev_v, 6 * h + (2, 2, 3, 4)[j])
                    pe.matmul(ps[:, 3 + j % 2, :], k.sel[:, j, :], gT[:, :], start=True, stop=True).then_inc(sel_mm, 1)

            def values(h):
                pe.wait_ge(ev_a, 2 * h + 2)
                pe.wait_ge(ev_v, 6 * h + 1)
                pe.wait_ge(val_two, NT * (h + 1))
                if h >= 1:
                    pe.wait_ge(o_ev, h)
                for i in range(NT):
                    mm = pe.matmul(ps[:, 5, i * P:S],
                                   val[:, i, h, :, :].rearrange("p a d -> p (a d)"),
                                   pT[:, OFF[i]:OFF[i] + S - i * P], start=i == 0, stop=i == NT - 1)
                mm.then_inc(pv_mm, 1)

            def out(h, j):
                if h < 0:
                    return
                pe.wait_ge(ev_v, 6 * h + 3 + j)
                for t in range(NT):
                    first = (h, j) == (0, 0)
                    mm = pe.matmul(ps[:, 6 + t // 2, (t % 2) * D:(t % 2 + 1) * D], og[:, h % 2, j, t * P:(t + 1) * P],
                                   k.oxB[:, h, j, :], start=first and t % 2 == 0,
                                   stop=(h, j) == (HB - 1, NJ - 1) and t % 2 == 1, skip_group_check=True)
                if j == NJ - 1:
                    mm.then_inc(out_mm, 1)

            pe.wait_ge(k.ld_vx, 16 * NC)
            pe.wait_ge(g_exp, 1)
            for u in range(HB * NT):
                h, t = u // NT, u % NT
                if u == EARLY:
                    scores(0)
                if u >= 2:
                    pe.wait_ge(val_mul, u - 1)
                for c in range(NC):
                    mm = pe.matmul(ps[:, 6 + u % 2, :], k.xT[:, c, t * P:(t + 1) * P], k.vxB[:, c, h, :],
                                   start=c == 0, stop=c == NC - 1)
                mm.then_inc(val_mm, 1)

            pe.wait_ge(val_mul, HB * NT)
            pe.wait_ge(k.ld_ox, 16 * 4)
            for h in range(HB):
                turn(h)
                if h + 1 < HB:
                    scores(h + 1)
                out(h - 1, 1)
                values(h)
                gates(h)
            for j in range(NJ):
                out(HB - 1, j)

        @block.scalar
        def _(act):
            turned_scalar(act, k, n, k.xT)
            act.wait_ge(g_mm, 1)
            nc.scalar.activation(gate[:, 0, :], ps[:, 6, 0:NT * HB * EB], ACT.Exp, scale=-1.0).then_inc(g_exp, 1)
            act.wait_ge(zero_q, 1)
            for m in range(HB // 2):
                act.wait_ge(qk_mm, 2 * m + 1)
                for a in range(2):
                    nc.scalar.mul(qz[DB * a:DB * a + DB, 2 * m + a, :], ps[DB * a:DB * a + DB, 2 + m % 2, :],
                                  SCALE_B).then_inc(q_ev, 1)

            def probabilities(h):
                for o, t in enumerate(ORDER):
                    act.wait_ge(top, NT * h + DONE[o])
                    if h >= 2 and o == 0:
                        act.wait_ge(turned, 3 * (h - 1))
                    bank, off = SC[t]
                    nc.scalar.activation(prob[:, h % 2, POFF[t]:POFF[t] + (t + 1) * P],
                                         ps[:, bank, off:off + (t + 1) * P], ACT.Exp, bias=mx[:, h, t:t + 1],
                                         accum_out=rs[:, h, t:t + 1]).then_inc(exped, 1)

            def read_turned(h):
                for g in (0, 2):
                    act.wait_ge(turned, 3 * h + g + 1)
                    w = (4, 3, 3)[g] * P
                    nc.scalar.copy(pT[:, OFF[g]:OFF[g] + w], ps[:, 3 + g % 2, 0:w]).then_inc(ev_a, 1)

            probabilities(0)
            for h in range(HB):
                read_turned(h)
                if h + 1 < HB:
                    probabilities(h + 1)
                act.wait_ge(pv_mm, h + 1)
                if h >= 1:
                    act.wait_ge(ev_v, 6 * h)
                nc.scalar.copy(oT[:, :], ps[:, 5, :]).then_inc(o_ev, 1)

        @block.vector
        def _(v):
            norm_vector(v, n, k.x, k.xn)
            turned_vector(v, k, n, k.xT)
            v.wait_ge(g_exp, 1)
            v.tensor_scalar(gate[:, 1, :], gate[:, 0, :], 1.0, None, ALU.add).then_inc(g_one, 1)
            v.wait_ge(g_one, 1)
            v.reciprocal(gate[:, 2, :], gate[:, 1, :]).then_inc(g_sig, 1)
            v.wait_ge(g_sig, 1)
            g8 = [gate[:, i, :].rearrange("p (a e) -> p a e", e=EB) for i in range(3)]
            wide = [P, NT * HB, EB]
            v.tensor_reduce(gtop[:, 0, :], g8[2], AX_X, ALU.max).then_inc(g_top, 1)
            v.wait_ge(g_top, 1)
            v.tensor_tensor(g8[0], g8[2], gtop[:, 0, :].unsqueeze(2).to_broadcast(wide), ALU.is_equal).then_inc(g_eq, 1)
            v.wait_ge(g_eq, 1)
            v.tensor_tensor(g8[1], g8[0], k.desc[:, :].unsqueeze(1).to_broadcast(wide), ALU.mult).then_inc(g_key, 1)
            v.wait_ge(g_key, 1)
            v.tensor_reduce(gtop[:, 1, :], g8[1], AX_X, ALU.max).then_inc(g_first, 1)
            v.wait_ge(g_first, 1)
            v.tensor_tensor(g8[0], g8[1], gtop[:, 1, :].unsqueeze(2).to_broadcast(wide), ALU.is_equal).then_inc(g_pick, 1)
            v.wait_ge(g_pick, 1)
            gma = gm[:, :, :, :].rearrange("p t h e -> p (t h) e")
            v.tensor_tensor(gma, g8[0], g8[2], ALU.mult).then_inc(g_gm, 1)
            v.wait_ge(g_gm, 1)
            for m in range(HB // 2):
                v.wait_ge(qk_mm, 2 * m + 2)
                v.tensor_copy(kT[:, m, :], ps[:, 4 + m % 2, :]).then_inc(k_ev, 1)
            def maxima(h):
                for o, t in enumerate(ORDER):
                    v.wait_ge(s_mm, NT * h + DONE[o])
                    bank, off = SC[t]
                    v.tensor_reduce(mx[:, h, t:t + 1], ps[:, bank, off:off + (t + 1) * P], AX_X, ALU.max,
                                    negate=True).then_inc(top, 1)

            def split_gates(h):
                gs = split
                v.wait_ge(exped, NT * (h + 1))
                v.reciprocal(ri[:, h, :], rs[:, h, :]).then_inc(rinv, 1)
                v.wait_ge(rinv, h + 1)
                v.tensor_tensor(gr[:, 0, :, :], gm[:, :, h, :], ri[:, h, :].unsqueeze(2).to_broadcast([P, NT, EB]),
                                ALU.mult).then_inc(gs, 1)
                if h >= 1:
                    v.wait_ge(g_turned, h)
                v.wait_ge(gs, 4 * h + 1)
                v.tensor_copy(gp[:, :, 0:EB], gr[:, 0, :, :]).then_inc(gs, 1)
                v.wait_ge(gs, 4 * h + 2)
                v.tensor_tensor(gr[:, 1, :, :], gr[:, 0, :, :], gp[:, :, 0:EB], ALU.subtract).then_inc(gs, 1)
                v.wait_ge(gs, 4 * h + 3)
                v.tensor_copy(gp[:, :, EB:2 * EB], gr[:, 1, :, :]).then_inc(gs, 1)
                v.wait_ge(gs, 4 * h + 4)
                v.tensor_tensor(gp[:, :, 2 * EB:3 * EB], gr[:, 1, :, :], gp[:, :, EB:2 * EB],
                                ALU.subtract).then_inc(gp_done, 1)

            for u in range(HB * NT):
                h, t = u // NT, u % NT
                if u == EARLY + 2:
                    maxima(0)
                v.wait_ge(val_mm, u + 1)
                if u >= 2:
                    v.wait_ge(val_sum, u - 1)
                v.tensor_tensor(tmp[:, u % 2, :].rearrange("p (e d) -> p e d", e=EB),
                                ps[:, 6 + u % 2, :].rearrange("p (e d) -> p e d", e=EB),
                                gm[:, t, h, :].unsqueeze(2).to_broadcast([P, EB, DB]), ALU.mult).then_inc(val_mul, 1)
                v.wait_ge(val_mul, u + 1)
                v.tensor_reduce(val[:, t, h, 0, :], tmp[:, u % 2, :].rearrange("p (e d) -> p d e", e=EB), AX_X,
                                ALU.add).then_inc(val_sum, 1)

            for h in range(HB):
                v.wait_ge(turned, 3 * h + 2)
                v.tensor_copy(pT[:, OFF[1]:OFF[1] + 3 * P], ps[:, 4, 0:3 * P]).then_inc(ev_v, 1)
                split_gates(h)
                if h + 1 < HB:
                    maxima(h + 1)
                v.wait_ge(g_turned, h + 1)
                v.tensor_copy(gT[:, :], ps[:, 4, 0:BANK // 2].bitcast(BF16)).then_inc(ev_v, 1)
                v.wait_ge(o_ev, h + 1)
                if h >= 2:
                    v.wait_ge(out_mm, h - 1)
                for j in range(NJ):
                    v.wait_ge(sel_mm, NJ * h + j + 1)
                    v.tensor_tensor(og[:, h % 2, j, :], oT[:, :], ps[:, 3 + j % 2, :], ALU.mult).then_inc(ev_v, 1)
            v.wait_ge(out_mm, HB)
            for t in range(NT):
                v.tensor_tensor(k.x[:, t, :], k.x[:, t, :], ps[:, 6 + t // 2, (t % 2) * D:(t % 2 + 1) * D],
                                ALU.add).then_inc(x_done, 1)


def split3(v, sem, at, f, parts, rest):
    v.tensor_copy(parts[0], f).then_inc(sem, 1)
    v.wait_ge(sem, at + 1)
    v.tensor_tensor(rest, f, parts[0], ALU.subtract).then_inc(sem, 1)
    v.wait_ge(sem, at + 2)
    v.tensor_copy(parts[1], rest).then_inc(sem, 1)
    v.wait_ge(sem, at + 3)
    v.tensor_tensor(parts[2], rest, parts[1], ALU.subtract).then_inc(sem, 1)
    return at + 4


def context_c(k, A):
    nc, ps = k.nc, k.ps
    ld_ctxT = [k.sem(f"x_ld_ctxT{i}") for i in range(2)]
    stored = [k.sem(f"x_stored{i}") for i in range(2)]
    NST = NG + 2
    (k_mm, k_ev, v_mm, v_ev, v_full, v_tail, split_k) = (
        k.sem("x_" + x) for x in ("k_mm", "k_ev", "v_mm", "v_ev", "v_full", "v_tail", "split_k"))
    with ExitStack() as own:
        kf = k.sb(own, "x_kf", [P, NC, SK])
        k3 = k.sb(own, "x_k3", [P, 2, 3, NC, SK], BF16)
        rest = k.sb(own, "x_rest", [P, 2, SK])
        vf = k.sb(own, "x_vf", [P, 2, NKT, D])
        ctxT = k.sb(own, "x_ctxT", [P, 2, NC, SK])
        block = own.enter_context(nc.Block())

        @block.sync
        def _(sp):
            def load(r):
                if r >= 2:
                    sp.wait_ge(v_mm, NKT * (r - 1))
                sp.dma_start(ctxT[:, r % 2], A["ctxT"][r].rearrange("(c p) s -> p c s", p=P)).then_inc(ld_ctxT[r % 2], 16)

            load(0)
            load(1)
            for r in range(NB):
                for m in range(NC):
                    sp.wait_ge(split_k, 4 * (NC * r + m + 1))
                    for a in range(2):
                        sp.dma_start(k.k_parts[r, 2 * m + a].rearrange("i p s -> p i s"),
                                     k3[a * GH * DC:(a + 1) * GH * DC, r % 2, :, m, :]).then_inc(stored[r % 2], 16)
                if r + 2 < NB:
                    load(r + 2)
                sp.wait_ge(v_full, r + 1)
                sp.dma_start(k.v_all[r, :, 0:NKT - 1], vf[:, r % 2, 0:NKT - 1]).then_inc(stored[r % 2], 16)
                sp.wait_ge(v_tail, r + 1)
                sp.dma_start(k.v_all[r, 0:KW[-1], NKT - 1], vf[0:KW[-1], r % 2, NKT - 1]).then_inc(stored[r % 2], 16)
            for i in range(2):
                sp.wait_ge(stored[i], 16 * NST * NB // 2)
            sp.wait_ge(k.loaded, 16 * k.late_weights)

        @block.gpsimd
        def _(g):
            g.wait_ge(ld_ctxT[1], 16)
            parts = k.table.rearrange("(i p t) d -> i p (t d)", i=ZFILL, p=P)
            for r in range(NB):
                for i in range(ZFILL // NB):
                    g.dma_start(parts[ZFILL // NB * r + i], k.xr[:, :, :].rearrange("p t d -> p (t d)")).then_inc(k.scattered, 16)
                g.wait_ge(v_ev, NKT * (r + 1))
                full = vf[:, r % 2, 0:NKT - 1, :]
                g.tensor_tensor(full, full, k.bvC[:, :].unsqueeze(1).to_broadcast([P, NKT - 1, D]), ALU.add).then_inc(v_full, 1)
                g.wait_ge(v_full, r + 1)
                tail = vf[0:KW[-1], r % 2, NKT - 1, :]
                g.tensor_tensor(tail, tail, k.bvC[0:KW[-1], :], ALU.add).then_inc(v_tail, 1)
                g.wait_ge(v_tail, r + 1)

        @block.tensor
        def _(pe):
            for r in range(NB):
                pe.wait_ge(ld_ctxT[r % 2], 16 * (r // 2 + 1))
                for m in range(NC):
                    for i in range(NKC):
                        if r + m:
                            pe.wait_ge(k_ev, NKC * (NC * r + m - 1) + i + 1)
                        for c in range(NC):
                            mm = pe.matmul(ps[:, i, 0:KC[i]], k.wkC[:, c, m * P:(m + 1) * P],
                                           ctxT[:, r % 2, c, i * BANK:i * BANK + KC[i]], start=c == 0, stop=c == NC - 1)
                        mm.then_inc(k_mm, 1)
                for i in range(NKT):
                    n = NKT * r + i
                    if n >= 4:
                        pe.wait_ge(v_ev, n - 3)
                    for c in range(NC):
                        mm = pe.matmul(ps[0:KW[i], 4 + n % 4, 0:D], ctxT[:, r % 2, c, i * P:i * P + KW[i]], k.wvC[:, c, :],
                                       start=c == 0, stop=c == NC - 1)
                    mm.then_inc(v_mm, 1)

        @block.scalar
        def _(act):
            for r in range(NB):
                for m in range(NC):
                    if r:
                        act.wait_ge(split_k, 4 * (NC * (r - 1) + m + 1) - 2)
                    for i in range(NKC):
                        act.wait_ge(k_mm, NKC * (NC * r + m) + i + 1)
                        nc.scalar.activation(kf[:, m, i * BANK:i * BANK + KC[i]], ps[:, i, 0:KC[i]], ACT.Identity,
                                             bias=k.bkC[:, m:m + 1]).then_inc(k_ev, 1)
                if r >= 2:
                    act.wait_ge(stored[r % 2], 16 * NST * (r // 2))
                for i in range(NKT):
                    n = NKT * r + i
                    act.wait_ge(v_mm, n + 1)
                    nc.scalar.copy(vf[0:KW[i], r % 2, i, :], ps[0:KW[i], 4 + n % 4, 0:D]).then_inc(v_ev, 1)

        @block.vector
        def _(v):
            at = 0
            for r in range(NB):
                if r >= 2:
                    v.wait_ge(stored[r % 2], 16 * NST * (r // 2))
                for m in range(NC):
                    v.wait_ge(k_ev, NKC * (NC * r + m + 1))
                    if at >= 8:
                        v.wait_ge(split_k, at - 4)
                    at = split3(v, split_k, at, kf[:, m, :], [k3[:, r % 2, i, m, :] for i in range(3)], rest[:, m % 2, :])


def attention_c(k, A, b):
    nc, ps = k.nc, k.ps
    n = NormSems(k, "nc")
    ld_maskN = [k.sem(f"c_ld_maskN{i}") for i in range(2)]
    ld_maskT = [k.sem(f"c_ld_maskT{i}") for i in range(2)]
    stored = [k.sem(f"c_stored{i}") for i in range(NC)]
    (ld_v, v_ev, q_mm, q_ev, split_q, biasN, biasT, tail) = (
        k.sem("c_" + x) for x in ("ld_v", "v_ev", "q_mm", "q_ev", "split_q", "biasN", "biasT", "tail"))
    ld_k = [k.sem(f"d_ld_k{i}") for i in range(NS)]
    ld_q = [k.sem(f"d_ld_q{i}") for i in range(NS)]
    (ld_m, mx_mm, mx_v, neg, split_m, m_turned, m_row, s_mm, exped, pv_mm, acc_ev, acc_turned, o_rec,
     o_nat, o_turned, oT_a, oT_v, f_mm, f_ev, xb_done, ones) = (
        k.sem("d_" + x) for x in (
            "ld_m", "mx_mm", "mx_v", "neg", "split_m", "m_turned", "m_row", "s_mm", "exp", "pv_mm",
            "acc_ev", "acc_turned", "o_rec", "o_nat", "o_turned", "oT_a", "oT_v", "f_mm", "f_ev", "xb", "ones"))
    NU = NT * GH * NKC

    def banks(g):
        return (5, 6, 0, 1) if g == 0 else (5, 6)

    with ExitStack() as own:
        kS = k.sb(own, "kS", [P, NS, GH, SK + SK % 2], BF16)
        qS = k.sb(own, "qS", [P, NS, GH, S], BF16)
        mp = k.sb(own, "d_mp", [P, NT, GH, NKC])
        m1 = k.sb(own, "d_m1", [P, 2, NT * GH])
        m3 = k.sb(own, "d_m3", [P, NT, 3, GH], BF16)
        mrow = k.sb(own, "d_mrow", [3 * GH, S], BF16)
        prob = k.sb(own, "d_prob", [P, 2, GH, S])
        acc = k.sb(own, "d_acc", [P, S])
        rec = k.sb(own, "d_rec", [P, NT, GH])
        oN = k.sb(own, "d_oN", [P, NT, D])
        oT = k.sb(own, "d_oT", [P, NC, S])
        xb = k.sb(own, "d_xb", [P, NT, D])
        maskN = k.sb(own, "maskN", [P, NT, SK], BF16)
        maskT = k.sb(own, "maskT", [P, NKT, S], BF16)
        vaug = k.sb(own, "vaug", [P, NKT, HC, VW])
        q3 = k.sb(own, "c_q3", [P, 3, NC, S], BF16)
        rawN = k.sb(own, "c_rawN", [P, 2, SK], I32)
        rawT = k.sb(own, "c_rawT", [P, 2, 2, S], I32)
        qf, rest = oT, oN[:, :, :].rearrange("p t d -> p (t d)").rearrange("p (c s) -> p c s", c=NC)
        vf = prob[:, :, :, :].rearrange("p a h s -> p (a h s)")[:, 0:NKT * D].rearrange("p (t d) -> p t d", d=D)
        block = own.enter_context(nc.Block())
        pairs = [(i, min(2, NKT - i)) for i in range(0, NKT, 2)]

        def load_q(eng, g):
            r = 0
            for w in (3, 2, 1):
                eng.dma_start(qS[r * DC:(r + w) * DC, g % NS, :, :], k.q_parts[g, 0:w].rearrange(
                    "j (d h) s -> (j d) h s", h=GH)).then_inc(ld_q[g % NS], 16)
                r += w

        @block.sync
        def _(sp):
            def load_k(g):
                r = 0
                for i, w in ((0, 3), (1, 2), (2, 1)):
                    for j in range(w):
                        sp.dma_start(kS[(r + j) * DC:(r + j + 1) * DC, g % NS, :, 0:SK], k.k_parts[bass.ds(b, 1), g, i].rearrange(
                            "a (d h) s -> d (a h) s", h=GH)).then_inc(ld_k[g % NS], 16)
                    r += w

            def load_maskN(t):
                sp.dma_start(rawN[:, t % 2, :], A["mask"][bass.ds(b, 1), t * P:(t + 1) * P].rearrange(
                    "a p s -> p (a s)")).then_inc(ld_maskN[t % 2], 16)

            load_maskN(0)
            load_k(0)
            sp.wait_ge(ld_q[0], 48)
            load_maskN(1)
            sp.wait_ge(biasN, 1)
            load_maskN(2)
            sp.dma_start(vf[:, 0:NKT - 1, :], k.v_all[bass.ds(b, 1), :, 0:NKT - 1, :].rearrange("a p t d -> p (a t) d")).then_inc(ld_v, 16)
            sp.dma_start(vf[0:KW[-1], NKT - 1, :], k.v_all[bass.ds(b, 1), 0:KW[-1], NKT - 1, :].rearrange("a p d -> p (a d)")).then_inc(ld_v, 16)
            for j, (i, w) in enumerate(pairs):
                if j == 2:
                    sp.wait_ge(biasN, 2)
                    load_maskN(3)
                if j == 3:
                    load_k(1)
                    load_q(sp, 1)
                if j >= 2:
                    sp.wait_ge(biasT, j - 1)
                rows = KW[i + w - 1]
                sp.dma_start(rawT[0:rows, j % 2, 0:w, :], A["maskT"][bass.ds(b, 1), i * P:i * P + (w - 1) * P + rows].rearrange(
                    "a (w p) s -> p (a w) s", w=w)).then_inc(ld_maskT[j % 2], 16)
            for g in range(NG):
                sp.wait_ge(m_row, g + 1)
                for i in range(3):
                    sp.dma_start(qS[KROWS + i:KROWS + i + 1, g % NS, :, :],
                                 mrow[i * GH:(i + 1) * GH, :]).then_inc(ld_m, 16)
                if g == 0:
                    sp.wait_ge(stored[1], 32)
                    load_k(2)
                    load_q(sp, 2)
                elif g + NS - 1 < NG:
                    sp.wait_ge(s_mm, 2 * NKT * g)
                    load_k(g + NS - 1)
                    load_q(sp, g + NS - 1)

        @block.gpsimd
        def _(g):
            norm_gpsimd(g, n)
            for i in range(NS):
                g.memset(kS[KROWS:KROWS + 3, i, :, :].rearrange("p h s -> p (h s)").bitcast(F32), TWO_ONES).then_inc(ones, 1)
            g.wait_ge(ones, NS)
            g.tensor_tensor(xb[:, :, :], k.x[:, :, :], k.boC[:, :].unsqueeze(1).to_broadcast([P, NT, D]),
                            ALU.add).then_inc(xb_done, 1)
            g.memset(vaug[:, :, :, DC:DC + 1], 1.0).then_inc(tail, 1)
            g.memset(vaug[:, :, :, DC + 1:VW], 0.0).then_inc(tail, 1)
            for j, (i, w) in enumerate(pairs):
                g.wait_ge(ld_maskT[j % 2], 16 * (j // 2 + 1))
                g.tensor_scalar(maskT[0:KW[i], i:i + w, :], rawT[0:KW[i], j % 2, 0:w, :], 0.0, MASKED, ALU.is_equal,
                                ALU.mult).then_inc(biasT, 1)

        @block.tensor
        def _(pe):
            def maxima(g, u):
                t, h, i = u // (GH * NKC), u // NKC % GH, u % NKC
                n = NU * g + u
                if u == 0:
                    pe.wait_ge(ld_q[g % NS], 16 * 3 * (g // NS + 1))
                    pe.wait_ge(ld_k[g % NS], 16 * len(TERMS) * (g // NS + 1))
                if n >= len(banks(g)):
                    pe.wait_ge(mx_v, n - len(banks(g)) + 1)
                pe.matmul(ps[:, banks(g)[n % len(banks(g))], 0:MC[i]], qS[0:KROWS, g % NS, h, t * P:(t + 1) * P],
                          kS[0:KROWS, g % NS, h, MO[i]:MO[i] + MC[i]], start=True, stop=True).then_inc(mx_mm, 1)

            def turn_maxima(g):
                pe.wait_ge(split_m, 4 * (g + 1))
                if g >= 2:
                    pe.wait_ge(o_nat, g - 1)
                for t in range(NT):
                    mm = pe.transpose(ps[0:3 * GH, 7, 0:BANK // 2].bitcast(BF16)[:, t * P:(t + 1) * P],
                                      m3[:, t, :, :].rearrange("p a h -> p (a h)"), k.identb[:, :])
                mm.then_inc(m_turned, 1)

            def scores(g, i, a, between):
                w = KW[i]
                if g == 0 and a == 0 and i % 2 == 0:
                    pe.wait_ge(biasT, i // 2 + 1)
                if i == 0 and a == 0:
                    pe.wait_ge(ld_m, 48 * (g + 1))
                    pe.wait_ge(ones, min(g + 1, NS))
                if g + i >= 1:
                    pe.wait_ge(exped, 2 * (NKT * g + i) - 1 + a)
                for j in range(2):
                    h = 2 * a + j
                    pe.matmul(ps[0:w, h, :], k.identb[0:w, 0:w], maskT[0:w, i, :], start=True, stop=False)
                    mm = pe.matmul(ps[0:w, h, :], kS[0:KROWS + 3, g % NS, h, i * P:i * P + w],
                                   qS[0:KROWS + 3, g % NS, h, :], start=False, stop=True)
                    if j:
                        mm.then_inc(s_mm, 1)
                    between()

            def values(g, i, between):
                w = KW[i]
                pe.wait_ge(exped, 2 * (NKT * g + i) + 2)
                if g == 0 and i == 0:
                    pe.wait_ge(tail, 2)
                    pe.wait_ge(v_ev, 2)
                if g >= 1 and i == 0:
                    pe.wait_ge(acc_ev, g)
                for h in range(GH):
                    mm = pe.matmul(ps[VW * h:VW * (h + 1), 4, :], vaug[0:w, i, GH * g + h, :],
                                   prob[0:w, i % 2, h, :], start=i == 0, stop=i == NKT - 1)
                    if h in (0, 2):
                        between()
                mm.then_inc(pv_mm, 1)

            def turn_out(g):
                pe.wait_ge(acc_ev, g + 1)
                pe.wait_ge(m_row, min(g + 2, NG))
                if g >= 1:
                    pe.wait_ge(o_nat, g)
                for t in range(NT):
                    mm = pe.transpose(ps[:, 7, t * P:(t + 1) * P], acc[:, t * P:(t + 1) * P], k.ident[:, :])
                mm.then_inc(acc_turned, 1)

            norm_tensor(pe, k, n, k.xn)
            turned_wait(pe, n)
            for m in range(NC):
                for c in range(NC):
                    mm = pe.matmul(ps[:, 2 + m, :], k.wqC[:, c, m * P:(m + 1) * P], k.xT[:, c, :],
                                   start=c == 0, stop=c == NC - 1)
                mm.then_inc(q_mm, 1)
            for u in range(NU):
                maxima(0, u)
            turn_maxima(0)
            for g in range(NG):
                chunks = iter(range(NU if g + 1 < NG else 0))

                def maximum():
                    u = next(chunks, None)
                    if u is not None:
                        maxima(g + 1, u)

                for i in range(NKT):
                    if i == NKT - 1 and g + 1 < NG:
                        turn_maxima(g + 1)
                    scores(g, i, 0, maximum)
                    scores(g, i, 1, maximum)
                    if i == 1 and g >= 1:
                        turn_out(g - 1)
                    if i >= 1:
                        values(g, i - 1, maximum)
                values(g, NKT - 1, maximum)
            turn_out(NG - 1)
            for t in range(NT):
                if t == 0:
                    pe.wait_ge(exped, 2 * NKT * NG)
                    pe.wait_ge(o_nat, NG)
                for c in range(NC):
                    mm = pe.transpose(ps[:, c, t * P:(t + 1) * P], oN[:, t, c * P:(c + 1) * P], k.ident[:, :])
            mm.then_inc(o_turned, 1)
            pe.wait_ge(oT_a, 1)
            pe.wait_ge(oT_v, 1)
            for t in range(NT):
                if t >= 2:
                    pe.wait_ge(f_ev, t - 1)
                for c in range(NC):
                    mm = pe.matmul(ps[:, 2 + t % 2, 0:D], oT[:, c, t * P:(t + 1) * P], k.woC[:, c, :],
                                   start=c == 0, stop=c == NC - 1)
                mm.then_inc(f_mm, 1)

        @block.scalar
        def _(act):
            turned_scalar(act, k, n, k.xT)
            for m in range(NC):
                act.wait_ge(q_mm, m + 1)
                nc.scalar.activation(qf[:, m, :], ps[:, 2 + m, :], ACT.Identity,
                                     bias=k.bqC[:, m:m + 1]).then_inc(q_ev, 1)
            for m in range(NC):
                act.wait_ge(split_q, 4 * (m + 1))
                for a in range(2):
                    act.dma_start(k.q_parts[2 * m + a].rearrange("i p s -> p i s"),
                                  q3[a * GH * DC:(a + 1) * GH * DC, :, m, :]).then_inc(stored[m], 16)
                act.wait_ge(stored[m], 32)
                if m == 0:
                    load_q(act, 0)
            act.wait_ge(ld_v, 32)
            act.wait_ge(tail, 2)
            nc.scalar.copy(vaug[:, 0:NKT - 1, :, 0:DC], vf[:, 0:NKT - 1, :].rearrange("p t (h d) -> p t h d", d=DC)).then_inc(v_ev, 1)
            nc.scalar.copy(vaug[0:KW[-1], NKT - 1, :, 0:DC], vf[0:KW[-1], NKT - 1, :].rearrange("p (h d) -> p h d", d=DC)).then_inc(v_ev, 1)
            act.wait_ge(v_ev, 2)
            for g in range(NG):
                for i in range(NKT):
                    w = KW[i]
                    for a in range(2):
                        act.wait_ge(s_mm, 2 * (NKT * g + i) + a + 1)
                        if NKT * g + i >= 2:
                            act.wait_ge(pv_mm, NKT * g + i - 1)
                        nc.scalar.activation(prob[0:w, i % 2, 2 * a:2 * a + 2, :], ps[0:w, 2 * a:2 * a + 2, :],
                                             ACT.Exp, scale=SCALE_C).then_inc(exped, 1)
                act.wait_ge(pv_mm, NKT * (g + 1))
                if g >= 1:
                    act.wait_ge(acc_turned, g)
                nc.scalar.copy(acc[:, :], ps[:, 4, :]).then_inc(acc_ev, 1)
            act.wait_ge(o_turned, 1)
            nc.scalar.copy(oT[:, 0, :], ps[:, 0, :]).then_inc(oT_a, 1)

        @block.vector
        def _(v):
            def maxima(g):
                for u in range(NU):
                    if u == 8 and g >= 2:
                        outputs(g - 2)
                    if g == 0 and u % (GH * NKC) == 0:
                        if u:
                            bias(u // (GH * NKC))
                        v.wait_ge(biasN, u // (GH * NKC) + 1)
                    t, h, i = u // (GH * NKC), u // NKC % GH, u % NKC
                    n = NU * g + u
                    v.wait_ge(mx_mm, n + 1)
                    bank = ps[:, banks(g)[n % len(banks(g))], 0:MC[i]]
                    v.tensor_tensor_reduce(bank, bank, maskN[:, t, MO[i]:MO[i] + MC[i]], 1.0, -3.0e38,
                                           ALU.add, ALU.max, mp[:, t, h, i:i + 1]).then_inc(mx_v, 1)
                v.wait_ge(mx_v, NU * (g + 1))
                if g >= 1:
                    v.wait_ge(split_m, 4 * g)
                v.tensor_reduce(m1[:, 0, :], mp[:, :, :, :].rearrange("p t h i -> p (t h) i"), AX_X, ALU.max,
                                negate=True).then_inc(neg, 1)
                v.wait_ge(neg, g + 1)
                if g >= 1:
                    v.wait_ge(m_turned, g)
                f = [m1[:, i, :].rearrange("p (t h) -> p t h", t=NT) for i in range(2)]
                split3(v, split_m, 4 * g, f[0], [m3[:, :, i, :] for i in range(3)], f[1])
                v.wait_ge(m_turned, g + 1)
                if g >= 1:
                    v.wait_ge(ld_m, 48 * g)
                v.tensor_copy(mrow[:, :], ps[0:3 * GH, 7, 0:BANK // 2].bitcast(BF16)).then_inc(m_row, 1)

            def outputs(g):
                v.wait_ge(acc_turned, g + 1)
                o = ps[:, 7, :].rearrange("p (t h c) -> p t h c", t=NT, h=GH)
                v.reciprocal(rec[:, :, :], o[:, :, :, DC]).then_inc(o_rec, 1)
                v.wait_ge(o_rec, g + 1)
                v.tensor_tensor(oN[:, :, GH * DC * g:GH * DC * (g + 1)].rearrange("p t (h c) -> p t h c", h=GH),
                                o[:, :, :, 0:DC], rec[:, :, :].unsqueeze(3).to_broadcast([P, NT, GH, DC]),
                                ALU.mult).then_inc(o_nat, 1)

            norm_vector(v, n, k.x, k.xn)
            turned_vector(v, k, n, k.xT)

            def bias(t):
                v.wait_ge(ld_maskN[t % 2], 16 * (t // 2 + 1))
                v.tensor_scalar(maskN[:, t, :], rawN[:, t % 2, :], 0.0, MASKED, ALU.is_equal,
                                ALU.mult).then_inc(biasN, 1)

            bias(0)
            for m in range(NC):
                v.wait_ge(q_ev, m + 1)
                split3(v, split_q, 4 * m, qf[:, m, :], [q3[:, i, m, :] for i in range(3)], rest[:, m, :])
            v.wait_ge(split_q, 4 * NC)
            maxima(0)
            for g in range(NG):
                if g + 1 < NG:
                    maxima(g + 1)
            outputs(NG - 2)
            outputs(NG - 1)
            v.wait_ge(o_turned, 1)
            v.tensor_copy(oT[:, 1, :], ps[:, 1, :]).then_inc(oT_v, 1)
            v.wait_ge(xb_done, 1)
            for t in range(NT):
                v.wait_ge(f_mm, t + 1)
                v.tensor_tensor(k.xr[:, t, 0:D], ps[:, 2 + t % 2, 0:D], xb[:, t, :], ALU.add).then_inc(f_ev, 1)


def route_last(k, slots):
    with ExitStack() as own:
        r = Route(k, own, "r")
        block = own.enter_context(k.nc.Block())

        @block.sync
        def _(sp):
            r.keep(sp, NB)
            sp.wait_ge(r.kept, 16)

        @block.tensor
        def _(pe):
            r.turn(pe)
            r.logits(pe)
            r.counts(pe)

        @block.scalar
        def _(act):
            turned_scalar(act, k, r.n, r.xT, bank=6)
            r.exponentials(act)

        @block.gpsimd
        def _(g):
            norm_gpsimd(g, r.n)
            r.tokens(g)

        @block.vector
        def _(v):
            statistics(v, r.n, r.x)
            r.normalise(v)
            turned_vector(v, k, r.n, r.xT, bank=6)
            r.shift(v)
            r.choose(v)
            r.places(v)
            v.wait_ge(r.placed, 2)
            v.wait_ge(slots.step, find_slots(v, k, slots))


def experts(k, A, out):
    nc, ps = k.nc, k.ps
    ld = [k.sem(f"e_ld{i}") for i in range(NE)]
    (turned, bT_ev, g_mm, u_mm, silu, h_done, d_mm, o_ev, copied, padded) = (
        k.sem("e_" + x) for x in ("turned", "bT_ev", "g_mm", "u_mm", "silu", "h", "d_mm", "o_ev", "copied", "padded"))
    F2 = FD - P
    with ExitStack() as own:
        up = k.sb(own, "e_up", [P, NE, NC, 2 * FD])
        down = k.sb(own, "e_down", [P, NE, 2, D])
        buf = k.sb(own, "e_buf", [P, NE, 2, ROW])
        bT = k.sb(own, "e_bT", [P, 2, NC, CAP])
        sg = k.sb(own, "e_sg", [P, 2, 2, CAP])
        hT = k.sb(own, "e_hT", [P, 2, 2, CAP])
        o = k.sb(own, "e_o", [P, NO, 2, D])
        block = own.enter_context(nc.Block())

        @block.gpsimd
        def _(g):
            for i in range(AHEAD):
                scatter_rows(g, k, [i], k.last[i])
            for e in range(ED):
                if e + AHEAD < KD:
                    scatter_rows(g, k, [e + AHEAD], k.last[e + AHEAD])
                g.wait_ge(o_ev, 2 * (e + 1))
                if e >= 1:
                    g.wait_ge(k.added, 32 * e)
                for s in range(2):
                    g.indirect_dma_start(out=k.total[:, :], out_offset=bass.IndirectOffsetOnAxis(
                        ap=buf[:, e % NE, s, TOKEN:ROW].bitcast(I32), axis=0), in_=o[:, e % NO, s, :], in_offset=None,
                        bounds_check=SPARE + CAP - 1, oob_is_err=True, compute_op=ALU.add).then_inc(k.added, 16)

        @block.sync
        def _(sp):
            for e in range(ED):
                if e >= NE:
                    sp.wait_ge(d_mm, e - NE + 1)
                    sp.wait_ge(k.added, 32 * (e - NE + 1))
                i = e % NE
                sp.dma_start(up[:, i], A["D_up"][e]).then_inc(ld[i], 16)
                sp.dma_start(down[:, i, 0], A["D_down"][e, 0:P]).then_inc(ld[i], 16)
                sp.dma_start(down[0:F2, i, 1], A["D_down"][e, P:FD]).then_inc(ld[i], 16)
                if e == 0:
                    sp.wait_ge(k.scattered, 16 * (ZFILL + 1) + 16 * NT * KD * NB)
                if e < KD:
                    sp.wait_ge(k.last[e], 16 * NT)
                sp.dma_start(buf[:, i], k.table[e * CAP:(e + 1) * CAP].rearrange("(p s) d -> p s d", p=P)).then_inc(ld[i], 16)

            sp.wait_ge(k.added, 32 * ED)
            sp.dma_start(out.rearrange("b s d -> (b s) d"), k.total[S:SPARE, :]).then_inc(copied, 16)
            sp.wait_ge(copied, 16)

        @block.tensor
        def _(pe):
            def turn(e):
                pe.wait_ge(ld[e % NE], 64 * (e // NE + 1))
                if e >= 2:
                    pe.wait_ge(bT_ev, e - 1)
                for c in range(NC):
                    for s in range(2):
                        mm = pe.transpose(ps[:, e % 2, c * CAP + s * P:c * CAP + (s + 1) * P],
                                          buf[:, e % NE, s, c * P:(c + 1) * P], k.ident[:, :])
                mm.then_inc(turned, 1)

            def out_of(e):
                pe.wait_ge(h_done, 2 * (e + 1))
                if e >= 2:
                    pe.wait_ge(o_ev, 2 * (e - 1))
                for s in range(2):
                    for j in range(2):
                        mm = pe.matmul(ps[:, 6 + e % 2, s * D:(s + 1) * D], hT[:, e % 2, j, s * P:(s + 1) * P],
                                       down[:, e % NE, j, :], start=j == 0, stop=j == 1)
                mm.then_inc(d_mm, 1)

            turn(0)
            for e in range(ED):
                if e + 1 < ED:
                    turn(e + 1)
                pe.wait_ge(bT_ev, e + 1)
                if e >= 2:
                    pe.wait_ge(h_done, 2 * (e - 1))
                for bank, half, cols, done in ((2, 0, 0, None), (2, 1, 2 * P, g_mm), (4, 0, P, u_mm)):
                    for c in range(NC):
                        mm = pe.matmul(ps[:, bank + e % 2, half * CAP:(half + 1) * CAP], up[:, e % NE, c, cols:cols + P],
                                       bT[:, e % 2, c, :], start=c == 0, stop=c == NC - 1)
                    if done:
                        mm.then_inc(done, 1)
                if e >= 1:
                    out_of(e - 1)
            out_of(ED - 1)

        @block.scalar
        def _(act):
            for e in range(ED):
                act.wait_ge(turned, e + 1)
                if e >= 2:
                    act.wait_ge(u_mm, e - 1)
                nc.scalar.copy(bT[:, e % 2].rearrange("p c s -> p (c s)"), ps[:, e % 2, :]).then_inc(bT_ev, 1)
                act.wait_ge(g_mm, e + 1)
                if e >= 2:
                    act.wait_ge(h_done, 2 * (e - 1))
                nc.scalar.activation(sg[:, e % 2].rearrange("p c s -> p (c s)"), ps[:, 2 + e % 2, :],
                                     ACT.Silu).then_inc(silu, 1)

        @block.vector
        def _(v):
            v.memset(hT[F2:P, :, 1, :], 0.0).then_inc(padded, 1)
            v.memset(down[F2:P, :, 1, :], 0.0).then_inc(padded, 1)

            def read_out(e):
                v.wait_ge(d_mm, e + 1)
                if e >= NO:
                    v.wait_ge(k.added, 32 * (e - NO + 1))
                for s in range(2):
                    v.tensor_scalar(o[:, e % NO, s, :], ps[:, 6 + e % 2, s * D:(s + 1) * D],
                                    buf[:, e % NE, s, WEIGHT + e:WEIGHT + e + 1], None, ALU.mult).then_inc(o_ev, 1)

            for e in range(ED):
                v.wait_ge(silu, e + 1)
                v.wait_ge(u_mm, e + 1)
                if e >= 2:
                    v.wait_ge(d_mm, e - 1)
                v.tensor_tensor(hT[:, e % 2, 0, :], sg[:, e % 2, 0, :], ps[:, 4 + e % 2, 0:CAP], ALU.mult).then_inc(h_done, 1)
                v.tensor_tensor(hT[0:F2, e % 2, 1, :], sg[0:F2, e % 2, 1, :], ps[F2:P, 2 + e % 2, CAP:2 * CAP],
                                ALU.mult).then_inc(h_done, 1)
                if e >= 1:
                    read_out(e - 1)
            read_out(ED - 1)


class Row(Build):

    def __init__(self, nc, ctx):
        super().__init__(nc, ctx)

        def sb(name, shape, dt=F32):
            return self.sb(ctx, name, shape, dt)

        def dram(name, shape, dt):
            return nc.dram_tensor(name, shape, dt, kind="Internal").ap()

        self.ps = ctx.enter_context(nc.psum_tensor("ps", [P, 8, BANK], F32))
        self.ident = sb("ident", [P, P])
        self.identb = sb("identb", [P, P], BF16)
        self.causal = sb("causal", [P, P], BF16)
        self.sel = sb("sel", [P, NJ, P], BF16)
        self.desc = sb("desc", [P, EB])
        self.norm_memory = [NormMemory(sb, x) for x in ("norm", "norm_routed")]
        self.x = sb("x", [P, NT, D])
        self.xn = sb("xn", [P, NT, D])
        self.xT = sb("xT", [P, NC, S])
        self.gp = sb("gp", [P, NT, P], BF16)
        self.wqA, self.wkTA, self.wvA = (sb(x, [P, NC, D]) for x in ("wqA", "wkTA", "wvA"))
        self.bqA, self.bkA, self.bqC, self.bkC = (sb(x, [P, NC]) for x in ("bqA", "bkA", "bqC", "bkC"))
        self.bvA, self.bvC, self.boC = (sb(x, [P, D]) for x in ("bvA", "bvC", "boC"))
        self.wqB, self.wkB = (sb(x, [P, NC, HB * DB]) for x in ("wqB", "wkB"))
        self.wgB = sb("wgB", [P, NC, HB * EB])
        self.wqC, self.wkC, self.wvC, self.woC = (sb(x, [P, NC, D]) for x in ("wqC", "wkC", "wvC", "woC"))
        self.q_parts = dram("q_parts", [NG, 3, DC * GH, S], BF16)
        self.k_parts = dram("k_parts", [NB, NG, 3, DC * GH, SK], BF16)
        self.v_all = dram("v_all", [NB, P, NKT, D], F32)
        self.total = dram("total", [SPARE + CAP, D], F32)
        self.table = dram("table", [NSLOT, ROW], F32)
        self.onesb = sb("onesb", [P, P], BF16)
        self.before = sb("before", [P, P], BF16)
        self.base = sb("base", [P, ED])
        self.carry = sb("carry", [P, ED])
        self.wgD = sb("wgD", [P, NC, ED])

        self.xr = sb("xr", [P, NT, ROW])
        self.chosen = sb("chosen", [P, NT, ED])
        self.place = sb("place", [P, NT, ED])
        self.slot = sb("slot", [P, NT * KD], I32)
        self.token = sb("token", [P, NT], I32)
        self.live = sb("live", [P, 1])
        self.scattered = ctx.enter_context(nc.semaphore("scattered"))
        self.last = [ctx.enter_context(nc.semaphore(f"last{i}")) for i in range(KD)]
        self.loaded = ctx.enter_context(nc.semaphore("loaded"))
        self.added = ctx.enter_context(nc.semaphore("added"))

    def weights(self, A):
        yield self.wkC[:, :, :], A["C_wk"].rearrange("(c p) n -> p c n", p=P)
        yield self.wvC[:, :, :], A["C_wv"].rearrange("(c p) n -> p c n", p=P)
        yield self.bkC[:, :], A["C_bk"]
        yield self.bvC[:, :], A["C_bv"].partition_broadcast(P)
        for dst, src in ((self.wqA, "A_wq"), (self.wkTA, "A_wkT"), (self.wvA, "A_wv"), (self.wqB, "B_wq"),
                         (self.wkB, "B_wk"), (self.wgB, "B_wg"), (self.wqC, "C_wq"), (self.woC, "C_wo"),
                         (self.wgD, "D_wg")):
            yield dst[:, :, :], A[src].rearrange("(c p) n -> p c n", p=P)
        for dst, src in ((self.bqA, "A_bq"), (self.bkA, "A_bk"), (self.bqC, "C_bq")):
            yield dst[:, :], A[src]
        for dst, src in ((self.bvA, "A_bv"), (self.boC, "C_bo")):
            yield dst[:, :], A[src].partition_broadcast(P)


def program(nc, A, out):
    with ExitStack() as whole:
        k = Row(nc, whole)
        with k.semaphores():
            setup(k, A)
        with k.semaphores():
            context_c(k, A)
        with nc.Fori(0, NB) as b:
            with k.semaphores(), ExitStack() as second:
                k.vxB = k.sb(second, "vxB", [P, NC, HB, EB * DB])
                k.oxB = k.sb(second, "oxB", [P, HB, NJ, D])
                attention_a(k, A, b)
                attention_b(k, A, b)
            with k.semaphores():
                attention_c(k, A, b)
        with k.semaphores():
            with ExitStack() as last:
                route_last(k, Slots(k, last, "slots"))
            experts(k, A, out)


def layouts(i):
    import numpy as _np

    c = _np.ascontiguousarray
    vx, ox = _np.asarray(i["L0_ffn_value_experts"]), _np.asarray(i["L0_ffn_output_experts"])
    ctx, mask = _np.asarray(i["ctx_1024"]), _np.asarray(i["mask_Bx1xSxS2_ik1"])[:, 0]
    T = lambda x: _np.asarray(x).T
    cols = lambda x: _np.asarray(x).reshape(-1, 128).T
    heads = lambda x: x.reshape(x.shape[0], NG, GH, DC).transpose(0, 1, 3, 2).reshape(x.shape)
    up = _np.asarray(i["L1_ffn_gate_up_proj"]).transpose(0, 2, 1)
    up = _np.concatenate([up[:, :, 0:128], up[:, :, 192:320], up[:, :, 128:192], up[:, :, 320:384]], axis=2)
    a = {
        "x": i["x"], "ctx": ctx, "ctxT": ctx.transpose(0, 2, 1), "mask": mask, "maskT": mask.transpose(0, 2, 1),
        "A_wq": i["L0_xattn_Wq"], "A_wkT": T(i["L0_xattn_Wk"]), "A_wv": i["L0_xattn_Wv"],
        "A_bq": cols(i["L0_xattn_bq"]), "A_bk": cols(i["L0_xattn_bk"]), "A_bv": i["L0_xattn_bv"],
        "B_wq": i["L0_ffn_w_q"], "B_wk": i["L0_ffn_w_k"], "B_wg": i["L0_ffn_w_gate"],
        "B_vx": vx.transpose(2, 1, 0, 3).reshape(256, 8, 512),
        "B_ox": ox.transpose(1, 0, 2, 3).reshape(8, 4, 2, 64, 256),
        "C_wq": heads(T(i["L1_xattn_wq_w"])), "C_wk": heads(T(i["L1_xattn_wk_w"])), "C_wv": T(i["L1_xattn_wv_w"]),
        "C_wo": T(i["L1_xattn_fo_w"]), "C_bq": cols(heads(_np.asarray(i["L1_xattn_wq_b"])[None])), "C_bk": cols(heads(_np.asarray(i["L1_xattn_wk_b"])[None])),
        "C_bv": i["L1_xattn_wv_b"], "C_bo": i["L1_xattn_fo_b"],
        "D_wg": T(i["L1_ffn_gate_weight"]),
        "D_up": up.reshape(32, 2, 128, 384).transpose(0, 2, 1, 3),
        "D_down": _np.asarray(i["L1_ffn_down_proj"]).transpose(0, 2, 1),
    }
    return {n: c(_np.asarray(x)) for n, x in a.items()}


def kernel(**inputs):
    import concourse.bacc as _bacc
    from concourse.bass_utils import run_bass_kernel_spmd as _run

    nc = _bacc.Bacc("TRN2", target_bir_lowering=False, num_devices=1)
    arrays, A = {}, {}
    for name, a in layouts(inputs).items():
        arrays[f"in_{name}"] = a
        A[name] = nc.dram_tensor(f"in_{name}", a.shape, mybir.dt.from_np(a.dtype), kind="ExternalInput").ap()
    out = nc.dram_tensor("out_0", (NB, S, D), F32, kind="ExternalOutput").ap()
    program(nc, A, out)
    r = _run(nc, [arrays], core_ids=[0])
    return r.results[0]["out_0"]
```
